# Optimizing a Trainium2 kernel written in Bass

```python
import numpy as np
import jax
import jax.numpy as jnp

def _softmax(x, axis=-1):
    return jax.nn.softmax(x, axis=axis)

def _gelu(x):
    return jax.nn.gelu(x, approximate=True)

def _silu(x):
    return jax.nn.silu(x)

def _sigmoid(x):
    return jax.nn.sigmoid(x)

def _layernorm(x, axis=-1, eps=1e-05):
    m = jnp.mean(x, axis=axis, keepdims=True)
    v = jnp.var(x, axis=axis, keepdims=True)
    return (x - m) / jnp.sqrt(v + eps)

def _scatter_add(tgt, idx, src, axis=0):
    return tgt.at[idx].add(src)

def _segment_sum(src, seg, n):
    return jax.ops.segment_sum(src, seg, n)
kernel_name = 'mk_early_fusion_d2_tok_img768_r4_703fcb'

def setup_inputs(seed: int=0):
    np.random.seed(seed)
    _w = jnp.asarray

    def _rec_inputs():
        import jax
        import jax.numpy as jnp
        _rk = jax.random.key(seed)
        x = -0.000356955 + 1 * jax.random.normal(jax.random.fold_in(_rk, 1), (16, 3, 96, 96), jnp.float32)
        txt = 0.000370516 + 0.554004 * jax.random.normal(jax.random.fold_in(_rk, 2), (16, 32, 192), jnp.float32)
        return (x, txt)
    x, txt = _rec_inputs()

    def _L0_tok_setup():
        import jax, jax.numpy as jnp
        import numpy as np
        PATCH = 16
        EMB = 192
        key = jax.random.key(seed)
        k1, k2 = jax.random.split(key)
        x = jax.random.normal(k1, (128, 3, 224, 224), dtype=jnp.float32)
        W = jax.random.normal(k2, (EMB, PATCH * PATCH * 3), dtype=jnp.float32) * 0.02
        return {'x': x, 'W': W}
    _L0_tok_all = _L0_tok_setup()
    _L0_tok_in = {k: v for k, v in _L0_tok_all.items() if k in ('W',)}
    del _L0_tok_all

    def _L0_attn_setup():
        import jax, jax.numpy as jnp
        import numpy as np
        N_HEAD = 12
        N_EMBD = 192
        BLOCK = 512
        THETA = 10000.0

        def _rope_tables(head_dim, end, theta=THETA):
            half = head_dim // 2
            freqs = 1.0 / theta ** (jnp.arange(0, head_dim, 2, dtype=jnp.float32) / head_dim)
            t = jnp.arange(end, dtype=jnp.float32)
            ang = jnp.outer(t, freqs)
            return (jnp.cos(ang), jnp.sin(ang))

        def _apply_rope(x, cos, sin):
            B, H, T, hd = x.shape
            xr = x.reshape(B, H, T, hd // 2, 2)
            x0, x1 = (xr[..., 0], xr[..., 1])
            c = cos[None, None, :T, :]
            s = sin[None, None, :T, :]
            o0 = x0 * c - x1 * s
            o1 = x0 * s + x1 * c
            return jnp.stack([o0, o1], axis=-1).reshape(B, H, T, hd)
        key = jax.random.key(seed)
        ks = jax.random.split(key, 9)
        B, T, C = (2, 512, N_EMBD)
        std = 0.02
        return {'x': jax.random.normal(ks[0], (B, T, C), jnp.float32), 'norm_scale': jnp.ones((C,), jnp.float32), 'norm_bias': jnp.zeros((C,), jnp.float32), 'W_attn': jax.random.normal(ks[1], (C, 3 * C), jnp.float32) * std, 'b_attn': jax.random.normal(ks[2], (3 * C,), jnp.float32) * std, 'W_proj': jax.random.normal(ks[3], (C, C), jnp.float32) * std, 'b_proj': jax.random.normal(ks[4], (C,), jnp.float32) * std, 'sinks': jax.random.normal(ks[5], (N_HEAD,), jnp.float32) * 0.5, 'rezero': jax.random.normal(ks[6], (1,), jnp.float32) * 0.1}
    _L0_attn_all = _L0_attn_setup()
    _L0_attn_in = {k: v for k, v in _L0_attn_all.items() if k in ('norm_scale', 'norm_bias', 'W_attn', 'b_attn', 'W_proj', 'b_proj', 'sinks', 'rezero')}
    del _L0_attn_all

    def _L0_ffn_setup():
        import jax, jax.numpy as jnp
        import numpy as np
        D_MODEL = 192
        N_EXPERTS = 16
        TOP_K = 2
        D_FF = 4 * D_MODEL
        B, L = (4, 512)
        key = jax.random.key(seed)
        ks = jax.random.split(key, 6)
        s_in = 1.0 / np.sqrt(D_MODEL)
        s_ff = 1.0 / np.sqrt(D_FF)
        x = jax.random.normal(ks[0], (B, L, D_MODEL), dtype=jnp.float32)
        Wr = jax.random.uniform(ks[1], (N_EXPERTS, D_MODEL), jnp.float32, -s_in, s_in)
        W1 = jax.random.uniform(ks[2], (N_EXPERTS, D_MODEL, D_FF), jnp.float32, -s_in, s_in)
        b1 = jax.random.uniform(ks[3], (N_EXPERTS, D_FF), jnp.float32, -s_in, s_in)
        W2 = jax.random.uniform(ks[4], (N_EXPERTS, D_FF, D_MODEL), jnp.float32, -s_ff, s_ff)
        b2 = jax.random.uniform(ks[5], (N_EXPERTS, D_MODEL), jnp.float32, -s_ff, s_ff)
        return {'x': x, 'Wr': Wr, 'W1': W1, 'b1': b1, 'W2': W2, 'b2': b2}
    _L0_ffn_all = _L0_ffn_setup()
    _L0_ffn_in = {k: v for k, v in _L0_ffn_all.items() if k in ('Wr', 'W1', 'b1', 'W2', 'b2')}
    del _L0_ffn_all

    def _L1_attn_setup():
        import jax, jax.numpy as jnp
        import numpy as np
        ALPHA = 0.35

        def _round_ln_pow2(x):
            y = jnp.floor(jnp.log2(x))
            up = x - 2.0 ** y > 2.0 ** (y + 1.0) - x
            return 2.0 ** (y + up.astype(x.dtype))
        key = jax.random.key(seed)
        k1, k2, k3, k4, k5 = jax.random.split(key, 5)
        B, N, C = (64, 197, 192)
        return {'x': jax.random.normal(k1, (B, N, C), dtype=jnp.float32), 'qkv_weight': jax.random.normal(k2, (3 * C, C), dtype=jnp.float32) * 0.02, 'qkv_bias': jax.random.normal(k3, (3 * C,), dtype=jnp.float32) * 0.02, 'proj_weight': jax.random.normal(k4, (C, C), dtype=jnp.float32) * 0.02, 'proj_bias': jax.random.normal(k5, (C,), dtype=jnp.float32) * 0.02}
    _L1_attn_all = _L1_attn_setup()
    _L1_attn_in = {k: v for k, v in _L1_attn_all.items() if k in ('qkv_weight', 'qkv_bias', 'proj_weight', 'proj_bias')}
    del _L1_attn_all

    def _L1_ffn_setup():
        import jax, jax.numpy as jnp
        import numpy as np
        H = 192
        R = 64
        E = 8
        B, S = (8, 512)
        key = jax.random.key(seed)
        ks = jax.random.split(key, 10)
        s_in = 1.0 / np.sqrt(H)
        s_r = 1.0 / np.sqrt(R)
        return {'x': jax.random.normal(ks[0], (B, S, H), dtype=jnp.float32), 'enc_w': jax.random.uniform(ks[1], (H, R), jnp.float32, -s_in, s_in), 'enc_b': jax.random.uniform(ks[2], (R,), jnp.float32, -s_in, s_in), 'sw_w': jax.random.uniform(ks[3], (R, E), jnp.float32, -s_r, s_r), 'sw_b': jax.random.uniform(ks[4], (E,), jnp.float32, -s_r, s_r), 'w1': jax.random.uniform(ks[5], (E, H, R), jnp.float32, -s_in, s_in), 'b1': jax.random.uniform(ks[6], (E, R), jnp.float32, -s_in, s_in), 'w2': jax.random.uniform(ks[7], (E, R, H), jnp.float32, -s_r, s_r), 'b2': jax.random.uniform(ks[8], (E, H), jnp.float32, -s_r, s_r)}
    _L1_ffn_all = _L1_ffn_setup()
    _L1_ffn_in = {k: v for k, v in _L1_ffn_all.items() if k in ('enc_w', 'enc_b', 'sw_w', 'sw_b', 'w1', 'b1', 'w2', 'b2')}
    del _L1_ffn_all
    return {'x': x, 'txt': txt, 'L0_tok_W': _L0_tok_in['W'], 'L0_attn_norm_scale': _L0_attn_in['norm_scale'], 'L0_attn_norm_bias': _L0_attn_in['norm_bias'], 'L0_attn_W_attn': _L0_attn_in['W_attn'], 'L0_attn_b_attn': _L0_attn_in['b_attn'], 'L0_attn_W_proj': _L0_attn_in['W_proj'], 'L0_attn_b_proj': _L0_attn_in['b_proj'], 'L0_attn_sinks': _L0_attn_in['sinks'], 'L0_attn_rezero': _L0_attn_in['rezero'], 'L0_ffn_Wr': _L0_ffn_in['Wr'], 'L0_ffn_W1': _L0_ffn_in['W1'], 'L0_ffn_b1': _L0_ffn_in['b1'], 'L0_ffn_W2': _L0_ffn_in['W2'], 'L0_ffn_b2': _L0_ffn_in['b2'], 'L1_attn_qkv_weight': _L1_attn_in['qkv_weight'], 'L1_attn_qkv_bias': _L1_attn_in['qkv_bias'], 'L1_attn_proj_weight': _L1_attn_in['proj_weight'], 'L1_attn_proj_bias': _L1_attn_in['proj_bias'], 'L1_ffn_enc_w': _L1_ffn_in['enc_w'], 'L1_ffn_enc_b': _L1_ffn_in['enc_b'], 'L1_ffn_sw_w': _L1_ffn_in['sw_w'], 'L1_ffn_sw_b': _L1_ffn_in['sw_b'], 'L1_ffn_w1': _L1_ffn_in['w1'], 'L1_ffn_b1': _L1_ffn_in['b1'], 'L1_ffn_w2': _L1_ffn_in['w2'], 'L1_ffn_b2': _L1_ffn_in['b2']}

def reference(x, txt, L0_tok_W, L0_attn_norm_scale, L0_attn_norm_bias, L0_attn_W_attn, L0_attn_b_attn, L0_attn_W_proj, L0_attn_b_proj, L0_attn_sinks, L0_attn_rezero, L0_ffn_Wr, L0_ffn_W1, L0_ffn_b1, L0_ffn_W2, L0_ffn_b2, L1_attn_qkv_weight, L1_attn_qkv_bias, L1_attn_proj_weight, L1_attn_proj_bias, L1_ffn_enc_w, L1_ffn_enc_b, L1_ffn_sw_w, L1_ffn_sw_b, L1_ffn_w1, L1_ffn_b1, L1_ffn_w2, L1_ffn_b2):
    import jax
    import jax.numpy as jnp

    def _L0_tok_ref(x, W):
        import jax, jax.numpy as jnp
        import numpy as np
        PATCH = 16
        EMB = 192
        B, C, H, Wd = x.shape
        p = PATCH
        hp, wp = (H // p, Wd // p)
        num_patches = hp * wp
        xp = x.reshape(B, C, hp, p, wp, p).transpose(0, 1, 2, 4, 3, 5)
        xp = xp.reshape(B, C, num_patches, p, p).transpose(0, 2, 1, 3, 4)
        xp = xp.reshape(B, num_patches, C * p * p)
        return jnp.einsum('bnf,ef->bne', xp, W)

    def _L0_attn_ref(x, norm_scale, norm_bias, W_attn, b_attn, W_proj, b_proj, sinks, rezero):
        import jax, jax.numpy as jnp
        import numpy as np
        N_HEAD = 12
        N_EMBD = 192
        BLOCK = 512
        THETA = 10000.0

        def _rope_tables(head_dim, end, theta=THETA):
            half = head_dim // 2
            freqs = 1.0 / theta ** (jnp.arange(0, head_dim, 2, dtype=jnp.float32) / head_dim)
            t = jnp.arange(end, dtype=jnp.float32)
            ang = jnp.outer(t, freqs)
            return (jnp.cos(ang), jnp.sin(ang))

        def _apply_rope(x, cos, sin):
            B, H, T, hd = x.shape
            xr = x.reshape(B, H, T, hd // 2, 2)
            x0, x1 = (xr[..., 0], xr[..., 1])
            c = cos[None, None, :T, :]
            s = sin[None, None, :T, :]
            o0 = x0 * c - x1 * s
            o1 = x0 * s + x1 * c
            return jnp.stack([o0, o1], axis=-1).reshape(B, H, T, hd)
        B, T, C = x.shape
        H = N_HEAD
        hd = C // H
        xn = norm_scale * x + norm_bias
        qkv = xn @ W_attn + b_attn
        q, k, v = jnp.split(qkv, 3, axis=-1)
        q = q.reshape(B, T, H, hd).transpose(0, 2, 1, 3)
        k = k.reshape(B, T, H, hd).transpose(0, 2, 1, 3)
        v = v.reshape(B, T, H, hd).transpose(0, 2, 1, 3)
        cos, sin = _rope_tables(hd, T)
        q = _apply_rope(q, cos, sin)
        k = _apply_rope(k, cos, sin)
        scale = 1.0 / jnp.sqrt(jnp.float32(hd))
        att = jnp.einsum('bhqd,bhkd->bhqk', q, k) * scale
        causal = jnp.tril(jnp.ones((T, T), dtype=bool))
        att = jnp.where(causal[None, None], att, -jnp.inf)
        sink_col = jnp.broadcast_to(sinks.reshape(1, H, 1, 1), (B, H, T, 1))
        att = jnp.concatenate([sink_col, att], axis=-1)
        att = jax.nn.softmax(att, axis=-1)[..., 1:]
        y = jnp.einsum('bhqk,bhkd->bhqd', att, v)
        y = y.transpose(0, 2, 1, 3).reshape(B, T, C)
        y = (y @ W_proj + b_proj) * rezero
        return y

    def _L0_ffn_ref(x, Wr, W1, b1, W2, b2):
        import jax, jax.numpy as jnp
        import numpy as np
        D_MODEL = 192
        N_EXPERTS = 16
        TOP_K = 2
        D_FF = 4 * D_MODEL
        B, L = (4, 512)
        logits = jnp.einsum('bld,ed->ble', x, Wr)
        probs = jax.nn.softmax(logits, axis=-1)
        top_p, top_idx = jax.lax.top_k(probs, TOP_K)
        gating = jnp.sum(jax.nn.one_hot(top_idx, N_EXPERTS, dtype=probs.dtype) * top_p[..., None], axis=-2)
        gate_e = jnp.moveaxis(gating, -1, 0)

        def step(y, params):
            W1e, b1e, W2e, b2e, ge = params
            h = jax.nn.gelu(jnp.einsum('bld,df->blf', x, W1e) + b1e, approximate=False)
            out = jnp.einsum('blf,fd->bld', h, W2e) + b2e
            return (y + ge[..., None] * out, None)
        y0 = jnp.zeros_like(x)
        y, _ = jax.lax.scan(step, y0, (W1, b1, W2, b2, gate_e))
        return x + y

    def _L1_attn_ref(x, qkv_weight, qkv_bias, proj_weight, proj_bias):
        import jax, jax.numpy as jnp
        import numpy as np
        ALPHA = 0.35

        def _round_ln_pow2(x):
            y = jnp.floor(jnp.log2(x))
            up = x - 2.0 ** y > 2.0 ** (y + 1.0) - x
            return 2.0 ** (y + up.astype(x.dtype))
        B, N, C = x.shape
        num_heads = 12
        head_dim = C // num_heads
        scale = head_dim ** (-0.5)
        global_max_x = jnp.abs(x).max(axis=(0, 1))
        max_weight = jnp.abs(qkv_weight).max(axis=0)
        channel_scale = _round_ln_pow2(global_max_x ** ALPHA / max_weight ** (1.0 - ALPHA))
        x_smoothed = x / channel_scale[None, None, :]
        weight_smoothed = qkv_weight * channel_scale[None, :]
        h = jnp.einsum('bnc,mc->bnm', x_smoothed, weight_smoothed) + qkv_bias
        qkv = h.reshape(B, N, 3, num_heads, head_dim).transpose(2, 0, 3, 1, 4)
        q, k, v = (qkv[0], qkv[1], qkv[2])
        attn = jnp.einsum('bhnd,bhmd->bhnm', q, k) * scale
        attn = jax.nn.softmax(attn, axis=-1)
        out = jnp.einsum('bhnm,bhmd->bhnd', attn, v)
        out = out.transpose(0, 2, 1, 3).reshape(B, N, C)
        out = jnp.einsum('bnc,mc->bnm', out, proj_weight) + proj_bias
        return out

    def _L1_ffn_ref(x, enc_w, enc_b, sw_w, sw_b, w1, b1, w2, b2):
        import jax, jax.numpy as jnp
        import numpy as np
        H = 192
        R = 64
        E = 8
        B, S = (8, 512)
        b, s, d = x.shape
        xt = x.reshape(-1, d)
        x_enc = xt @ enc_w + enc_b
        route_prob = jax.nn.softmax(x_enc @ sw_w + sw_b, axis=-1)
        route_prob_max = jnp.max(route_prob, axis=-1)
        routes = jnp.argmax(route_prob, axis=-1)
        onehot = jax.nn.one_hot(routes, E, dtype=xt.dtype)
        h = jnp.einsum('td,edr->ter', xt, w1) + b1[None]
        h = jax.nn.gelu(h, approximate=False)
        h = h * onehot[..., None]
        out = jnp.einsum('ter,erd->td', h, w2) + onehot @ b2
        out = out * route_prob_max[:, None]
        return out.reshape(b, s, d)
    h = _L0_tok_ref(x, L0_tok_W)
    h = jnp.concatenate([h, txt], axis=1)
    h = h + _L0_attn_ref(_layernorm(h, axis=-1), L0_attn_norm_scale, L0_attn_norm_bias, L0_attn_W_attn, L0_attn_b_attn, L0_attn_W_proj, L0_attn_b_proj, L0_attn_sinks, L0_attn_rezero)
    h = h + _L0_ffn_ref(_layernorm(h, axis=-1), L0_ffn_Wr, L0_ffn_W1, L0_ffn_b1, L0_ffn_W2, L0_ffn_b2)
    h = h + _L1_attn_ref(_layernorm(h, axis=-1), L1_attn_qkv_weight, L1_attn_qkv_bias, L1_attn_proj_weight, L1_attn_proj_bias)
    h = h + _L1_ffn_ref(_layernorm(h, axis=-1), L1_ffn_enc_w, L1_ffn_enc_b, L1_ffn_sw_w, L1_ffn_sw_b, L1_ffn_w1, L1_ffn_b1, L1_ffn_w2, L1_ffn_b2)
    return h

_drawn_inputs = setup_inputs


def setup_inputs(seed=0):
    import zlib

    import numpy as np

    out = dict(_drawn_inputs(seed))
    spreads = {'L0_attn_norm_scale': (1.0, 0.6), 'L0_attn_norm_bias': (0.0, 0.8)}
    factors = {'L0_attn_W_attn': 8.0,
     'L0_attn_b_attn': 8.0,
     'L0_attn_W_proj': 8.0,
     'L0_attn_b_proj': 8.0,
     'L0_attn_sinks': 8.0,
     'L0_ffn_b1': 8.0,
     'L0_ffn_b2': 8.0,
     'L1_attn_qkv_weight': 8.0,
     'L1_attn_qkv_bias': 8.0,
     'L1_attn_proj_weight': 7.617,
     'L1_attn_proj_bias': 11.945,
     'L1_ffn_enc_b': 39.406,
     'L1_ffn_sw_b': 4.061,
     'L1_ffn_b1': 64.0,
     'L1_ffn_b2': 6.217,
     'L1_ffn_w1': 5.777,
     'L1_ffn_w2': 4.775}
    for name, (base, spread) in spreads.items():
        noise = np.random.default_rng([zlib.crc32(name.encode()), seed]).standard_normal(out[name].shape)
        drawn = base * np.exp(spread * noise) if base else spread * noise
        out[name] = jnp.asarray(drawn.astype(out[name].dtype))
    for name, factor in factors.items():
        out[name] = (out[name] * factor).astype(out[name].dtype)
    return out
```

```python
from contextlib import ExitStack

import concourse.bass as bass
from concourse import mybir

ALU = mybir.AluOpType
ACT = mybir.ActivationFunctionType
F32 = mybir.dt.float32
BF16 = mybir.dt.bfloat16
AX_X = mybir.AxisListType.X

P = 128
B = 16
NPATCH = 36
NTXT = 32
T = NPATCH + NTXT
C = 192
C1 = C - P
HEADS = 12
HD = C // HEADS
SLOT = 32
NG = HEADS // 4
HALF = 6 * T
PF = 6
E0, F0 = 16, 768
E1, R1 = 8, 64
FC = F0 // P
RC = E1 * R1 // P
G4 = 4 * T
EPS = 1e-5
MASKED = -1.0e30


def fusion_kernel(nc, t, out):
    with ExitStack() as ctx:
        def sb(name, shape, dt=F32):
            return ctx.enter_context(nc.sbuf_tensor(name, shape, dt))

        def sem(name):
            return ctx.enter_context(nc.semaphore(name))

        bank = [ctx.enter_context(nc.psum_tensor(f"bank{i}", [P, 512], F32)) for i in range(8)]

        ident = sb("ident", [P, P])
        ident16 = sb("ident16", [T, T], BF16)
        mask16 = sb("mask16", [T, HALF], BF16)
        mask_in = sb("mask_in", [T, T])
        sel_in = sb("sel_in", [E1, RC * P])
        rope_c = sb("rope_c", [T, HD])
        rope_s = sb("rope_s", [T, HD])
        patches = sb("patches", [P, PF, B // 2, P])
        w_tok = sb("w_tok", [P, PF, C])
        qkv_w0 = [sb(f"qkv_w0_{l}", [P, 3 * C]) for l in range(2)]
        qkv_w1 = [sb(f"qkv_w1_{l}", [C1 + 1, 3 * C]) for l in range(2)]
        proj_w0 = [sb(f"proj_w0_{l}", [P, C]) for l in range(2)]
        proj_w1 = [sb(f"proj_w1_{l}", [C1 + 1, C]) for l in range(2)]
        ln_scale0, ln_scale1 = sb("ln_scale0", [P, 1]), sb("ln_scale1", [C1, 1])
        ln_bias0, ln_bias1 = sb("ln_bias0", [P, 1]), sb("ln_bias1", [C1, 1])
        sinks = sb("sinks", [T, HEADS])
        sinks4 = sb("sinks4", [T, HEADS])
        rezero = sb("rezero", [T, 1])
        router0, router1 = sb("router0", [P, E0]), sb("router1", [C1, E0])
        enc_w0, enc_w1 = sb("enc_w0", [P, R1]), sb("enc_w1", [C1 + 1, R1])
        sw_w = sb("sw_w", [R1 + 1, E1])
        f1_w0, f1_w1 = sb("f1_w0", [P, E1 * R1]), sb("f1_w1", [C1 + 1, E1 * R1])
        f1_w2 = sb("f1_w2", [P, RC, C])
        f1_b2 = sb("f1_b2", [E1, C])
        sel16 = sb("sel16", [E1, RC, P], BF16)
        expert_no = sb("expert_no", [T, E0])

        h = sb("h", [T, B, C])
        stats = sb("stats", [T, B, 6])
        lnv = sb("lnv", [T, 8, B])
        mean, rstd = sb("mean", [T, B]), sb("rstd", [T, B])

        xn = sb("xn", [T, C])
        xT0, xT1 = sb("xT0", [P, T]), sb("xT1", [C1 + 1, T])
        v_all = sb("v_all", [T, B, HEADS, HD + 1])
        rope_a, rope_b = sb("rope_a", [T, 2 * HEADS, HD]), sb("rope_b", [T, 2 * HEADS, HD])
        qk = sb("qk", [T, 2 * HEADS, SLOT])
        qT = sb("qT", [P, NG, T])
        kT = sb("kT", [P, NG, 4, T])
        top = sb("top", [T, B, HEADS])
        sink_e = sb("sink_e", [T, B, HEADS])
        sc = sb("sc", [T, HEADS, T])
        pT = sb("pT", [T, HEADS, T])
        den = sb("den", [T, HEADS])
        rden = sb("rden", [T, HEADS])
        o = sb("o", [T, HEADS, HD])
        oT0, oT1 = sb("oT0", [P, T]), sb("oT1", [C1 + 1, T])

        XT0, XT1 = sb("XT0", [P, B * T]), sb("XT1", [C1 + 1, B * T])
        encT = sb("encT", [R1 + 1, T])
        lg = sb("lg", [T, B, E0])
        r1, r2, r3 = (sb(f"route{i}", [T, B, E0]) for i in range(3))
        one_hot1 = sb("one_hot1", [T, B, E1])
        oneT = sb("oneT", [E1, B * T])
        oneTc = sb("oneTc", [E1, G4])
        oneTc16 = sb("oneTc16", [E1, G4], BF16)
        rs = [sb(f"rs{i}", [T, B]) for i in range(4)]
        gate = sb("gate", [T, B, E0])
        w1a = [sb(f"w1a{i}", [P, F0]) for i in range(2)]
        w1b = [sb(f"w1b{i}", [C1 + 1, F0]) for i in range(2)]
        w2a = [sb(f"w2a{i}", [P, FC, C]) for i in range(2)]
        b2a = [sb(f"b2a{i}", [1, C]) for i in range(2)]
        ones_row = sb("ones_row", [1, T])
        hT = [sb(f"hT{i}", [P, FC, G4]) for i in range(2)]
        gm = sb("gm", [P, RC, G4])
        yout = sb("yout", [T, B, C])

        const_in, moe_in0, moe_in1, out_sent = (sem(x) for x in ("const_in", "moe_in0", "moe_in1", "out_sent"))
        moe_in = [moe_in0, moe_in1]
        (filled, patch_ps, patch_sb, stats_done, sqrt_done, ln_step, ln_done, xn_done, xT_ps, xT_sb, qkv_ps, v_sb,
         rope_mul, qk_done, qkT_ps, q_sb, k_sb, s_ps, top_raw, top_done, s_sub, e_done, sink_done, pT_ps, pT_sb, o_ps,
         den_done, rden_done, o_done, oT_ps, oT_sb, y_ps, h_done) = (sem(x) for x in (
             "filled", "patch_ps", "patch_sb", "stats_done", "sqrt_done", "ln_step", "ln_done", "xn_done", "xT_ps",
             "xT_sb", "qkv_ps", "v_sb", "rope_mul", "qk_done", "qkT_ps", "q_sb", "k_sb", "s_ps", "top_raw",
             "top_done", "s_sub", "e_done", "sink_done", "pT_ps", "pT_sb", "o_ps", "den_done", "rden_done", "o_done",
             "oT_ps", "oT_sb", "y_ps", "h_done"))
        (f_xT_ps, f_xT_sb, f_hadd, f_enc_ps, f_enc_sb, f_log_ps, f_route, f_exp, gate_done,
         f_hid_ps, f_hid_sb, f_y_ps, f_acc, oneT_ps, oneT_sb, oneTc_sb, mask_ps, gm_done, yout_done) = (sem(x) for x in (
             "f_xT_ps", "f_xT_sb", "f_hadd", "f_enc_ps", "f_enc_sb", "f_log_ps", "f_route", "f_exp", "gate_done",
             "f_hid_ps", "f_hid_sb", "f_y_ps", "f_acc", "oneT_ps", "oneT_sb", "oneTc_sb", "mask_ps", "gm_done",
             "yout_done"))

        consts = [
            (w_tok[:, :, :], t["wtokT"]), (patches[:, :, :, :], t["patchT"]), (ident[:, :], t["ident"]),
            (h[NPATCH:T, :, :], t["txt"].rearrange("b n c -> n b c")),
            (qkv_w0[0][:, :], t["qkv0"][0:P]), (qkv_w1[0][0:C1, :], t["qkv0"][P:C]), (qkv_w1[0][C1:C1 + 1, :], t["bqkv0"]),
            (ln_scale0[:, :], t["nscale"][0:P]), (ln_scale1[:, :], t["nscale"][P:C]),
            (ln_bias0[:, :], t["nbias"][0:P]), (ln_bias1[:, :], t["nbias"][P:C]),
            (rope_c[:, :], t["rope_c"]), (rope_s[:, :], t["rope_s"]),
            (mask_in[:, :], t["mask"]), (sel_in[:, :], t["sel"]),
            (proj_w0[0][:, :], t["proj0"][0:P]), (proj_w1[0][0:C1, :], t["proj0"][P:C]), (proj_w1[0][C1:C1 + 1, :], t["bproj0"]),
            (sinks[:, :], t["sinks"].to_broadcast([T, HEADS])), (rezero[:, :], t["rezero"].to_broadcast([T, 1])),
            (router0[:, :], t["wrT"][0:P]), (router1[:, :], t["wrT"][P:C]),
            (expert_no[:, :], t["expert_no"].to_broadcast([T, E0])),
            (qkv_w0[1][:, :], t["qkv1"][0:P]), (qkv_w1[1][0:C1, :], t["qkv1"][P:C]), (qkv_w1[1][C1:C1 + 1, :], t["bqkv1"]),
            (proj_w0[1][:, :], t["proj1"][0:P]), (proj_w1[1][0:C1, :], t["proj1"][P:C]), (proj_w1[1][C1:C1 + 1, :], t["bproj1"]),
            (enc_w0[:, :], t["encw"][0:P]), (enc_w1[0:C1, :], t["encw"][P:C]), (enc_w1[C1:C1 + 1, :], t["encb"]),
            (sw_w[0:R1, :], t["sww"]), (sw_w[R1:R1 + 1, :], t["swb"]),
            (f1_w0[:, :], t["f1w1"][0:P]), (f1_w1[0:C1, :], t["f1w1"][P:C]), (f1_w1[C1:C1 + 1, :], t["f1b1"]),
            (f1_w2[:, :, :], t["f1w2"].rearrange("(c p) n -> p c n", p=P)), (f1_b2[:, :], t["f1b2"]),
        ]
        ALL_IN = 16 * len(consts)

        block = ctx.enter_context(nc.Block())

        @block.sync
        def _(sp):
            for dst, src in consts:
                sp.dma_start(dst, src).then_inc(const_in, 16)
            def load_expert(p, e, free):
                if free is not None:
                    sp.wait_ge(f_y_ps, free)
                w1 = t["w1"][bass.ds(e, 1), :, :].rearrange("o k f -> (o k) f")
                w2 = t["w2"][bass.ds(e, 1), :, :].rearrange("o (c p) n -> (o p) c n", p=P)
                sp.dma_start(w1a[p][:, :], w1[0:P]).then_inc(moe_in[p], 16)
                sp.dma_start(w1b[p][0:C1, :], w1[P:C]).then_inc(moe_in[p], 16)
                sp.dma_start(w1b[p][C1:C1 + 1, :], t["b1"][bass.ds(e, 1), :]).then_inc(moe_in[p], 16)
                sp.dma_start(w2a[p][:, :, :], w2).then_inc(moe_in[p], 16)
                sp.dma_start(b2a[p][:, :], t["b2"][bass.ds(e, 1), :]).then_inc(moe_in[p], 16)
            load_expert(0, 0, None)
            load_expert(1, 1, None)
            with sp.Fori(2, E0 - 1, 2) as e:
                for p in range(2):
                    load_expert(p, e + p, B * (e + p - 1))
            sp.wait_ge(yout_done, B)
            sp.dma_start(out.rearrange("b n c -> n b c"), yout[:, :, :]).then_inc(out_sent, 16)
            sp.wait_ge(out_sent, 16)

        @block.gpsimd
        def _(pool):
            nc.gpsimd.memset(qk[:, :, :], 0.0).then_inc(filled, 1)
            nc.gpsimd.memset(kT[:, :, :, :], 0.0).then_inc(filled, 1)
            nc.gpsimd.memset(v_all[:, :, :, :], 1.0).then_inc(filled, 1)
            nc.gpsimd.memset(xT1[:, :], 1.0).then_inc(filled, 1)
            nc.gpsimd.memset(oT1[:, :], 1.0).then_inc(filled, 1)
            nc.gpsimd.memset(XT1[:, :], 1.0).then_inc(filled, 1)
            nc.gpsimd.memset(encT[:, :], 1.0).then_inc(filled, 1)
            nc.gpsimd.memset(ones_row[:, :], 1.0).then_inc(filled, 1)
            pool.wait_ge(filled, 8)

            def rope_add(b):
                pool.wait_ge(rope_mul, b + 1)
                if not isinstance(b, int) or b:
                    pool.wait_ge(qkT_ps, b)
                nc.gpsimd.tensor_tensor(qk[:, :, 0:HD], rope_a[:, :, :], rope_b[:, :, :],
                                        ALU.add).then_inc(qk_done, 1)
            rope_add(0)
            with pool.Fori(1, B) as b:
                rope_add(b)

            def add_ln(b):
                pool.wait_ge(xn_done, B + b + 1)
                nc.gpsimd.tensor_tensor(h[:, b, :], h[:, b, :], xn[:, :], ALU.add).then_inc(f_hadd, 1)
            with pool.Fori(0, B) as b:
                add_ln(b)
            with pool.Fori(0, B // 4) as g:
                pool.wait_ge(oneT_sb, 4)
                pool.wait_ge(f_y_ps, E0 * B + 4 * g)
                nc.gpsimd.tensor_copy(oneTc16[:, :], oneT[:, bass.ds(g * G4, G4)]).then_inc(oneTc_sb, 1)
                nc.gpsimd.tensor_copy(oneTc[:, :], oneT[:, bass.ds(g * G4, G4)]).then_inc(oneTc_sb, 1)

        @block.scalar
        def _(act):
            def sqrt_var(k):
                act.wait_ge(ln_step, 10 * k + 5)
                nc.scalar.activation(lnv[:, 5, :], lnv[:, 4, :], ACT.Sqrt).then_inc(sqrt_done, 1)

            def attention(l):
                base = l * B

                def evac_qk(b):
                    act.wait_ge(qkT_ps, base + b + 1)
                    act.wait_ge(s_ps, base + b)
                    nc.scalar.copy(qT[2 * SLOT:P, :, :], bank[3][2 * SLOT:P, 0:NG * T]).then_inc(q_sb, 1)
                    for j in range(2, 4):
                        nc.scalar.copy(kT[SLOT * j:SLOT * j + SLOT, :, j, :],
                                       bank[3][SLOT * j:SLOT * j + SLOT, NG * T:2 * NG * T]).then_inc(k_sb, 1)

                def evac_x(b):
                    act.wait_ge(xT_ps, base + (B if l else 0) + b + 1)
                    act.wait_ge(qkv_ps, base + b)
                    if l == 0:
                        nc.scalar.activation(xT0[:, :], bank[0][:, 0:T], ACT.Identity, bias=ln_bias0[:, :],
                                             scale=ln_scale0[:, :]).then_inc(xT_sb, 1)
                        nc.scalar.activation(xT1[0:C1, :], bank[0][0:C1, T:2 * T], ACT.Identity, bias=ln_bias1[:, :],
                                             scale=ln_scale1[:, :]).then_inc(xT_sb, 1)
                    else:
                        nc.scalar.copy(xT0[:, :], bank[0][:, 0:T]).then_inc(xT_sb, 1)
                        nc.scalar.copy(xT1[0:C1, :], bank[0][0:C1, T:2 * T]).then_inc(xT_sb, 1)

                def evac_p(b):
                    act.wait_ge(pT_ps, base + b + 1)
                    act.wait_ge(o_ps, base + b)
                    nc.scalar.copy(pT[:, 0:6, :], bank[6][0:T, 0:HALF]).then_inc(pT_sb, 1)
                    nc.scalar.copy(pT[:, 6:12, :], bank[7][0:T, 0:HALF]).then_inc(pT_sb, 1)

                def evac_o(b):
                    act.wait_ge(oT_ps, base + b + 1)
                    act.wait_ge(y_ps, base + b)
                    nc.scalar.copy(oT0[:, :], bank[0][:, 2 * T:3 * T]).then_inc(oT_sb, 1)
                    nc.scalar.copy(oT1[0:C1, :], bank[0][0:C1, 3 * T:4 * T]).then_inc(oT_sb, 1)

                def exp(b):
                    act.wait_ge(s_sub, base + b + 1)
                    nc.scalar.activation(sc[:, :, :], sc[:, :, :], ACT.Exp, scale=0.25).then_inc(e_done, 1)
                    if l == 0:
                        nc.scalar.activation(sink_e[:, b, :], sink_e[:, b, :], ACT.Exp,
                                             scale=0.25).then_inc(sink_done, 1)

                def evac_v(b):
                    act.wait_ge(qkv_ps, base + b + 1)
                    nc.scalar.copy(v_all[:, b, :, 0:HD],
                                   bank[2][0:T, 0:C].rearrange("p (h d) -> p h d", d=HD)).then_inc(v_sb, 1)

                def step(s):
                    static = isinstance(s, int)
                    if not static or 1 <= s <= B:
                        evac_qk(s - 1)
                    if not static or s < B:
                        evac_x(s)
                    if not static or 2 <= s <= B + 1:
                        evac_p(s - 2)
                    if not static or s >= 3:
                        evac_o(s - 3)
                    if not static or s < B:
                        evac_v(s)
                    if not static or 1 <= s <= B:
                        exp(s - 1)
                for s in range(3):
                    step(s)
                with act.Fori(3, B) as s:
                    step(s)
                for s in range(B, B + 3):
                    step(s)

            act.wait_ge(filled, 8)
            act.wait_ge(const_in, ALL_IN)
            sqrt_var(0)
            attention(0)
            sqrt_var(1)
            def keep_x0(b):
                act.wait_ge(xT_ps, B + b + 1)
                act.wait_ge(f_log_ps, b)
                nc.scalar.copy(xT0[:, :], bank[0][:, 0:T]).then_inc(f_xT_sb, 1)
                nc.scalar.copy(xT1[0:C1, :], bank[0][0:C1, T:2 * T]).then_inc(f_xT_sb, 1)
                nc.scalar.copy(XT0[:, bass.ds(b * T, T)], bank[0][:, 0:T]).then_inc(f_xT_sb, 1)
                nc.scalar.copy(XT1[0:C1, bass.ds(b * T, T)], bank[0][0:C1, T:2 * T]).then_inc(f_xT_sb, 1)
            keep_x0(0)
            with act.Fori(1, B) as b:
                keep_x0(b)
            act.wait_ge(f_route, 2)
            nc.scalar.activation(r1[:, :, :], r1[:, :, :], ACT.Exp).then_inc(f_exp, 1)
            def gelus(e):
                for g in range(4):
                    for c in range(FC):
                        act.wait_ge(f_hid_ps, (e * 4 + g) * FC + c + 1)
                        if c == 0:
                            if g >= 2:
                                act.wait_ge(f_y_ps, e * B + 4 * (g - 1))
                            else:
                                act.wait_ge(f_y_ps, e * B)
                        nc.scalar.activation(hT[g % 2][:, c, :], bank[c % 4][:, 0:G4], ACT.Gelu).then_inc(f_hid_sb, 1)
            gelus(0)
            with act.Fori(1, E0) as e:
                gelus(e)
            sqrt_var(2)
            attention(1)
            sqrt_var(3)
            def keep_x1(b):
                act.wait_ge(xT_ps, 3 * B + b + 1)
                act.wait_ge(f_enc_ps, b)
                nc.scalar.copy(XT0[:, bass.ds(b * T, T)], bank[0][:, 0:T]).then_inc(f_xT_sb, 1)
                nc.scalar.copy(XT1[0:C1, bass.ds(b * T, T)], bank[0][0:C1, T:2 * T]).then_inc(f_xT_sb, 1)
                act.wait_ge(f_enc_ps, b + 1)
                act.wait_ge(f_log_ps, B + b)
                nc.scalar.copy(encT[0:R1, :], bank[1][0:R1, 0:T]).then_inc(f_enc_sb, 1)
            keep_x1(0)
            with act.Fori(1, B) as b:
                keep_x1(b)
            act.wait_ge(f_route, 14)
            nc.scalar.activation(r1[:, :, 0:E1], r1[:, :, 0:E1], ACT.Exp).then_inc(f_exp, 1)
            for g in range(4):
                act.wait_ge(oneT_ps, g + 1)
                nc.scalar.copy(oneT[:, g * G4:(g + 1) * G4], bank[g % 2][0:E1, 0:G4]).then_inc(oneT_sb, 1)
            with act.Fori(0, B // 4) as g:
                act.wait_ge(f_y_ps, E0 * B + 4 * g)
                for c in range(RC):
                    act.wait_ge(f_hid_ps, E0 * 4 * FC + g * RC + c + 1)
                    nc.scalar.activation(hT[0][:, c, :], bank[c][:, 0:G4], ACT.Gelu).then_inc(f_hid_sb, 1)

        @block.vector
        def _(dve):
            def row_stats(b):
                nc.vector.bn_stats(stats[:, b, :], h[:, b, :]).then_inc(stats_done, 1)

            def ln(k, rows):
                dve.wait_ge(stats_done, rows)
                n = 10 * k
                add, sub, mul = ALU.add, ALU.subtract, ALU.mult
                nc.vector.tensor_tensor(lnv[:, 0, :], stats[:, :, 1], stats[:, :, 4], add).then_inc(ln_step, 1)
                nc.vector.tensor_tensor(lnv[:, 1, :], stats[:, :, 1], stats[:, :, 4], sub).then_inc(ln_step, 1)
                nc.vector.tensor_tensor(lnv[:, 3, :], stats[:, :, 2], stats[:, :, 5], add).then_inc(ln_step, 1)
                dve.wait_ge(ln_step, n + 3)
                nc.vector.scalar_tensor_tensor(lnv[:, 2, :], lnv[:, 1, :], 0.25, lnv[:, 1, :], mul, mul).then_inc(ln_step, 1)
                nc.vector.tensor_scalar(mean[:, :], lnv[:, 0, :], 0.5, None, mul).then_inc(ln_done, 1)
                nc.vector.tensor_scalar(lnv[:, 6, :], lnv[:, 3, :], 1.0 / C, EPS, mul, add).then_inc(ln_done, 1)
                dve.wait_ge(ln_done, 2 * k + 2)
                dve.wait_ge(ln_step, n + 4)
                nc.vector.tensor_tensor(lnv[:, 4, :], lnv[:, 6, :], lnv[:, 2, :], add).then_inc(ln_step, 1)
                dve.wait_ge(sqrt_done, k + 1)
                nc.vector.reciprocal(lnv[:, 0, :], lnv[:, 5, :]).then_inc(ln_step, 1)
                dve.wait_ge(ln_step, n + 6)
                nc.vector.tensor_tensor(lnv[:, 1, :], lnv[:, 4, :], lnv[:, 0, :], mul).then_inc(ln_step, 1)
                dve.wait_ge(ln_step, n + 7)
                nc.vector.tensor_tensor(lnv[:, 2, :], lnv[:, 1, :], lnv[:, 5, :], add).then_inc(ln_step, 1)
                dve.wait_ge(ln_step, n + 8)
                nc.vector.tensor_scalar(lnv[:, 3, :], lnv[:, 2, :], 0.5, None, mul).then_inc(ln_step, 1)
                dve.wait_ge(ln_step, n + 9)
                nc.vector.reciprocal(rstd[:, :], lnv[:, 3, :]).then_inc(ln_step, 1)
                dve.wait_ge(ln_step, n + 10)

            def normalise(b, n, also=None):
                if n is not None:
                    dve.wait_ge(xT_ps, n)
                nc.vector.tensor_scalar(xn[:, :], h[:, b, :], mean[:, bass.ds(b, 1)], rstd[:, bass.ds(b, 1)],
                                        ALU.subtract, ALU.mult).then_inc(xn_done, 1)

            def attention(l):
                base = l * B
                xbase = 2 * l * B

                def evac_k(b):
                    dve.wait_ge(qkT_ps, base + b + 1)
                    dve.wait_ge(s_ps, base + b)
                    nc.vector.tensor_copy(qT[0:2 * SLOT, :, :], bank[3][0:2 * SLOT, 0:NG * T]
                                          .rearrange("p (g t) -> p g t", g=NG)).then_inc(q_sb, 1)
                    for j in range(2):
                        nc.vector.tensor_copy(kT[SLOT * j:SLOT * j + SLOT, :, j, :],
                                              bank[3][SLOT * j:SLOT * j + SLOT, NG * T:2 * NG * T]
                                              .rearrange("p (g t) -> p g t", g=NG)).then_inc(k_sb, 1)

                def row_max(b):
                    dve.wait_ge(s_ps, base + b + 1)
                    for j in range(2):
                        nc.vector.tensor_reduce(top[:, b, 6 * j:6 * j + 6],
                                                bank[4 + j][0:T, 0:HALF].rearrange("p (h k) -> p h k", k=T),
                                                AX_X, ALU.max).then_inc(top_raw, 1)
                    dve.wait_ge(top_raw, 2 * (base + b + 1))
                    if l == 0:
                        nc.vector.tensor_tensor(top[:, b, :], top[:, b, :], sinks4[:, :], ALU.max).then_inc(top_done, 1)
                        dve.wait_ge(top_done, b + 1)
                        nc.vector.tensor_tensor(sink_e[:, b, :], sinks4[:, :], top[:, b, :], ALU.subtract)
                    dve.wait_ge(pT_ps, base + b)
                    for j in range(2):
                        ins = nc.vector.tensor_tensor(
                            sc[:, 6 * j:6 * j + 6, :], bank[4 + j][0:T, 0:HALF].rearrange("p (h k) -> p h k", k=T),
                            top[:, b, 6 * j:6 * j + 6].unsqueeze(2).to_broadcast([T, 6, T]), ALU.subtract)
                    ins.then_inc(s_sub, 1)

                def rope(b):
                    dve.wait_ge(qkv_ps, base + b + 1)
                    x = bank[1][0:T, 0:2 * C].rearrange("p (h d) -> p h d", d=HD)
                    if l == 1:
                        dve.wait_ge(qkT_ps, base + b)
                        nc.vector.tensor_copy(qk[:, :, 0:HD], x).then_inc(rope_mul, 1)
                        return
                    if not isinstance(b, int) or b:
                        dve.wait_ge(qk_done, b)
                    nc.vector.tensor_tensor(rope_a[:, :, :], x, rope_c[:, :].unsqueeze(1).to_broadcast([T, 2 * HEADS, HD]),
                                            ALU.mult)
                    xs = bank[1][0:T, 0:2 * C].rearrange("p (h i two) -> p h i two", i=HD // 2, two=2)
                    nc.vector.tensor_tensor(
                        rope_b[:, :, :].rearrange("p h (i two) -> p h i two", two=2), xs[:, :, :, ::-1],
                        rope_s[:, :].rearrange("p (i two) -> p i two", two=2).unsqueeze(1)
                        .to_broadcast([T, 2 * HEADS, HD // 2, 2]), ALU.mult).then_inc(rope_mul, 1)

                def residual(b):
                    dve.wait_ge(y_ps, base + b + 1)
                    y = bank[0][0:T, 4 * T:4 * T + C]
                    if l == 0:
                        nc.vector.scalar_tensor_tensor(h[:, b, :], y, rezero[:, 0:1], h[:, b, :], ALU.mult,
                                                       ALU.add).then_inc(h_done, 1)
                    else:
                        nc.vector.tensor_tensor(h[:, b, :], y, h[:, b, :], ALU.add).then_inc(h_done, 1)
                    dve.wait_ge(h_done, base + b + 1)
                    row_stats(b)

                def weigh(b):
                    dve.wait_ge(o_ps, base + b + 1)
                    x = bank[2][0:T, C:C + HEADS * (HD + 1)].rearrange("p (h d) -> p h d", d=HD + 1)
                    if l == 0:
                        dve.wait_ge(sink_done, b + 1)
                        nc.vector.tensor_tensor(den[:, :], x[:, :, HD], sink_e[:, b, :], ALU.add).then_inc(den_done, 1)
                        dve.wait_ge(den_done, b + 1)
                        nc.vector.reciprocal(rden[:, :], den[:, :]).then_inc(rden_done, 1)
                    else:
                        nc.vector.reciprocal(rden[:, :], x[:, :, HD]).then_inc(rden_done, 1)
                    dve.wait_ge(rden_done, base + b + 1)
                    dve.wait_ge(oT_ps, base + b)
                    nc.vector.tensor_tensor(o[:, :, :], x[:, :, 0:HD],
                                            rden[:, :].unsqueeze(2).to_broadcast([T, HEADS, HD]),
                                            ALU.mult).then_inc(o_done, 1)

                def step(s):
                    static = isinstance(s, int)
                    if not static or 1 <= s <= B:
                        evac_k(s - 1)
                        row_max(s - 1)
                    if not static or s < B:
                        rope(s)
                    if not static or s >= 3:
                        residual(s - 3)
                    if not static or 2 <= s <= B + 1:
                        weigh(s - 2)
                    if not static or s < B - 1:
                        normalise(s + 1, xbase + s + 1)

                normalise(0, xbase)
                for s in range(3):
                    step(s)
                with dve.Fori(3, B - 1) as s:
                    step(s)
                for s in range(B - 1, B + 3):
                    step(s)

            dve.wait_ge(const_in, ALL_IN)
            dve.wait_ge(filled, 8)
            nc.vector.tensor_copy(ident16[:, :], ident[0:T, 0:T])
            nc.vector.tensor_copy(mask16[:, :].rearrange("p (h k) -> p h k", k=T),
                                  mask_in[:, :].unsqueeze(1).to_broadcast([T, 6, T]))
            nc.vector.tensor_copy(sel16[:, :, :].rearrange("p c n -> p (c n)"), sel_in[:, :])
            nc.vector.tensor_scalar(sinks4[:, :], sinks[:, :], 4.0, None, ALU.mult)
            for i in range(B // 2):
                dve.wait_ge(patch_ps, i + 1)
                nc.vector.tensor_copy(h[0:NPATCH, 2 * i, :], bank[i % 2][0:NPATCH, 0:C])
                nc.vector.tensor_copy(h[0:NPATCH, 2 * i + 1, :], bank[i % 2][64:64 + NPATCH, 0:C]).then_inc(patch_sb, 1)
                dve.wait_ge(patch_sb, i + 1)
                row_stats(2 * i)
                row_stats(2 * i + 1)
            ln(0, B)
            attention(0)
            ln(1, 2 * B)

            normalise(0, B)
            with dve.Fori(1, B) as b:
                dve.wait_ge(f_hadd, b)
                normalise(b, B + b)
            dve.wait_ge(f_log_ps, B)
            r = [10 * 1]

            def seq(ins):
                r[0] += 1
                ins.then_inc(f_route, 1)
            bc = lambda x, n: x.unsqueeze(2).to_broadcast([T, B, n])
            logit0 = bank[2][0:T, 0:B * E0].rearrange("p (b e) -> p b e", e=E0)
            nexp = expert_no[:, :].unsqueeze(1).to_broadcast([T, B, E0])
            nc.vector.tensor_reduce(rs[0][:, :], logit0, AX_X, ALU.max).then_inc(f_route, 1)
            dve.wait_ge(f_route, 1)
            nc.vector.tensor_tensor(r1[:, :, :], logit0, bc(rs[0][:, :], E0), ALU.subtract).then_inc(f_route, 1)
            dve.wait_ge(f_exp, 1)
            nc.vector.tensor_reduce(rs[1][:, :], r1[:, :, :], AX_X, ALU.add).then_inc(f_route, 1)
            dve.wait_ge(f_route, 3)
            nc.vector.reciprocal(rs[2][:, :], rs[1][:, :]).then_inc(f_route, 1)
            dve.wait_ge(f_route, 4)
            nc.vector.tensor_tensor(r1[:, :, :], r1[:, :, :], bc(rs[2][:, :], E0), ALU.mult).then_inc(f_route, 1)
            cnt = 5
            for k in range(2):
                dve.wait_ge(f_route, cnt)
                nc.vector.tensor_reduce(rs[0][:, :], r1[:, :, :], AX_X, ALU.max).then_inc(f_route, 1)
                dve.wait_ge(f_route, cnt + 1)
                nc.vector.tensor_tensor(r2[:, :, :], r1[:, :, :], bc(rs[0][:, :], E0), ALU.is_lt).then_inc(gate_done, 1)
                dve.wait_ge(gate_done, 4 * k + 1)
                nc.vector.scalar_tensor_tensor(r3[:, :, :], r2[:, :, :], float(E0), nexp, ALU.mult, ALU.add).then_inc(gate_done, 1)
                dve.wait_ge(gate_done, 4 * k + 2)
                nc.vector.tensor_reduce(rs[1][:, :], r3[:, :, :], AX_X, ALU.min).then_inc(gate_done, 1)
                dve.wait_ge(gate_done, 4 * k + 3)
                nc.vector.tensor_tensor(r2[:, :, :], nexp, bc(rs[1][:, :], E0), ALU.is_equal).then_inc(gate_done, 1)
                dve.wait_ge(gate_done, 4 * k + 4)
                if k == 0:
                    nc.vector.tensor_tensor(gate[:, :, :], r2[:, :, :], r1[:, :, :], ALU.mult).then_inc(f_route, 1)
                    nc.vector.scalar_tensor_tensor(r1[:, :, :], r2[:, :, :], -2.0, r1[:, :, :], ALU.mult, ALU.add) \
                        .then_inc(f_route, 1)
                    cnt = 8
                else:
                    nc.vector.tensor_tensor(r3[:, :, :], r2[:, :, :], r1[:, :, :], ALU.mult).then_inc(f_route, 1)
                    dve.wait_ge(f_route, cnt + 2)
                    nc.vector.tensor_tensor(gate[:, :, :], gate[:, :, :], r3[:, :, :], ALU.add).then_inc(f_route, 1)
            dve.wait_ge(f_route, 11)
            dve.wait_ge(f_hadd, B)
            def add_expert(e):
                for b in range(B):
                    dve.wait_ge(f_y_ps, e * B + b + 1)
                    if b == 0:
                        dve.wait_ge(f_acc, e * B)
                    nc.vector.scalar_tensor_tensor(h[:, b, :], bank[4 + b % 4][0:T, 0:C],
                                                   gate[:, b, bass.ds(e, 1)], h[:, b, :], ALU.mult,
                                                   ALU.add).then_inc(f_acc, 1)
            add_expert(0)
            with dve.Fori(1, E0) as e:
                add_expert(e)
            dve.wait_ge(f_acc, E0 * B)
            for b in range(B):
                row_stats(b)
            ln(2, 3 * B)
            attention(1)
            ln(3, 4 * B)

            normalise(0, 3 * B)
            with dve.Fori(1, B) as b:
                normalise(b, 3 * B + b)
            dve.wait_ge(f_log_ps, 2 * B)
            logit1 = bank[2][0:T, 0:B * E1].rearrange("p (b e) -> p b e", e=E1)
            q1, q2, q3 = (x[:, :, 0:E1] for x in (r1, r2, r3))
            nexp1 = expert_no[:, 0:E1].unsqueeze(1).to_broadcast([T, B, E1])
            nc.vector.tensor_reduce(rs[0][:, :], logit1, AX_X, ALU.max).then_inc(f_route, 1)
            dve.wait_ge(f_route, 12)
            nc.vector.tensor_tensor(q2, logit1, bc(rs[0][:, :], E1), ALU.is_lt).then_inc(f_route, 1)
            nc.vector.tensor_tensor(q1, logit1, bc(rs[0][:, :], E1), ALU.subtract).then_inc(f_route, 1)
            dve.wait_ge(f_route, 14)
            nc.vector.scalar_tensor_tensor(q3, q2, float(E0), nexp1, ALU.mult, ALU.add).then_inc(f_route, 1)
            dve.wait_ge(f_route, 15)
            nc.vector.tensor_reduce(rs[1][:, :], q3, AX_X, ALU.min).then_inc(f_route, 1)
            dve.wait_ge(f_route, 16)
            nc.vector.tensor_tensor(one_hot1[:, :, :], nexp1, bc(rs[1][:, :], E1), ALU.is_equal).then_inc(f_route, 1)
            dve.wait_ge(f_exp, 2)
            nc.vector.tensor_reduce(rs[2][:, :], q1, AX_X, ALU.add).then_inc(f_route, 1)
            dve.wait_ge(f_route, 18)
            nc.vector.reciprocal(rs[3][:, :], rs[2][:, :]).then_inc(f_route, 1)
            dve.wait_ge(f_route, 19)

            def weighted(g):
                for c in range(RC):
                    dve.wait_ge(f_hid_sb, E0 * 4 * FC + g * RC + c + 1)
                    dve.wait_ge(mask_ps, g * RC + c + 1)
                    if c == 0:
                        dve.wait_ge(f_y_ps, E0 * B + 4 * g)
                    nc.vector.tensor_tensor(gm[:, c, :], hT[0][:, c, :], bank[4 + c % 2][:, 0:G4],
                                            ALU.mult).then_inc(gm_done, 1)
                for j in range(4):
                    dve.wait_ge(f_y_ps, E0 * B + 4 * g + j + 1)
                    b = 4 * g + j
                    nc.vector.scalar_tensor_tensor(yout[:, b, :], bank[6 + j % 2][0:T, 0:C],
                                                   rs[3][:, bass.ds(b, 1)], h[:, b, :], ALU.mult,
                                                   ALU.add).then_inc(yout_done, 1)
            with dve.Fori(0, B // 4) as g:
                weighted(g)

        @block.tensor
        def _(pe):
            mm = nc.tensor.matmul

            def product(dst, pairs, last):
                for i, (lhsT, rhs) in enumerate(pairs):
                    ins = mm(dst, lhsT, rhs, start=(i == 0), stop=(i == len(pairs) - 1))
                if last is not None:
                    ins.then_inc(last, 1)

            def turn_x(b, n, frees):
                pe.wait_ge(xn_done, n)
                for free, free_at in frees:
                    if not isinstance(free_at, int) or free_at > 0:
                        pe.wait_ge(free, free_at)
                nc.tensor.transpose(bank[0][:, 0:T], xn[:, 0:P], ident[0:T, 0:T])
                nc.tensor.transpose(bank[0][0:C1, T:2 * T], xn[:, P:C], ident[0:T, 0:T]).then_inc(xT_ps, 1)

            def attention(l):
                base = l * B

                def turn_qk(b):
                    if l == 0:
                        pe.wait_ge(qk_done, b + 1)
                    else:
                        pe.wait_ge(rope_mul, base + b + 1)
                    pe.wait_ge(q_sb, 2 * (base + b))
                    pe.wait_ge(k_sb, 4 * (base + b))
                    for g in range(2 * NG):
                        ins = nc.tensor.transpose(bank[3][:, g * T:(g + 1) * T],
                                                  qk[:, 4 * g:4 * g + 4, :].rearrange("p h d -> p (h d)"),
                                                  ident[0:T, 0:T])
                    ins.then_inc(qkT_ps, 1)

                def turn_p(b):
                    pe.wait_ge(e_done, base + b + 1)
                    pe.wait_ge(pT_sb, 2 * (base + b))
                    for i in range(HEADS):
                        ins = nc.tensor.transpose(bank[6 + i // 6][0:T, (i % 6) * T:(i % 6 + 1) * T], sc[:, i, :],
                                                  ident[0:T, 0:T])
                    ins.then_inc(pT_ps, 1)

                def turn_o(b):
                    pe.wait_ge(o_done, base + b + 1)
                    pe.wait_ge(xT_sb, 2 * (base + (min(b + 4, B) if isinstance(b, int) else b + 4)))
                    of = o[:, :, :].rearrange("p h d -> p (h d)")
                    nc.tensor.transpose(bank[0][:, 2 * T:3 * T], of[:, 0:P], ident[0:T, 0:T])
                    nc.tensor.transpose(bank[0][0:C1, 3 * T:4 * T], of[:, P:C], ident[0:T, 0:T]).then_inc(oT_ps, 1)

                def scores(b):
                    pe.wait_ge(q_sb, 2 * (base + b + 1))
                    pe.wait_ge(k_sb, 4 * (base + b + 1))
                    pe.wait_ge(s_sub, base + b)
                    parts = [(0, 0, 4, 0), (1, 0, 2, 0), (1, 2, 4, 1), (2, 0, 4, 1)]
                    for g, a, z, half in parts:
                        col = (4 * g + a) * T - half * HALF
                        first = (g, a) in ((0, 0), (1, 2))
                        ins = mm(bank[4 + half][0:T, col:col + (z - a) * T], qT[:, g, :],
                                 kT[:, g, a:z, :].rearrange("p h t -> p (h t)"), start=True, stop=(l == 1),
                                 skip_group_check=True)
                        if l == 0:
                            ins = mm(bank[4 + half][0:T, col:col + (z - a) * T], ident16[:, :],
                                     mask16[:, 0:(z - a) * T], start=False, stop=True, skip_group_check=True)
                    ins.then_inc(s_ps, 1)

                def qkv(b):
                    pe.wait_ge(xT_sb, 2 * (base + b + 1))
                    pe.wait_ge(v_sb, base + b)
                    pe.wait_ge(rope_mul, base + b)
                    if not isinstance(b, int) or base + b > 2:
                        pe.wait_ge(o_done, base + b - 2)
                    product(bank[1][0:T, 0:2 * C], [(xT0[:, :], qkv_w0[l][:, 0:2 * C]), (xT1[:, :], qkv_w1[l][:, 0:2 * C])], None)
                    product(bank[2][0:T, 0:C], [(xT0[:, :], qkv_w0[l][:, 2 * C:]), (xT1[:, :], qkv_w1[l][:, 2 * C:])], qkv_ps)

                def project(b):
                    pe.wait_ge(oT_sb, 2 * (base + b + 1))
                    pe.wait_ge(h_done, base + b)
                    product(bank[0][0:T, 4 * T:4 * T + C], [(oT0[:, :], proj_w0[l][:, :]), (oT1[:, :], proj_w1[l][:, :])], y_ps)

                def values(b):
                    pe.wait_ge(pT_sb, 2 * (base + b + 1))
                    pe.wait_ge(v_sb, base + (min(b + 3, B) if isinstance(b, int) else b + 3))
                    pe.wait_ge(o_done, base + b)
                    for i in range(HEADS):
                        c = C + i * (HD + 1)
                        ins = mm(bank[2][0:T, c:c + HD + 1], pT[:, i, :], v_all[:, b, i, :], start=True, stop=True)
                    ins.then_inc(o_ps, 1)

                def step(s):
                    static = isinstance(s, int)
                    if not static or 1 <= s <= B:
                        turn_qk(s - 1)
                    if not static or s < B:
                        turn_x(s, 2 * l * B + s + 1, [(xT_sb, 2 * (base + s)), (h_done, base + s - 3)])
                    if not static or 2 <= s <= B + 1:
                        turn_p(s - 2)
                    if not static or s >= 3:
                        turn_o(s - 3)
                    if not static or 1 <= s <= B:
                        scores(s - 1)
                    if not static or s < B:
                        qkv(s)
                    if not static or s >= 3:
                        project(s - 3)
                    if not static or 2 <= s <= B + 1:
                        values(s - 2)

                for s in range(3):
                    step(s)
                with pe.Fori(3, B) as s:
                    step(s)
                for s in range(B, B + 3):
                    step(s)

            pe.wait_ge(const_in, ALL_IN)
            pe.wait_ge(filled, 8)
            for i in range(B // 2):
                if i >= 2:
                    pe.wait_ge(patch_sb, i - 1)
                product(bank[i % 2][0:100, 0:C], [(patches[:, c, i, 0:100], w_tok[:, c, :]) for c in range(PF)], patch_ps)
            pe.wait_ge(patch_sb, B // 2)
            attention(0)

            def route0(b):
                pe.wait_ge(f_xT_sb, 4 * (b + 1))
                product(bank[2][0:T, bass.ds(b * E0, E0)], [(xT0[:, :], router0[:, :]), (xT1[0:C1, :], router1[:, :])], f_log_ps)
            turn_x(0, B + 1, [(h_done, B)])
            with pe.Fori(1, B) as b:
                route0(b - 1)
                turn_x(b, B + b + 1, [(f_xT_sb, 4 * b)])
            route0(B - 1)
            pe.wait_ge(f_xT_sb, 4 * B)
            pe.wait_ge(f_route, 2)

            def hidden(p, e, g):
                for c in range(FC):
                    n = (e * 4 + g) * FC + c
                    back = 3 if c >= 4 else 1 if c < 2 else 5
                    if not isinstance(n, int) or n >= FC or c >= 4:
                        pe.wait_ge(f_hid_sb, n - back)
                    cols = slice(g * G4, (g + 1) * G4)
                    product(bank[c % 4][:, 0:G4], [(w1a[p][:, c * P:(c + 1) * P], XT0[:, cols]),
                                                   (w1b[p][:, c * P:(c + 1) * P], XT1[:, cols])], f_hid_ps)

            def down(p, e, g):
                pe.wait_ge(f_hid_sb, (e * 4 + g + 1) * FC)
                for j in range(4):
                    if not (isinstance(e, int) and e == 0 and g == 0):
                        pe.wait_ge(f_acc, e * B + 4 * (g - 1) + j + 1)
                    product(bank[4 + j][0:T, 0:C],
                            [(hT[g % 2][:, c, j * T:(j + 1) * T], w2a[p][:, c, :]) for c in range(FC)]
                            + [(ones_row[:, :], b2a[p][:, :])], f_y_ps)

            def expert(p, e, n):
                pe.wait_ge(moe_in[p], n)
                hidden(p, e, 0)
                for g in range(1, 4):
                    hidden(p, e, g)
                    down(p, e, g - 1)
                down(p, e, 3)
            expert(0, 0, 80)
            expert(1, 1, 80)
            with pe.Fori(2, E0 - 1, 2) as e:
                for p in range(2):
                    expert(p, e + p, 40 * (e + 2))

            pe.wait_ge(f_acc, E0 * B)
            attention(1)

            def encode(b):
                pe.wait_ge(f_xT_sb, 4 * B + 2 * (b + 1))
                pe.wait_ge(f_enc_sb, b) if not isinstance(b, int) or b else None
                cols = bass.ds(b * T, T)
                product(bank[1][0:R1, 0:T], [(enc_w0[:, :], XT0[:, cols]), (enc_w1[:, :], XT1[:, cols])], f_enc_ps)

            def route1(b):
                pe.wait_ge(f_enc_sb, b + 1)
                product(bank[2][0:T, bass.ds(b * E1, E1)], [(encT[:, :], sw_w[:, :])], f_log_ps)
            turn_x(0, 3 * B + 1, [(h_done, 2 * B)])
            encode(0)
            turn_x(1, 3 * B + 2, [(f_xT_sb, 4 * B + 2)])
            route1(0)
            with pe.Fori(2, B) as b:
                encode(b - 1)
                turn_x(b, 3 * B + b + 1, [(f_xT_sb, 4 * B + 2 * b)])
                route1(b - 1)
            encode(B - 1)
            route1(B - 1)
            for g in range(4):
                pe.wait_ge(f_route, 17)
                if g >= 2:
                    pe.wait_ge(oneT_sb, g - 1)
                for j in range(4):
                    ins = nc.tensor.transpose(bank[g % 2][0:E1, j * T:(j + 1) * T], one_hot1[:, 4 * g + j, :], ident[0:T, 0:T])
                ins.then_inc(oneT_ps, 1)
            pe.wait_ge(oneT_sb, 4)

            def dense(g):
                cols = bass.ds(g * G4, G4)
                for c in range(RC):
                    pe.wait_ge(f_hid_sb, E0 * 4 * FC + g * RC)
                    product(bank[c][:, 0:G4], [(f1_w0[:, c * P:(c + 1) * P], XT0[:, cols]),
                                               (f1_w1[:, c * P:(c + 1) * P], XT1[:, cols])], f_hid_ps)
                pe.wait_ge(oneTc_sb, 2 * (g + 1))
                for c in range(RC):
                    pe.wait_ge(gm_done, g * RC + max(c - 1, 0))
                    product(bank[4 + c % 2][:, 0:G4], [(sel16[:, c, :], oneTc16[:, :])], mask_ps)
                pe.wait_ge(gm_done, (g + 1) * RC)
                for j in range(4):
                    pe.wait_ge(yout_done, 4 * g + max(j - 1, 0))
                    tok = slice(j * T, (j + 1) * T)
                    product(bank[6 + j % 2][0:T, 0:C], [(gm[:, c, tok], f1_w2[:, c, :]) for c in range(RC)]
                            + [(oneTc[:, tok], f1_b2[:, :])], f_y_ps)
            dense(0)
            with pe.Fori(1, B // 4) as g:
                dense(g)


def _layout(inputs):
    import numpy as np
    a = {k: np.asarray(v) for k, v in inputs.items()}
    f = np.ascontiguousarray
    hp = 6
    x = a["x"].reshape(B, 3, hp, 16, hp, 16).transpose(1, 3, 5, 0, 2, 4).reshape(PF, P, B // 2, 2, NPATCH)
    patch = np.zeros((PF, P, B // 2, 2, 64), x.dtype)
    patch[..., :NPATCH] = x
    d = {
        "patchT": f(patch.transpose(1, 0, 2, 3, 4).reshape(P, PF, B // 2, P)),
        "wtokT": f(a["L0_tok_W"].T.reshape(PF, P, C).transpose(1, 0, 2)),
        "txt": f(a["txt"]),
        "qkv0": f(a["L0_attn_W_attn"]), "bqkv0": f(a["L0_attn_b_attn"].reshape(1, -1)),
        "proj0": f(a["L0_attn_W_proj"]), "bproj0": f(a["L0_attn_b_proj"].reshape(1, -1)),
        "nscale": f(a["L0_attn_norm_scale"].reshape(-1, 1)), "nbias": f(a["L0_attn_norm_bias"].reshape(-1, 1)),
        "sinks": f(a["L0_attn_sinks"].reshape(1, -1)), "rezero": f(a["L0_attn_rezero"].reshape(1, 1)),
        "wrT": f(a["L0_ffn_Wr"].T), "w1": f(a["L0_ffn_W1"]), "b1": f(a["L0_ffn_b1"]),
        "w2": f(a["L0_ffn_W2"]), "b2": f(a["L0_ffn_b2"]),
        "qkv1": f(a["L1_attn_qkv_weight"].T), "bqkv1": f(a["L1_attn_qkv_bias"].reshape(1, -1)),
        "proj1": f(a["L1_attn_proj_weight"].T), "bproj1": f(a["L1_attn_proj_bias"].reshape(1, -1)),
        "encw": f(a["L1_ffn_enc_w"]), "encb": f(a["L1_ffn_enc_b"].reshape(1, -1)),
        "sww": f(a["L1_ffn_sw_w"]), "swb": f(a["L1_ffn_sw_b"].reshape(1, -1)),
        "f1w1": f(a["L1_ffn_w1"].transpose(1, 0, 2).reshape(C, E1 * R1)), "f1b1": f(a["L1_ffn_b1"].reshape(1, -1)),
        "f1w2": f(a["L1_ffn_w2"].reshape(E1 * R1, C)), "f1b2": f(a["L1_ffn_b2"]),
    }
    ang = np.outer(np.arange(T, dtype=np.float32),
                   (1.0 / np.float32(10000.0) ** (np.arange(0, HD, 2, dtype=np.float32) / HD)).astype(np.float32))
    cos, sin = np.cos(ang).astype(np.float32), np.sin(ang).astype(np.float32)
    d["rope_c"] = f(np.repeat(cos, 2, axis=1))
    d["rope_s"] = f(np.stack([-sin, sin], axis=-1).reshape(T, HD))
    d["ident"] = np.eye(P, dtype=np.float32)
    d["mask"] = np.triu(np.full((T, T), MASKED, np.float32), 1)
    d["expert_no"] = np.arange(E0, dtype=np.float32).reshape(1, -1)
    sel = np.zeros((E1, RC * P), np.float32)
    for e in range(E1):
        sel[e, e * R1:(e + 1) * R1] = 1.0
    d["sel"] = sel
    return d


def kernel(**inputs):
    import concourse.bacc as _bacc
    from concourse import mybir as _mybir
    from concourse.bass_utils import run_bass_kernel_spmd as _run

    nc = _bacc.Bacc("TRN2", target_bir_lowering=False, num_devices=1)
    data = _layout(inputs)
    arrays, aps = {}, {}
    for name, a in data.items():
        arrays[f"in_{name}_dram"] = a
        aps[name] = nc.dram_tensor(f"in_{name}_dram", a.shape, _mybir.dt.from_np(a.dtype), kind="ExternalInput").ap()
    out = nc.dram_tensor("out_0_dram", (B, T, C), F32, kind="ExternalOutput").ap()
    fusion_kernel(nc, aps, out)
    r = _run(nc, [arrays], core_ids=[0])
    return r.results[0]["out_0_dram"]
```

```python
from contextlib import ExitStack

import concourse.bass as bass
from concourse import mybir

ALU = mybir.AluOpType
ACT = mybir.ActivationFunctionType
F32 = mybir.dt.float32
BF16 = mybir.dt.bfloat16
AX_X = mybir.AxisListType.X

P = 128
B = 16
NPATCH = 36
NTXT = 32
T = NPATCH + NTXT
C = 192
C1 = C - P
HEADS = 12
HD = C // HEADS
SLOT = 32
NG = HEADS // 4
HALF = 6 * T
PF = 6
E0, F0 = 16, 768
E1, R1 = 8, 64
FC = F0 // P
TOK = B * T
TOPK = 2
S = P
NBLK = (TOPK * TOK + E0 * (S - 1)) // S
NPICK = TOPK * B
MAXB = -(-TOK // S)
ROUND = 12582912.0
U32 = mybir.dt.uint32
I32 = mybir.dt.int32
RC = E1 * R1 // P
G4 = 4 * T
EPS = 1e-5
MASKED = -1.0e30


def fusion_kernel(nc, t, out):
    with ExitStack() as ctx:
        def sb(name, shape, dt=F32):
            return ctx.enter_context(nc.sbuf_tensor(name, shape, dt))

        def sem(name):
            return ctx.enter_context(nc.semaphore(name))

        bank = [ctx.enter_context(nc.psum_tensor(f"bank{i}", [P, 512], F32)) for i in range(8)]

        ident = sb("ident", [P, P])
        ident16 = sb("ident16", [T, T], BF16)
        mask16 = sb("mask16", [T, HALF], BF16)
        mask_in = sb("mask_in", [T, T])
        sel_in = sb("sel_in", [E1, RC * P])
        rope_c = sb("rope_c", [T, HD])
        rope_s = sb("rope_s", [T, HD])
        patches = sb("patches", [P, PF, B // 2, P])
        w_tok = sb("w_tok", [P, PF, C])
        qkv_w0 = [sb(f"qkv_w0_{l}", [P, 3 * C]) for l in range(2)]
        qkv_w1 = [sb(f"qkv_w1_{l}", [C1 + 1, 3 * C]) for l in range(2)]
        proj_w = [sb(f"proj_w{l}", [P, NG, C]) for l in range(2)]
        proj_b = [sb(f"proj_b{l}", [T, C]) for l in range(2)]
        ln_scale0, ln_scale1 = sb("ln_scale0", [P, 1]), sb("ln_scale1", [C1, 1])
        ln_bias0, ln_bias1 = sb("ln_bias0", [P, 1]), sb("ln_bias1", [C1, 1])
        sinks = sb("sinks", [T, HEADS])
        sinks4 = sb("sinks4", [T, HEADS])
        rezero = sb("rezero", [T, 1])
        router0, router1 = sb("router0", [P, E0]), sb("router1", [C1, E0])
        enc_w0, enc_w1 = sb("enc_w0", [P, R1]), sb("enc_w1", [C1 + 1, R1])
        sw_w = sb("sw_w", [R1 + 1, E1])
        f1_w0, f1_w1 = sb("f1_w0", [P, E1 * R1]), sb("f1_w1", [C1 + 1, E1 * R1])
        f1_w2 = sb("f1_w2", [P, RC, C])
        f1_b2 = sb("f1_b2", [E1, C])
        sel16 = sb("sel16", [E1, RC, P], BF16)

        h = sb("h", [T, B, C])
        stats = sb("stats", [T, B, 6])
        lnv = sb("lnv", [T, 8, B])
        mean, rstd = sb("mean", [T, B]), sb("rstd", [T, B])

        xn = sb("xn", [T, C])
        xT0, xT1 = sb("xT0", [P, T]), sb("xT1", [C1 + 1, T])
        v_all = sb("v_all", [T, B, HEADS, HD])
        v_cur = sb("v_cur", [T, HEADS, SLOT])
        rope_a, rope_b = sb("rope_a", [T, 2 * HEADS, HD]), sb("rope_b", [T, 2 * HEADS, HD])
        qk = sb("qk", [T, 2 * HEADS, SLOT])
        qT = sb("qT", [P, NG, T])
        kT = sb("kT", [P, NG, 4, T])
        top = sb("top", [T, B, HEADS])
        sink_e = sb("sink_e", [T, B, HEADS])
        sc = sb("sc", [T, HEADS, T])
        pT = sb("pT", [T, HEADS, T])
        prob = sb("prob", [T, HEADS, T])
        den, rden = sb("den", [T, HEADS]), sb("rden", [T, HEADS])
        oT = sb("oT", [P, NG, T])

        XT0, XT1 = sb("XT0", [P, B * T]), sb("XT1", [C1 + 1, B * T])
        encT = sb("encT", [R1 + 1, T])
        lg = sb("lg", [T, B, E0])
        r1, r2, r3 = (sb(f"route{i}", [T, B, E0]) for i in range(3))
        one_hot1 = sb("one_hot1", [T, B, E1])
        oneT = sb("oneT", [E1, B * T])
        oneTc = sb("oneTc", [E1, G4])
        oneTc16 = sb("oneTc16", [E1, G4], BF16)
        rs = [sb(f"rs{i}", [T, B]) for i in range(4)]
        iota = sb("iota", [P, P])
        tri_in = sb("tri_in", [T, T])
        tri16, ones16 = sb("tri16", [T, T], BF16), sb("ones16", [T, T], BF16)
        tick = sb("tick", [1, 1])
        tok1, pad = sb("tok1", [T, 1]), sb("pad", [P, NBLK])
        pick = [sb(f"pick{k}", [T, B, E0]) for k in range(TOPK)]
        gates = sb("gates", [T, TOPK, B])
        picks16 = sb("picks16", [T, B, E0], BF16)
        total, run_a, run_b = (sb(x, [T, B, E0]) for x in ("total", "run_a", "run_b"))
        limits = sb("limits", [T, MAXB])
        over = sb("over", [T, E0, MAXB])
        nblk, blk_a, blk_b, first_slot = (sb(x, [T, E0]) for x in ("nblk", "blk_a", "blk_b", "first_slot"))
        place = sb("place", [T, B, E0])
        slot, blk_of, in_blk = (sb(x, [T, TOPK, B]) for x in ("slot", "blk_of", "in_blk"))
        in_hot = sb("in_hot", [T, NPICK, S], BF16)
        blk_hot = sb("blk_hot", [T, NPICK, NBLK], BF16)
        named = sb("named", [T, NPICK, 2, NBLK], BF16)
        passed = sb("passed", [1, NBLK, E0])
        expert_f = sb("expert_f", [1, NBLK])
        expert_i = sb("expert_i", [1, NBLK], I32)
        who = sb("who", [P, 2, NBLK])
        wt = [sb(f"wt{i}", [P, NBLK]) for i in range(4)]
        row_in, row_out = sb("row_in", [P, NBLK], U32), sb("row_out", [P, NBLK], U32)
        idx_in = [sb(f"idx_in{i}", [P, 1], U32) for i in range(2)]
        idx_out = [sb(f"idx_out{i}", [P, 1], U32) for i in range(2)]
        xg = [sb(f"xg{i}", [P, C]) for i in range(2)]
        xs0 = [sb(f"xs0_{i}", [P, S]) for i in range(2)]
        xs1 = [sb(f"xs1_{i}", [C1 + 1, S]) for i in range(2)]
        w1a = [sb(f"w1a{i}", [P, F0]) for i in range(2)]
        w1b = [sb(f"w1b{i}", [C1 + 1, F0]) for i in range(2)]
        w2a = [sb(f"w2a{i}", [P, FC, C]) for i in range(2)]
        b2a = [sb(f"b2a{i}", [P, C]) for i in range(2)]
        hb = [sb(f"hb{i}", [P, FC, S]) for i in range(2)]
        ys = [sb(f"ys{i}", [P, C]) for i in range(2)]
        xn_all = sb("xn_all", [T, B, C])
        yout = v_all[:, :, :, :].rearrange("t b h d -> t b (h d)")
        yk = [yout, xn_all]
        pixels = patches[:, :, :, :].rearrange("p c i n -> p (c i n)")
        hid, gm = (pixels[:, i * RC * G4:(i + 1) * RC * G4].rearrange("p (c n) -> p c n", c=RC) for i in range(2))

        const_in, ln_stored, picks_in, out_sent = (sem(x) for x in ("const_in", "ln_stored", "picks_in", "out_sent"))
        w1_in = [sem(f"w1_in{i}") for i in range(2)]
        w2_in = [sem(f"w2_in{i}") for i in range(2)]
        x_in = [sem(f"x_in{i}") for i in range(2)]
        y_out = [sem(f"y_out{i}") for i in range(2)]
        (ln_kept, pick_done, count_ps, sort_step, who_ready, rb_set, who_ps, rows_ready, idx_set, xg_ps, xs_sb, hid_ps, hid_sb, who_part,
         blk_ps, ys_done, moe_done) = (sem(x) for x in (
             "ln_kept", "pick_done", "count_ps", "sort_step", "who_ready", "rb_set", "who_ps", "rows_ready", "idx_set", "xg_ps",
             "xs_sb", "hid_ps", "hid_sb", "who_part", "blk_ps", "ys_done", "moe_done"))
        (filled, patch_ps, patch_sb, stats_done, sqrt_done, ln_step, ln_done, xn_done, xT_ps, xT_sb, v_ps, qk_ps, v_sb,
         rope_mul, qk_done, qkT_ps, q_sb, k_sb, s_ps, top_raw, top_done, s_sub, e_done, sink_done, pT_ps, pT_sb, o_ps,
         den_done, rden_done, p_done, v_set, b_added, oT_sb, y_ps, h_done) = (sem(x) for x in (
             "filled", "patch_ps", "patch_sb", "stats_done", "sqrt_done", "ln_step", "ln_done", "xn_done", "xT_ps",
             "xT_sb", "v_ps", "qk_ps", "v_sb", "rope_mul", "qk_done", "qkT_ps", "q_sb", "k_sb", "s_ps", "top_raw",
             "top_done", "s_sub", "e_done", "sink_done", "pT_ps", "pT_sb", "o_ps", "den_done", "rden_done", "p_done",
             "v_set", "b_added", "oT_sb", "y_ps", "h_done"))
        (f_xT_ps, f_xT_sb, f_hadd, f_enc_ps, f_enc_sb, f_log_ps, f_route, f_exp, gate_done,
         f_hid_ps, f_hid_sb, f_y_ps, f_acc, oneT_ps, oneT_sb, oneTc_sb, mask_ps, gm_done, yout_done) = (sem(x) for x in (
             "f_xT_ps", "f_xT_sb", "f_hadd", "f_enc_ps", "f_enc_sb", "f_log_ps", "f_route", "f_exp", "gate_done",
             "f_hid_ps", "f_hid_sb", "f_y_ps", "f_acc", "oneT_ps", "oneT_sb", "oneTc_sb", "mask_ps", "gm_done",
             "yout_done"))

        ln_rows = nc.dram_tensor("ln_rows", (TOK, C), F32, kind="Internal").ap()
        y_rows = nc.dram_tensor("y_rows", (TOPK * TOK + NBLK * S, C), F32, kind="Internal").ap()

        consts = [
            (w_tok[:, :, :], t["wtokT"]), (patches[:, :, :, :], t["patchT"]), (ident[:, :], t["ident"]),
            (h[NPATCH:T, :, :], t["txt"].rearrange("b n c -> n b c")),
            (qkv_w0[0][:, :], t["qkv0"][0:P]), (qkv_w1[0][0:C1, :], t["qkv0"][P:C]), (qkv_w1[0][C1:C1 + 1, :], t["bqkv0"]),
            (ln_scale0[:, :], t["nscale"][0:P]), (ln_scale1[:, :], t["nscale"][P:C]),
            (ln_bias0[:, :], t["nbias"][0:P]), (ln_bias1[:, :], t["nbias"][P:C]),
            (rope_c[:, :], t["rope_c"]), (rope_s[:, :], t["rope_s"]),
            (mask_in[:, :], t["mask"]), (sel_in[:, :], t["sel"]),
            (proj_w[0][:, :, :], t["proj0"]), (proj_b[0][:, :], t["bproj0"].to_broadcast([T, C])),
            (sinks[:, :], t["sinks"].to_broadcast([T, HEADS])), (rezero[:, :], t["rezero"].to_broadcast([T, 1])),
            (router0[:, :], t["wrT"][0:P]), (router1[:, :], t["wrT"][P:C]),
            (iota[:, :], t["iota"].to_broadcast([P, P])), (tri_in[:, :], t["tri"]),
            (tok1[:, :], t["tok1"]), (pad[:, :], t["pad"]),
            (qkv_w0[1][:, :], t["qkv1"][0:P]), (qkv_w1[1][0:C1, :], t["qkv1"][P:C]), (qkv_w1[1][C1:C1 + 1, :], t["bqkv1"]),
            (proj_w[1][:, :, :], t["proj1"]), (proj_b[1][:, :], t["bproj1"].to_broadcast([T, C])),
            (enc_w0[:, :], t["encw"][0:P]), (enc_w1[0:C1, :], t["encw"][P:C]), (enc_w1[C1:C1 + 1, :], t["encb"]),
            (sw_w[0:R1, :], t["sww"]), (sw_w[R1:R1 + 1, :], t["swb"]),
            (f1_w0[:, :], t["f1w1"][0:P]), (f1_w1[0:C1, :], t["f1w1"][P:C]), (f1_w1[C1:C1 + 1, :], t["f1b1"]),
            (f1_w2[:, :, :], t["f1w2"].rearrange("(c p) n -> p c n", p=P)), (f1_b2[:, :], t["f1b2"]),
        ]
        FILLS = 9
        ALL_IN = 16 * len(consts)

        def blk(m, k):
            return 2 * m + k, k % 2, m + k // 2 + 1

        def positive(x):
            return not isinstance(x, int) or x > 0

        DEPTH = 5

        def in_flight(s, lag):
            return not isinstance(s, int) or lag <= s < B + lag

        block = ctx.enter_context(nc.Block())

        @block.sync
        def _(sp):
            for dst, src in consts:
                sp.dma_start(dst, src).then_inc(const_in, 16)
            sp.wait_ge(ln_kept, B)
            sp.dma_start(ln_rows.rearrange("(b t) c -> t b c", b=B), xn_all[:, :, :]).then_inc(ln_stored, 16)

            def expert_of(j):
                e = sp.value_load(expert_i[0:1, bass.ds(j, 1)], min_val=0, max_val=E0 - 1)
                return bass.ds(e, 1)

            def load_first(m, k):
                j, p, u = blk(m, k)
                e = expert_of(j)
                if positive(j - 1):
                    sp.wait_ge(hid_ps, 2 * (j - 1))
                w1 = t["w1"][e, :, :].rearrange("o k f -> (o k) f")
                sp.dma_start(w1a[p][:, :], w1[0:P]).then_inc(w1_in[p], 16)
                sp.dma_start(w1b[p][0:C1, :], w1[P:C]).then_inc(w1_in[p], 16)
                sp.dma_start(w1b[p][C1:C1 + 1, :], t["b1"][e, :]).then_inc(w1_in[p], 16)

            def load_second(m, k):
                j, p, u = blk(m, k)
                e = expert_of(j)
                if positive(j - 1):
                    sp.wait_ge(blk_ps, j - 1)
                    sp.wait_ge(ys_done, j - 1)
                w2 = t["w2"][e, :, :].rearrange("o (c p) n -> (o p) c n", p=P)
                sp.dma_start(w2a[p][:, :, :], w2).then_inc(w2_in[p], 16)
                sp.dma_start(b2a[p][:, :], t["b2"][e, :].to_broadcast([P, C])).then_inc(w2_in[p], 16)
            sp.wait_ge(who_ready, 1)
            load_first(0, 0)
            load_second(0, 0)
            load_first(0, 1)
            load_second(0, 1)
            load_first(0, 2)
            load_first(0, 3)
            load_second(0, 2)
            with sp.Fori(1, NBLK // 2 - 1) as m:
                for k in range(2):
                    load_first(m, k + 2)
                    load_second(m, k + 1)
            load_second(NBLK // 2 - 1, 1)
            for p in range(2):
                sp.wait_ge(y_out[p], 16 * (NBLK // 2))
            for k in range(TOPK):
                sp.dma_start(yk[k][:, :, :], y_rows[k * TOK:(k + 1) * TOK].rearrange("(b t) c -> t b c", b=B)) \
                    .then_inc(picks_in, 16)
            sp.wait_ge(yout_done, B)
            sp.dma_start(out.rearrange("b n c -> n b c"), yout[:, :, :]).then_inc(out_sent, 16)
            sp.wait_ge(out_sent, 16)

        @block.gpsimd
        def _(pool):
            nc.gpsimd.memset(qk[:, :, :], 0.0).then_inc(filled, 1)
            nc.gpsimd.memset(kT[:, :, :, :], 0.0).then_inc(filled, 1)
            nc.gpsimd.memset(v_cur[:, :, :], 0.0).then_inc(filled, 1)
            nc.gpsimd.memset(xT1[:, :], 1.0).then_inc(filled, 1)
            nc.gpsimd.memset(XT1[:, :], 1.0).then_inc(filled, 1)
            nc.gpsimd.memset(encT[:, :], 1.0).then_inc(filled, 1)
            for p in range(2):
                nc.gpsimd.memset(xs1[p][:, :], 1.0).then_inc(filled, 1)
            nc.gpsimd.memset(ones16[:, :], 1.0).then_inc(filled, 1)
            pool.wait_ge(filled, FILLS)
            pool.wait_ge(const_in, ALL_IN)

            def attention(l):
                base = l * B

                def set_v(b):
                    pool.wait_ge(v_sb, base + b + 1)
                    if positive(base + b):
                        pool.wait_ge(o_ps, base + b)
                    nc.gpsimd.tensor_copy(v_cur[:, :, 0:HD], v_all[:, b, :, :]).then_inc(v_set, 1)

                def add_bias(b):
                    pool.wait_ge(xn_done, 2 * base + b + 1)
                    nc.gpsimd.tensor_tensor(h[:, b, :], h[:, b, :], proj_b[l][:, :], ALU.add).then_inc(b_added, 1)

                def rope_add(b):
                    pool.wait_ge(rope_mul, b + 1)
                    if positive(b):
                        pool.wait_ge(qkT_ps, b)
                    nc.gpsimd.tensor_tensor(qk[:, :, 0:HD], rope_a[:, :, :], rope_b[:, :, :],
                                            ALU.add).then_inc(qk_done, 1)

                def divide(b):
                    pool.wait_ge(rden_done, base + b + 1)
                    if positive(base + b):
                        pool.wait_ge(pT_ps, base + b)
                    nc.gpsimd.tensor_tensor(prob[:, :, :], sc[:, :, :],
                                            rden[:, :].unsqueeze(2).to_broadcast([T, HEADS, T]),
                                            ALU.mult).then_inc(p_done, 1)

                def step(s):
                    if in_flight(s, 3):
                        divide(s - 3)
                    if in_flight(s, 3):
                        set_v(s - 3)
                    if in_flight(s, 0):
                        add_bias(s)
                    if l == 0 and in_flight(s, 0):
                        rope_add(s)
                for s in range(DEPTH + 1):
                    step(s)
                with pool.Fori(DEPTH + 1, B - 1, 2) as s:
                    step(s)
                    step(s + 1)
                for s in range(B, B + DEPTH):
                    step(s)
            pool.wait_ge(rb_set, 1)
            attention(0)

            def add_ln(b):
                pool.wait_ge(xn_done, B + b + 1)
                nc.gpsimd.tensor_tensor(h[:, b, :], h[:, b, :], xn[:, :], ALU.add).then_inc(f_hadd, 1)
                nc.gpsimd.tensor_copy(xn_all[:, b, :], xn[:, :]).then_inc(ln_kept, 1)
            with pool.Fori(0, B) as b:
                add_ln(b)

            def take_waits():
                nc.gpsimd.tensor_tensor(tick[:, :], tok1[0:1, 0:1], tok1[0:1, 0:1], ALU.add)

            def fetch(m, k, n):
                j, p, u = blk(m, k)
                if positive(u - 1):
                    pool.wait_ge(x_in[p], 16 * (u - 1))
                    pool.wait_ge(xg_ps, j - 1)
                pool.wait_ge(rows_ready, 1)
                nc.gpsimd.tensor_copy(idx_in[p][:, :], row_in[:, bass.ds(j, 1)]).then_inc(idx_set, 1)
                pool.wait_ge(idx_set, n)
                pool.wait_ge(ln_stored, 16)
                take_waits()
                nc.gpsimd.indirect_dma_start(xg[p][:, :], None, ln_rows,
                                             bass.IndirectOffsetOnAxis(idx_in[p][:, 0:1], 0)).then_inc(x_in[p], 16)

            def store(m, k, n):
                j, p, u = blk(m, k)
                if positive(u - 1):
                    pool.wait_ge(y_out[p], 16 * (u - 1))
                pool.wait_ge(rows_ready, 1)
                nc.gpsimd.tensor_copy(idx_out[p][:, :], row_out[:, bass.ds(j, 1)]).then_inc(idx_set, 1)
                pool.wait_ge(idx_set, n)
                pool.wait_ge(ys_done, j + 1)
                take_waits()
                nc.gpsimd.indirect_dma_start(y_rows, bass.IndirectOffsetOnAxis(idx_out[p][:, 0:1], 0), ys[p][:, :],
                                             None).then_inc(y_out[p], 16)
            for k in range(4):
                fetch(0, k, k + 1)
            for k in range(2):
                store(0, k, 2 * k + 5)
                fetch(1, k + 2, 2 * k + 6)
            with pool.Fori(1, NBLK // 2 - 2) as m:
                for k in range(2):
                    store(m, k, 4 * m + 2 * k + 5)
                    fetch(m, k + 4, 4 * m + 2 * k + 6)
            for k in range(4):
                store(NBLK // 2 - 2, k, 2 * NBLK - 3 + k)
            attention(1)

            def chunk_marks(g):
                pool.wait_ge(oneT_sb, 4)
                pool.wait_ge(f_y_ps, 4 * g) if positive(g) else None
                nc.gpsimd.tensor_copy(oneTc16[:, :], oneT[:, bass.ds(g * G4, G4)]).then_inc(oneTc_sb, 1)
                nc.gpsimd.tensor_copy(oneTc[:, :], oneT[:, bass.ds(g * G4, G4)]).then_inc(oneTc_sb, 1)
            chunk_marks(0)
            with pool.Fori(1, B // 4) as g:
                chunk_marks(g)

        @block.scalar
        def _(act):
            def sqrt_var(k):
                act.wait_ge(ln_step, 10 * k + 5)
                nc.scalar.activation(lnv[:, 5, :], lnv[:, 4, :], ACT.Sqrt).then_inc(sqrt_done, 1)

            def attention(l):
                base = l * B

                def evac_qk(b):
                    act.wait_ge(qkT_ps, base + b + 1)
                    act.wait_ge(s_ps, 2 * (base + b))
                    nc.scalar.copy(qT[:, :, :], bank[3][:, 0:NG * T]).then_inc(q_sb, 1)
                    for j in range(4):
                        nc.scalar.copy(kT[SLOT * j:SLOT * j + SLOT, :, j, :],
                                       bank[3][SLOT * j:SLOT * j + SLOT, NG * T:2 * NG * T]).then_inc(k_sb, 1)

                def evac_x(b):
                    act.wait_ge(xT_ps, base + (B if l else 0) + b + 1)
                    act.wait_ge(v_ps, base + b)
                    if l == 0:
                        nc.scalar.activation(xT0[:, :], bank[0][:, 0:T], ACT.Identity, bias=ln_bias0[:, :],
                                             scale=ln_scale0[:, :]).then_inc(xT_sb, 1)
                        nc.scalar.activation(xT1[0:C1, :], bank[0][0:C1, T:2 * T], ACT.Identity, bias=ln_bias1[:, :],
                                             scale=ln_scale1[:, :]).then_inc(xT_sb, 1)
                    else:
                        nc.scalar.copy(xT0[:, :], bank[0][:, 0:T]).then_inc(xT_sb, 1)
                        nc.scalar.copy(xT1[0:C1, :], bank[0][0:C1, T:2 * T]).then_inc(xT_sb, 1)

                def evac_p(b):
                    act.wait_ge(pT_ps, base + b + 1)
                    if positive(base + b):
                        act.wait_ge(o_ps, base + b)
                    nc.scalar.copy(pT[:, 0:6, :], bank[6][0:T, 0:HALF]).then_inc(pT_sb, 1)
                    nc.scalar.copy(pT[:, 6:12, :], bank[7][0:T, 0:HALF]).then_inc(pT_sb, 1)

                def evac_o(b):
                    act.wait_ge(o_ps, base + b + 1)
                    if positive(base + b):
                        act.wait_ge(y_ps, base + b)
                    nc.scalar.copy(oT[:, :, :], bank[2][:, C:C + NG * T]).then_inc(oT_sb, 1)

                def exp(b):
                    act.wait_ge(s_sub, base + b + 1)
                    nc.scalar.activation(sc[:, :, :], sc[:, :, :], ACT.Exp, scale=0.25).then_inc(e_done, 1)
                    if l == 0:
                        nc.scalar.activation(sink_e[:, b, :], sink_e[:, b, :], ACT.Exp,
                                             scale=0.25).then_inc(sink_done, 1)

                def evac_v(b):
                    act.wait_ge(v_ps, base + b + 1)
                    nc.scalar.copy(v_all[:, b, :, 0:HD],
                                   bank[2][0:T, 0:C].rearrange("p (h d) -> p h d", d=HD)).then_inc(v_sb, 1)

                def step(s):
                    if in_flight(s, 4):
                        evac_p(s - 4)
                    if in_flight(s, 0):
                        evac_x(s)
                    if in_flight(s, 4):
                        evac_o(s - 4)
                    if in_flight(s, 1):
                        evac_qk(s - 1)
                    if in_flight(s, 0):
                        evac_v(s)
                    if in_flight(s, 2):
                        exp(s - 2)
                for s in range(DEPTH + 1):
                    step(s)
                with act.Fori(DEPTH + 1, B - 1, 2) as s:
                    step(s)
                    step(s + 1)
                for s in range(B, B + DEPTH):
                    step(s)

            act.wait_ge(filled, FILLS)
            act.wait_ge(const_in, ALL_IN)
            sqrt_var(0)
            attention(0)
            sqrt_var(1)
            def keep_x0(b):
                act.wait_ge(xT_ps, B + b + 1)
                act.wait_ge(f_log_ps, b)
                nc.scalar.copy(xT0[:, :], bank[0][:, 0:T]).then_inc(f_xT_sb, 1)
                nc.scalar.copy(xT1[0:C1, :], bank[0][0:C1, T:2 * T]).then_inc(f_xT_sb, 1)
            keep_x0(0)
            with act.Fori(1, B) as b:
                keep_x0(b)
            act.wait_ge(f_route, 2)
            nc.scalar.activation(r1[:, :, :], r1[:, :, :], ACT.Exp).then_inc(f_exp, 1)
            def keep_block(m, k):
                j, p, u = blk(m, k)
                act.wait_ge(xg_ps, j + 1)
                if positive(j - 1):
                    act.wait_ge(hid_ps, 2 * (j - 1))
                nc.scalar.copy(xs0[p][:, :], bank[0][:, 0:S]).then_inc(xs_sb, 1)
                nc.scalar.copy(xs1[p][0:C1, :], bank[0][0:C1, S:2 * S]).then_inc(xs_sb, 1)

            def gelu_block(m, k):
                j, p, u = blk(m, k)
                if positive(j - 1):
                    act.wait_ge(blk_ps, j - 1)
                act.wait_ge(hid_ps, 2 * j + 1)
                nc.scalar.activation(hb[p][:, 0:4, :].rearrange("p c s -> p (c s)"), bank[1 + 2 * p][:, 0:4 * S],
                                     ACT.Gelu).then_inc(hid_sb, 1)
                act.wait_ge(hid_ps, 2 * j + 2)
                nc.scalar.activation(hb[p][:, 4:6, :].rearrange("p c s -> p (c s)"), bank[2 + 2 * p][:, 0:2 * S],
                                     ACT.Gelu).then_inc(hid_sb, 1)
            keep_block(0, 0)
            keep_block(0, 1)
            gelu_block(0, 0)
            for k in range(1, 3):
                keep_block(0, k + 1)
                gelu_block(0, k)
            with act.Fori(1, NBLK // 2 - 1) as m:
                for k in range(1, 3):
                    keep_block(m, k + 1)
                    gelu_block(m, k)
            gelu_block(NBLK // 2 - 1, 1)
            sqrt_var(2)
            attention(1)
            sqrt_var(3)
            def keep_x1(b):
                act.wait_ge(xT_ps, 3 * B + b + 1)
                act.wait_ge(f_enc_ps, b)
                nc.scalar.copy(XT0[:, bass.ds(b * T, T)], bank[0][:, 0:T]).then_inc(f_xT_sb, 1)
                nc.scalar.copy(XT1[0:C1, bass.ds(b * T, T)], bank[0][0:C1, T:2 * T]).then_inc(f_xT_sb, 1)
                act.wait_ge(f_enc_ps, b + 1)
                act.wait_ge(f_log_ps, B + b)
                nc.scalar.copy(encT[0:R1, :], bank[1][0:R1, 0:T]).then_inc(f_enc_sb, 1)
            keep_x1(0)
            with act.Fori(1, B) as b:
                keep_x1(b)
            act.wait_ge(f_route, 9)
            nc.scalar.activation(r1[:, :, 0:E1], r1[:, :, 0:E1], ACT.Exp).then_inc(f_exp, 1)
            for g in range(4):
                act.wait_ge(oneT_ps, g + 1)
                nc.scalar.copy(oneT[:, g * G4:(g + 1) * G4], bank[g % 2][0:E1, 0:G4]).then_inc(oneT_sb, 1)
            def gelus(g):
                act.wait_ge(f_y_ps, 4 * g) if positive(g) else None
                for c in range(RC):
                    act.wait_ge(f_hid_ps, g * RC + c + 1)
                    nc.scalar.activation(hid[:, c, :], bank[c][:, 0:G4], ACT.Gelu).then_inc(f_hid_sb, 1)
            gelus(0)
            with act.Fori(1, B // 4) as g:
                gelus(g)

        @block.vector
        def _(dve):
            def row_stats(b):
                nc.vector.bn_stats(stats[:, b, :], h[:, b, :]).then_inc(stats_done, 1)

            def ln(k, rows):
                dve.wait_ge(stats_done, rows)
                n = 10 * k
                add, sub, mul = ALU.add, ALU.subtract, ALU.mult
                nc.vector.tensor_tensor(lnv[:, 0, :], stats[:, :, 1], stats[:, :, 4], add).then_inc(ln_step, 1)
                nc.vector.tensor_tensor(lnv[:, 1, :], stats[:, :, 1], stats[:, :, 4], sub).then_inc(ln_step, 1)
                nc.vector.tensor_tensor(lnv[:, 3, :], stats[:, :, 2], stats[:, :, 5], add).then_inc(ln_step, 1)
                dve.wait_ge(ln_step, n + 3)
                nc.vector.scalar_tensor_tensor(lnv[:, 2, :], lnv[:, 1, :], 0.25, lnv[:, 1, :], mul, mul).then_inc(ln_step, 1)
                nc.vector.tensor_scalar(mean[:, :], lnv[:, 0, :], 0.5, None, mul).then_inc(ln_done, 1)
                nc.vector.tensor_scalar(lnv[:, 6, :], lnv[:, 3, :], 1.0 / C, EPS, mul, add).then_inc(ln_done, 1)
                dve.wait_ge(ln_done, 2 * k + 2)
                dve.wait_ge(ln_step, n + 4)
                nc.vector.tensor_tensor(lnv[:, 4, :], lnv[:, 6, :], lnv[:, 2, :], add).then_inc(ln_step, 1)
                dve.wait_ge(sqrt_done, k + 1)
                nc.vector.reciprocal(lnv[:, 0, :], lnv[:, 5, :]).then_inc(ln_step, 1)
                dve.wait_ge(ln_step, n + 6)
                nc.vector.tensor_tensor(lnv[:, 1, :], lnv[:, 4, :], lnv[:, 0, :], mul).then_inc(ln_step, 1)
                dve.wait_ge(ln_step, n + 7)
                nc.vector.tensor_tensor(lnv[:, 2, :], lnv[:, 1, :], lnv[:, 5, :], add).then_inc(ln_step, 1)
                dve.wait_ge(ln_step, n + 8)
                nc.vector.tensor_scalar(lnv[:, 3, :], lnv[:, 2, :], 0.5, None, mul).then_inc(ln_step, 1)
                dve.wait_ge(ln_step, n + 9)
                nc.vector.reciprocal(rstd[:, :], lnv[:, 3, :]).then_inc(ln_step, 1)
                dve.wait_ge(ln_step, n + 10)

            def normalise(b, n, also=None):
                if n is not None:
                    dve.wait_ge(xT_ps, n)
                nc.vector.tensor_scalar(xn[:, :], h[:, b, :], mean[:, bass.ds(b, 1)], rstd[:, bass.ds(b, 1)],
                                        ALU.subtract, ALU.mult).then_inc(xn_done, 1)

            def attention(l):
                base = l * B
                xbase = 2 * l * B

                def row_max(b):
                    for j in range(2):
                        dve.wait_ge(s_ps, 2 * (base + b) + 1 + j)
                        nc.vector.tensor_reduce(top[:, b, 6 * j:6 * j + 6],
                                                bank[4 + j][0:T, 0:HALF].rearrange("p (h k) -> p h k", k=T),
                                                AX_X, ALU.max).then_inc(top_raw, 1)
                    dve.wait_ge(top_raw, 2 * (base + b + 1))
                    if l == 0:
                        nc.vector.tensor_tensor(top[:, b, :], top[:, b, :], sinks4[:, :], ALU.max).then_inc(top_done, 1)
                        dve.wait_ge(top_done, b + 1)
                        nc.vector.tensor_tensor(sink_e[:, b, :], sinks4[:, :], top[:, b, :], ALU.subtract)
                    if positive(base + b):
                        dve.wait_ge(p_done, base + b)
                    for j in range(2):
                        ins = nc.vector.tensor_tensor(
                            sc[:, 6 * j:6 * j + 6, :], bank[4 + j][0:T, 0:HALF].rearrange("p (h k) -> p h k", k=T),
                            top[:, b, 6 * j:6 * j + 6].unsqueeze(2).to_broadcast([T, 6, T]), ALU.subtract)
                    ins.then_inc(s_sub, 1)

                def rope(b):
                    dve.wait_ge(qk_ps, base + b + 1)
                    x = bank[1][0:T, 0:2 * C].rearrange("p (h d) -> p h d", d=HD)
                    if l == 1:
                        dve.wait_ge(qkT_ps, base + b)
                        nc.vector.tensor_copy(qk[:, :, 0:HD], x).then_inc(rope_mul, 1)
                        return
                    if not isinstance(b, int) or b:
                        dve.wait_ge(qk_done, b)
                    nc.vector.tensor_tensor(rope_a[:, :, :], x, rope_c[:, :].unsqueeze(1).to_broadcast([T, 2 * HEADS, HD]),
                                            ALU.mult)
                    xs = bank[1][0:T, 0:2 * C].rearrange("p (h i two) -> p h i two", i=HD // 2, two=2)
                    nc.vector.tensor_tensor(
                        rope_b[:, :, :].rearrange("p h (i two) -> p h i two", two=2), xs[:, :, :, ::-1],
                        rope_s[:, :].rearrange("p (i two) -> p i two", two=2).unsqueeze(1)
                        .to_broadcast([T, 2 * HEADS, HD // 2, 2]), ALU.mult).then_inc(rope_mul, 1)

                def residual(b):
                    dve.wait_ge(y_ps, base + b + 1)
                    dve.wait_ge(b_added, base + b + 1)
                    y = bank[0][0:T, 2 * T:2 * T + C]
                    if l == 0:
                        nc.vector.scalar_tensor_tensor(h[:, b, :], y, rezero[:, 0:1], h[:, b, :], ALU.mult,
                                                       ALU.add).then_inc(h_done, 1)
                    else:
                        nc.vector.tensor_tensor(h[:, b, :], y, h[:, b, :], ALU.add).then_inc(h_done, 1)
                    dve.wait_ge(h_done, base + b + 1)
                    row_stats(b)

                def row_sum(b):
                    dve.wait_ge(e_done, base + b + 1)
                    nc.vector.tensor_reduce(den[:, :], sc[:, :, :], AX_X, ALU.add).then_inc(den_done, 1)
                    if l == 0:
                        dve.wait_ge(den_done, 2 * b + 1)
                        dve.wait_ge(sink_done, b + 1)
                        nc.vector.tensor_tensor(den[:, :], den[:, :], sink_e[:, b, :], ALU.add).then_inc(den_done, 1)
                        dve.wait_ge(den_done, 2 * b + 2)
                    else:
                        dve.wait_ge(den_done, 2 * B + b + 1)
                    nc.vector.reciprocal(rden[:, :], den[:, :]).then_inc(rden_done, 1)

                def step(s):
                    if in_flight(s, 3):
                        row_sum(s - 3)
                    if in_flight(s, 5):
                        residual(s - 5)
                    if in_flight(s, 2):
                        row_max(s - 2)
                    if in_flight(s, 0):
                        rope(s)
                    if in_flight(s + 1, 0):
                        normalise(s + 1, xbase + s + 1)
                normalise(0, xbase)
                for s in range(DEPTH):
                    step(s)
                with dve.Fori(DEPTH, B - 2, 2) as s:
                    step(s)
                    step(s + 1)
                for s in range(B - 1, B + DEPTH):
                    step(s)

            dve.wait_ge(const_in, ALL_IN)
            dve.wait_ge(filled, FILLS)
            nc.vector.tensor_copy(ident16[:, :], ident[0:T, 0:T])
            nc.vector.tensor_copy(mask16[:, :].rearrange("p (h k) -> p h k", k=T),
                                  mask_in[:, :].unsqueeze(1).to_broadcast([T, 6, T]))
            nc.vector.tensor_copy(tri16[:, :], tri_in[:, :])
            nc.vector.tensor_copy(sel16[:, :, :].rearrange("p c n -> p (c n)"), sel_in[:, :])
            nc.vector.tensor_scalar(proj_b[0][:, :], proj_b[0][:, :], rezero[:, 0:1], None, ALU.mult).then_inc(rb_set, 1)
            nc.vector.tensor_scalar(sinks4[:, :], sinks[:, :], 4.0, None, ALU.mult)
            for i in range(B // 2):
                dve.wait_ge(patch_ps, i + 1)
                nc.vector.tensor_copy(h[0:NPATCH, 2 * i, :], bank[i % 2][0:NPATCH, 0:C])
                nc.vector.tensor_copy(h[0:NPATCH, 2 * i + 1, :], bank[i % 2][64:64 + NPATCH, 0:C]).then_inc(patch_sb, 1)
                dve.wait_ge(patch_sb, i + 1)
                row_stats(2 * i)
                row_stats(2 * i + 1)
            ln(0, B)
            attention(0)
            ln(1, 2 * B)

            normalise(0, B)
            with dve.Fori(1, B) as b:
                dve.wait_ge(ln_kept, b)
                dve.wait_ge(f_hadd, b)
                normalise(b, B + b)
            dve.wait_ge(f_log_ps, B)
            bc = lambda x, n: x.unsqueeze(2).to_broadcast([T, B, n])
            logit0 = bank[2][0:T, 0:B * E0].rearrange("p (b e) -> p b e", e=E0)
            nexp = iota[0:T, 0:E0].unsqueeze(1).to_broadcast([T, B, E0])
            nc.vector.tensor_reduce(rs[0][:, :], logit0, AX_X, ALU.max).then_inc(f_route, 1)
            dve.wait_ge(f_route, 1)
            nc.vector.tensor_tensor(r1[:, :, :], logit0, bc(rs[0][:, :], E0), ALU.subtract).then_inc(f_route, 1)
            dve.wait_ge(f_exp, 1)
            nc.vector.tensor_reduce(rs[1][:, :], r1[:, :, :], AX_X, ALU.add).then_inc(f_route, 1)
            dve.wait_ge(f_route, 3)
            nc.vector.reciprocal(rs[2][:, :], rs[1][:, :]).then_inc(f_route, 1)
            dve.wait_ge(f_route, 4)
            nc.vector.tensor_tensor(r1[:, :, :], r1[:, :, :], bc(rs[2][:, :], E0), ALU.mult).then_inc(f_route, 1)
            cnt = 5
            for k in range(TOPK):
                best = gates[:, k, :]
                dve.wait_ge(f_route, cnt + k)
                nc.vector.tensor_reduce(best, r1[:, :, :], AX_X, ALU.max).then_inc(pick_done, 1)
                dve.wait_ge(pick_done, 5 * k + 1)
                nc.vector.tensor_tensor(r2[:, :, :], r1[:, :, :], bc(best, E0), ALU.is_lt).then_inc(pick_done, 1)
                dve.wait_ge(pick_done, 5 * k + 2)
                nc.vector.scalar_tensor_tensor(r3[:, :, :], r2[:, :, :], float(E0), nexp, ALU.mult, ALU.add).then_inc(pick_done, 1)
                dve.wait_ge(pick_done, 5 * k + 3)
                nc.vector.tensor_reduce(rs[1][:, :], r3[:, :, :], AX_X, ALU.min).then_inc(pick_done, 1)
                dve.wait_ge(pick_done, 5 * k + 4)
                nc.vector.tensor_tensor(pick[k][:, :, :], nexp, bc(rs[1][:, :], E0), ALU.is_equal).then_inc(pick_done, 1)
                dve.wait_ge(pick_done, 5 * k + 5)
                if k == 0:
                    nc.vector.scalar_tensor_tensor(r1[:, :, :], pick[0][:, :, :], -2.0, r1[:, :, :], ALU.mult, ALU.add) \
                        .then_inc(f_route, 1)
            steps = [0]

            def link(ins):
                steps[0] += 1
                ins.then_inc(sort_step, 1)
                dve.wait_ge(sort_step, steps[0])
            tt, ts, stt = nc.vector.tensor_tensor, nc.vector.tensor_scalar, nc.vector.scalar_tensor_tensor
            tt(picks16[:, :, :], pick[0][:, :, :], pick[1][:, :, :], ALU.add).then_inc(pick_done, 1)
            dve.wait_ge(count_ps, 1)
            link(nc.vector.tensor_copy(total[:, :, :], bank[1][0:T, 0:B * E0].rearrange("p (b e) -> p b e", e=E0)))
            src, dst = total, run_a
            for d in (1, 2, 4, 8):
                nc.vector.tensor_copy(dst[:, 0:d, :], src[:, 0:d, :]).then_inc(sort_step, 1)
                steps[0] += 1
                link(tt(dst[:, d:B, :], src[:, d:B, :], src[:, 0:B - d, :], ALU.add))
                src, dst = dst, (run_b if dst is run_a else run_a)
            running = src
            link(ts(limits[:, :], iota[0:T, 0:MAXB], float(S), None, ALU.mult))
            link(tt(over[:, :, :], running[:, B - 1, :].unsqueeze(2).to_broadcast([T, E0, MAXB]),
                    limits[:, :].unsqueeze(1).to_broadcast([T, E0, MAXB]), ALU.is_gt))
            link(nc.vector.tensor_reduce(nblk[:, :], over[:, :, :], AX_X, ALU.add))
            src, dst = nblk, blk_a
            for d in (1, 2, 4, 8):
                nc.vector.tensor_copy(dst[:, 0:d], src[:, 0:d]).then_inc(sort_step, 1)
                steps[0] += 1
                link(tt(dst[:, d:E0], src[:, d:E0], src[:, 0:E0 - d], ALU.add))
                src, dst = dst, (blk_b if dst is blk_a else blk_a)
            blk_end = src
            link(tt(passed[:, :, :], blk_end[0:1, :].unsqueeze(1).to_broadcast([1, NBLK, E0]),
                    iota[0:1, 0:NBLK].unsqueeze(2).to_broadcast([1, NBLK, E0]), ALU.is_le))
            link(nc.vector.tensor_reduce(expert_f[:, :], passed[:, :, :], AX_X, ALU.add))
            ts(expert_i[:, :], expert_f[:, :], float(E0 - 1), None, ALU.min).then_inc(who_ready, 1)
            link(tt(first_slot[:, :], blk_end[:, :], nblk[:, :], ALU.subtract))
            link(ts(first_slot[:, :], first_slot[:, :], float(S), None, ALU.mult))
            link(tt(place[:, :, :], bank[0][0:T, 0:B * E0].rearrange("p (b e) -> p b e", e=E0), running[:, :, :], ALU.add))
            link(tt(place[:, :, :], place[:, :, :], total[:, :, :], ALU.subtract))
            link(tt(place[:, :, :], place[:, :, :], first_slot[:, :].unsqueeze(1).to_broadcast([T, B, E0]), ALU.add))
            for k in range(TOPK):
                link(tt(r2[:, :, :], pick[k][:, :, :], place[:, :, :], ALU.mult))
                link(nc.vector.tensor_reduce(slot[:, k, :], r2[:, :, :], AX_X, ALU.add))
            link(ts(blk_of[:, :, :], slot[:, :, :], 1.0 / S, -(S - 1) / (2.0 * S), ALU.mult, ALU.add))
            link(ts(blk_of[:, :, :], blk_of[:, :, :], ROUND, -ROUND, ALU.add, ALU.add))
            link(stt(in_blk[:, :, :], blk_of[:, :, :], -float(S), slot[:, :, :], ALU.mult, ALU.add))
            flat = lambda x, n: x[:, :, :].rearrange("p k b -> p (k b)").unsqueeze(2).to_broadcast([T, NPICK, n])
            link(tt(blk_hot[:, :, :], flat(blk_of, NBLK), iota[0:T, 0:NBLK].unsqueeze(1).to_broadcast([T, NPICK, NBLK]),
                    ALU.is_equal))
            link(ts(named[:, :, 0, :], blk_hot[:, :, :], tok1[:, 0:1], None, ALU.mult))
            link(tt(named[:, :, 1, :], blk_hot[:, :, :], iota[0:T, 0:NPICK].unsqueeze(2).to_broadcast([T, NPICK, NBLK]),
                    ALU.mult))
            tt(in_hot[:, :, :], flat(in_blk, S), iota[0:T, :].unsqueeze(1).to_broadcast([T, NPICK, S]),
               ALU.is_equal).then_inc(who_ready, 1)
            dve.wait_ge(who_ps, 1)
            link(nc.vector.tensor_copy(who[:, :, :], bank[2][:, 0:2 * NBLK].rearrange("p (x j) -> p x j", x=2)))
            link(stt(wt[0][:, :], who[:, 1, :], float(T), who[:, 0, :], ALU.mult, ALU.add))
            link(ts(wt[1][:, :], wt[0][:, :], float(TOK), -float(TOK), ALU.is_gt, ALU.mult))
            link(tt(wt[1][:, :], wt[1][:, :], wt[0][:, :], ALU.add))
            link(ts(wt[1][:, :], wt[1][:, :], -1.0, 0.0, ALU.add, ALU.max))
            link(nc.vector.tensor_copy(row_in[:, :], wt[1][:, :]))
            link(ts(wt[2][:, :], who[:, 0, :], 0.0, None, ALU.is_gt))
            link(stt(wt[3][:, :], wt[0][:, :], -1.0, pad[:, :], ALU.add, ALU.subtract))
            link(tt(wt[3][:, :], wt[3][:, :], wt[2][:, :], ALU.mult))
            link(tt(wt[3][:, :], wt[3][:, :], pad[:, :], ALU.add))
            nc.vector.tensor_copy(row_out[:, :], wt[3][:, :]).then_inc(rows_ready, 1)

            def finish_block(m, k):
                j, p, u = blk(m, k)
                if positive(u - 1):
                    dve.wait_ge(y_out[p], 16 * (u - 1))
                dve.wait_ge(w2_in[p], 32 * u)
                dve.wait_ge(blk_ps, j + 1)
                nc.vector.tensor_tensor(ys[p][:, :], bank[5 + p][:, 0:C], b2a[p][:, :], ALU.add).then_inc(ys_done, 1)
            finish_block(0, 0)
            finish_block(0, 1)
            with dve.Fori(1, NBLK // 2) as m:
                finish_block(m, 0)
                finish_block(m, 1)

            dve.wait_ge(picks_in, 16 * TOPK)
            dve.wait_ge(f_hadd, B)

            def add_picks(b):
                for k in range(TOPK):
                    if k:
                        dve.wait_ge(moe_done, 2 * b + 1)
                    nc.vector.scalar_tensor_tensor(h[:, b, :], yk[k][:, b, :], gates[:, k, bass.ds(b, 1)], h[:, b, :],
                                                   ALU.mult, ALU.add).then_inc(moe_done, 1)
                dve.wait_ge(moe_done, 2 * b + 2)
                row_stats(b)
            with dve.Fori(0, B) as b:
                add_picks(b)
            ln(2, 3 * B)
            attention(1)
            ln(3, 4 * B)

            normalise(0, 3 * B)
            with dve.Fori(1, B) as b:
                normalise(b, 3 * B + b)
            dve.wait_ge(f_log_ps, 2 * B)
            logit1 = bank[2][0:T, 0:B * E1].rearrange("p (b e) -> p b e", e=E1)
            q1, q2, q3 = (x[:, :, 0:E1] for x in (r1, r2, r3))
            nexp1 = iota[0:T, 0:E1].unsqueeze(1).to_broadcast([T, B, E1])
            nc.vector.tensor_reduce(rs[0][:, :], logit1, AX_X, ALU.max).then_inc(f_route, 1)
            dve.wait_ge(f_route, 7)
            nc.vector.tensor_tensor(q2, logit1, bc(rs[0][:, :], E1), ALU.is_lt).then_inc(f_route, 1)
            nc.vector.tensor_tensor(q1, logit1, bc(rs[0][:, :], E1), ALU.subtract).then_inc(f_route, 1)
            dve.wait_ge(f_route, 9)
            nc.vector.scalar_tensor_tensor(q3, q2, float(E0), nexp1, ALU.mult, ALU.add).then_inc(f_route, 1)
            dve.wait_ge(f_route, 10)
            nc.vector.tensor_reduce(rs[1][:, :], q3, AX_X, ALU.min).then_inc(f_route, 1)
            dve.wait_ge(f_route, 11)
            nc.vector.tensor_tensor(one_hot1[:, :, :], nexp1, bc(rs[1][:, :], E1), ALU.is_equal).then_inc(f_route, 1)
            dve.wait_ge(f_exp, 2)
            nc.vector.tensor_reduce(rs[2][:, :], q1, AX_X, ALU.add).then_inc(f_route, 1)
            dve.wait_ge(f_route, 13)
            nc.vector.reciprocal(rs[3][:, :], rs[2][:, :]).then_inc(f_route, 1)
            dve.wait_ge(f_route, 14)

            def weighted(g):
                for c in range(RC):
                    dve.wait_ge(f_hid_sb, g * RC + c + 1)
                    dve.wait_ge(mask_ps, g * RC + c + 1)
                    if c == 0 and positive(g):
                        dve.wait_ge(f_y_ps, 4 * g)
                    nc.vector.tensor_tensor(gm[:, c, :], hid[:, c, :], bank[4 + c % 2][:, 0:G4],
                                            ALU.mult).then_inc(gm_done, 1)
                for j in range(4):
                    dve.wait_ge(f_y_ps, 4 * g + j + 1)
                    b = 4 * g + j
                    nc.vector.scalar_tensor_tensor(yout[:, b, :], bank[6 + j % 2][0:T, 0:C],
                                                   rs[3][:, bass.ds(b, 1)], h[:, b, :], ALU.mult,
                                                   ALU.add).then_inc(yout_done, 1)
            weighted(0)
            with dve.Fori(1, B // 4) as g:
                weighted(g)

        @block.tensor
        def _(pe):
            mm = nc.tensor.matmul

            def product(dst, pairs, last):
                for i, (lhsT, rhs) in enumerate(pairs):
                    ins = mm(dst, lhsT, rhs, start=(i == 0), stop=(i == len(pairs) - 1))
                if last is not None:
                    ins.then_inc(last, 1)

            def turn_x(b, n, frees):
                pe.wait_ge(xn_done, n)
                for free, free_at in frees:
                    if not isinstance(free_at, int) or free_at > 0:
                        pe.wait_ge(free, free_at)
                nc.tensor.transpose(bank[0][:, 0:T], xn[:, 0:P], ident[0:T, 0:T])
                nc.tensor.transpose(bank[0][0:C1, T:2 * T], xn[:, P:C], ident[0:T, 0:T]).then_inc(xT_ps, 1)

            def attention(l):
                base = l * B

                def turn_qk(b):
                    if l == 0:
                        pe.wait_ge(qk_done, b + 1)
                    else:
                        pe.wait_ge(rope_mul, base + b + 1)
                    pe.wait_ge(q_sb, base + b)
                    pe.wait_ge(k_sb, 4 * (base + b))
                    for g in range(2 * NG):
                        ins = nc.tensor.transpose(bank[3][:, g * T:(g + 1) * T],
                                                  qk[:, 4 * g:4 * g + 4, :].rearrange("p h d -> p (h d)"),
                                                  ident[0:T, 0:T])
                    ins.then_inc(qkT_ps, 1)

                def turn_p(b):
                    pe.wait_ge(p_done, base + b + 1)
                    pe.wait_ge(pT_sb, 2 * (base + b))
                    for i in range(HEADS):
                        ins = nc.tensor.transpose(bank[6 + i // 6][0:T, (i % 6) * T:(i % 6 + 1) * T], prob[:, i, :],
                                                  ident[0:T, 0:T])
                    ins.then_inc(pT_ps, 1)

                def scores(b):
                    pe.wait_ge(q_sb, base + b + 1)
                    pe.wait_ge(k_sb, 4 * (base + b + 1))
                    pe.wait_ge(s_sub, base + b)
                    parts = [(0, 0, 4, 0), (1, 0, 2, 0), (1, 2, 4, 1), (2, 0, 4, 1)]
                    for g, a, z, half in parts:
                        col = (4 * g + a) * T - half * HALF
                        first = (g, a) in ((0, 0), (1, 2))
                        ins = mm(bank[4 + half][0:T, col:col + (z - a) * T], qT[:, g, :],
                                 kT[:, g, a:z, :].rearrange("p h t -> p (h t)"), start=True, stop=(l == 1),
                                 skip_group_check=True)
                        if l == 0:
                            ins = mm(bank[4 + half][0:T, col:col + (z - a) * T], ident16[:, :],
                                     mask16[:, 0:(z - a) * T], start=False, stop=True, skip_group_check=True)
                        if z * T + 4 * g * T - half * HALF == HALF:
                            ins.then_inc(s_ps, 1)

                def qk_product(b):
                    pe.wait_ge(xT_sb, 2 * (base + b + 1))
                    pe.wait_ge(rope_mul, base + b)
                    product(bank[1][0:T, 0:2 * C], [(xT0[:, :], qkv_w0[l][:, 0:2 * C]), (xT1[:, :], qkv_w1[l][:, 0:2 * C])],
                            qk_ps)

                def v_product(b):
                    pe.wait_ge(v_sb, base + b)
                    if positive(base + b - 3):
                        pe.wait_ge(oT_sb, base + b - 3)
                    product(bank[2][0:T, 0:C], [(xT0[:, :], qkv_w0[l][:, 2 * C:]), (xT1[:, :], qkv_w1[l][:, 2 * C:])], v_ps)

                def project(b):
                    pe.wait_ge(oT_sb, base + b + 1)
                    pe.wait_ge(xT_sb, 2 * (base + (min(b + 5, B) if isinstance(b, int) else b + 5)))
                    if positive(base + b):
                        pe.wait_ge(h_done, base + b)
                    product(bank[0][0:T, 2 * T:2 * T + C], [(oT[:, g, :], proj_w[l][:, g, :]) for g in range(NG)], y_ps)

                def values(b):
                    pe.wait_ge(pT_sb, 2 * (base + b + 1))
                    pe.wait_ge(v_set, base + b + 1)
                    pe.wait_ge(v_sb, base + (min(b + 4, B) if isinstance(b, int) else b + 4))
                    if positive(base + b):
                        pe.wait_ge(oT_sb, base + b)
                    for i in range(HEADS):
                        g, j = i // 4, i % 4
                        ins = mm(bank[2][SLOT * j:SLOT * j + SLOT, C + g * T:C + (g + 1) * T], v_cur[:, i, :], pT[:, i, :],
                                 start=True, stop=True)
                    ins.then_inc(o_ps, 1)

                def step(s):
                    if in_flight(s, 2):
                        scores(s - 2)
                    if in_flight(s, 0):
                        turn_x(s, 2 * l * B + s + 1, [(xT_sb, 2 * (base + s)), (h_done, base + s - 4)])
                    if in_flight(s, 4):
                        values(s - 4)
                    if in_flight(s, 1):
                        turn_qk(s - 1)
                    if in_flight(s, 0):
                        qk_product(s)
                    if in_flight(s, 0):
                        v_product(s)
                    if in_flight(s, 4):
                        project(s - 4)
                    if in_flight(s, 3):
                        turn_p(s - 3)
                for s in range(DEPTH + 1):
                    step(s)
                with pe.Fori(DEPTH + 1, B - 1, 2) as s:
                    step(s)
                    step(s + 1)
                for s in range(B, B + DEPTH):
                    step(s)

            pe.wait_ge(const_in, ALL_IN)
            pe.wait_ge(filled, FILLS)
            for i in range(B // 2):
                if i >= 2:
                    pe.wait_ge(patch_sb, i - 1)
                product(bank[i % 2][0:100, 0:C], [(patches[:, c, i, 0:100], w_tok[:, c, :]) for c in range(PF)], patch_ps)
            pe.wait_ge(patch_sb, B // 2)
            attention(0)

            def route0(b):
                pe.wait_ge(f_xT_sb, 2 * (b + 1))
                product(bank[2][0:T, bass.ds(b * E0, E0)], [(xT0[:, :], router0[:, :]), (xT1[0:C1, :], router1[:, :])], f_log_ps)
            turn_x(0, B + 1, [(h_done, B)])
            with pe.Fori(1, B) as b:
                route0(b - 1)
                turn_x(b, B + b + 1, [(f_xT_sb, 2 * b)])
            route0(B - 1)
            pe.wait_ge(pick_done, 11)
            pe.wait_ge(f_xT_sb, 2 * B)
            picks = picks16[:, :, :].rearrange("p b e -> p (b e)")
            product(bank[0][0:T, 0:B * E0], [(tri16[:, :], picks)], None)
            product(bank[1][0:T, 0:B * E0], [(ones16[:, :], picks)], count_ps)
            pe.wait_ge(who_ready, 2)
            names = named[:, :, :, :].rearrange("p i x j -> p i (x j)")
            mm(bank[2][:, 0:2 * NBLK], in_hot[:, 0, :], names[:, 0, :], start=True, stop=False, skip_group_check=True)
            with pe.Fori(1, NPICK) as i:
                mm(bank[2][:, 0:2 * NBLK], in_hot[:, bass.ds(i, 1), :].rearrange("p o s -> p (o s)"),
                   names[:, bass.ds(i, 1), :].rearrange("p o s -> p (o s)"), start=False, stop=True,
                   skip_group_check=True).then_inc(who_part, 1)
            pe.wait_ge(who_part, NPICK - 1)
            pe.nop().then_inc(who_ps, 1)

            def turn_block(m, k):
                j, p, u = blk(m, k)
                pe.wait_ge(x_in[p], 16 * u)
                if positive(j):
                    pe.wait_ge(xs_sb, 2 * j)
                nc.tensor.transpose(bank[0][:, 0:S], xg[p][:, 0:P], ident[:, :])
                nc.tensor.transpose(bank[0][0:C1, S:2 * S], xg[p][:, P:C], ident[:, :]).then_inc(xg_ps, 1)

            def hidden_block(m, k):
                j, p, u = blk(m, k)
                pe.wait_ge(w1_in[p], 48 * u)
                pe.wait_ge(xs_sb, 2 * j + 2)
                if positive(j - 1):
                    pe.wait_ge(hid_sb, 2 * (j - 1))
                for c in range(FC):
                    cols = slice(c * P, (c + 1) * P)
                    product(bank[1 + 2 * p + c // 4][:, (c % 4) * S:(c % 4 + 1) * S],
                            [(w1a[p][:, cols], xs0[p][:, :]), (w1b[p][:, cols], xs1[p][:, :])],
                            hid_ps if c in (3, FC - 1) else None)

            def down_block(m, k):
                j, p, u = blk(m, k)
                pe.wait_ge(w2_in[p], 32 * u)
                pe.wait_ge(hid_sb, 2 * j + 2)
                if positive(j - 1):
                    pe.wait_ge(ys_done, j - 1)
                product(bank[5 + p][:, 0:C], [(hb[p][:, c, :], w2a[p][:, c, :]) for c in range(FC)], blk_ps)
            turn_block(0, 0)
            turn_block(0, 1)
            hidden_block(0, 0)
            for k in range(1, 3):
                turn_block(0, k + 1)
                hidden_block(0, k)
                down_block(0, k - 1)
            with pe.Fori(1, NBLK // 2 - 1) as m:
                for k in range(1, 3):
                    turn_block(m, k + 1)
                    hidden_block(m, k)
                    down_block(m, k - 1)
            hidden_block(NBLK // 2 - 1, 1)
            down_block(NBLK // 2 - 1, 0)
            down_block(NBLK // 2 - 1, 1)
            attention(1)

            def encode(b):
                pe.wait_ge(f_xT_sb, 2 * B + 2 * (b + 1))
                pe.wait_ge(f_enc_sb, b) if not isinstance(b, int) or b else None
                cols = bass.ds(b * T, T)
                product(bank[1][0:R1, 0:T], [(enc_w0[:, :], XT0[:, cols]), (enc_w1[:, :], XT1[:, cols])], f_enc_ps)

            def route1(b):
                pe.wait_ge(f_enc_sb, b + 1)
                product(bank[2][0:T, bass.ds(b * E1, E1)], [(encT[:, :], sw_w[:, :])], f_log_ps)
            turn_x(0, 3 * B + 1, [(h_done, 2 * B)])
            encode(0)
            turn_x(1, 3 * B + 2, [(f_xT_sb, 2 * B + 2)])
            route1(0)
            with pe.Fori(2, B) as b:
                encode(b - 1)
                turn_x(b, 3 * B + b + 1, [(f_xT_sb, 2 * B + 2 * b)])
                route1(b - 1)
            encode(B - 1)
            route1(B - 1)
            for g in range(4):
                pe.wait_ge(f_route, 12)
                if g >= 2:
                    pe.wait_ge(oneT_sb, g - 1)
                for j in range(4):
                    ins = nc.tensor.transpose(bank[g % 2][0:E1, j * T:(j + 1) * T], one_hot1[:, 4 * g + j, :], ident[0:T, 0:T])
                ins.then_inc(oneT_ps, 1)
            pe.wait_ge(oneT_sb, 4)

            def dense(g):
                cols = bass.ds(g * G4, G4)
                for c in range(RC):
                    pe.wait_ge(f_hid_sb, g * RC)
                    product(bank[c][:, 0:G4], [(f1_w0[:, c * P:(c + 1) * P], XT0[:, cols]),
                                               (f1_w1[:, c * P:(c + 1) * P], XT1[:, cols])], f_hid_ps)
                pe.wait_ge(oneTc_sb, 2 * (g + 1))
                for c in range(RC):
                    pe.wait_ge(gm_done, g * RC + max(c - 1, 0))
                    product(bank[4 + c % 2][:, 0:G4], [(sel16[:, c, :], oneTc16[:, :])], mask_ps)
                pe.wait_ge(gm_done, (g + 1) * RC)
                for j in range(4):
                    pe.wait_ge(yout_done, 4 * g + max(j - 1, 0))
                    tok = slice(j * T, (j + 1) * T)
                    product(bank[6 + j % 2][0:T, 0:C], [(gm[:, c, tok], f1_w2[:, c, :]) for c in range(RC)]
                            + [(oneTc[:, tok], f1_b2[:, :])], f_y_ps)
            dense(0)
            with pe.Fori(1, B // 4) as g:
                dense(g)


def _layout(inputs):
    import numpy as np
    a = {k: np.asarray(v) for k, v in inputs.items()}
    f = np.ascontiguousarray
    hp = 6
    x = a["x"].reshape(B, 3, hp, 16, hp, 16).transpose(1, 3, 5, 0, 2, 4).reshape(PF, P, B // 2, 2, NPATCH)
    patch = np.zeros((PF, P, B // 2, 2, 64), x.dtype)
    patch[..., :NPATCH] = x

    def slots(w):
        r = np.zeros((NG, 4, SLOT, C), w.dtype)
        r[:, :, :HD] = w.reshape(NG, 4, HD, C)
        return f(r.reshape(NG, P, C).transpose(1, 0, 2))
    d = {
        "patchT": f(patch.transpose(1, 0, 2, 3, 4).reshape(P, PF, B // 2, P)),
        "wtokT": f(a["L0_tok_W"].T.reshape(PF, P, C).transpose(1, 0, 2)),
        "txt": f(a["txt"]),
        "qkv0": f(a["L0_attn_W_attn"]), "bqkv0": f(a["L0_attn_b_attn"].reshape(1, -1)),
        "proj0": slots(a["L0_attn_W_proj"]), "bproj0": f(a["L0_attn_b_proj"].reshape(1, -1)),
        "nscale": f(a["L0_attn_norm_scale"].reshape(-1, 1)), "nbias": f(a["L0_attn_norm_bias"].reshape(-1, 1)),
        "sinks": f(a["L0_attn_sinks"].reshape(1, -1)), "rezero": f(a["L0_attn_rezero"].reshape(1, 1)),
        "wrT": f(a["L0_ffn_Wr"].T), "w1": f(a["L0_ffn_W1"]), "b1": f(a["L0_ffn_b1"]),
        "w2": f(a["L0_ffn_W2"]), "b2": f(a["L0_ffn_b2"]),
        "qkv1": f(a["L1_attn_qkv_weight"].T), "bqkv1": f(a["L1_attn_qkv_bias"].reshape(1, -1)),
        "proj1": slots(a["L1_attn_proj_weight"].T), "bproj1": f(a["L1_attn_proj_bias"].reshape(1, -1)),
        "encw": f(a["L1_ffn_enc_w"]), "encb": f(a["L1_ffn_enc_b"].reshape(1, -1)),
        "sww": f(a["L1_ffn_sw_w"]), "swb": f(a["L1_ffn_sw_b"].reshape(1, -1)),
        "f1w1": f(a["L1_ffn_w1"].transpose(1, 0, 2).reshape(C, E1 * R1)), "f1b1": f(a["L1_ffn_b1"].reshape(1, -1)),
        "f1w2": f(a["L1_ffn_w2"].reshape(E1 * R1, C)), "f1b2": f(a["L1_ffn_b2"]),
    }
    ang = np.outer(np.arange(T, dtype=np.float32),
                   (1.0 / np.float32(10000.0) ** (np.arange(0, HD, 2, dtype=np.float32) / HD)).astype(np.float32))
    cos, sin = np.cos(ang).astype(np.float32), np.sin(ang).astype(np.float32)
    d["rope_c"] = f(np.repeat(cos, 2, axis=1))
    d["rope_s"] = f(np.stack([-sin, sin], axis=-1).reshape(T, HD))
    d["ident"] = np.eye(P, dtype=np.float32)
    d["mask"] = np.triu(np.full((T, T), MASKED, np.float32), 1)
    d["iota"] = np.arange(P, dtype=np.float32).reshape(1, -1)
    d["tri"] = np.triu(np.ones((T, T), np.float32), 1)
    d["tok1"] = np.arange(1, T + 1, dtype=np.float32).reshape(-1, 1)
    d["pad"] = f(TOPK * TOK + np.arange(NBLK * S, dtype=np.float32).reshape(NBLK, S).T)
    sel = np.zeros((E1, RC * P), np.float32)
    for e in range(E1):
        sel[e, e * R1:(e + 1) * R1] = 1.0
    d["sel"] = sel
    return d


def kernel(**inputs):
    import concourse.bacc as _bacc
    from concourse import mybir as _mybir
    from concourse.bass_utils import run_bass_kernel_spmd as _run

    nc = _bacc.Bacc("TRN2", target_bir_lowering=False, num_devices=1)
    data = _layout(inputs)
    arrays, aps = {}, {}
    for name, a in data.items():
        arrays[f"in_{name}_dram"] = a
        aps[name] = nc.dram_tensor(f"in_{name}_dram", a.shape, _mybir.dt.from_np(a.dtype), kind="ExternalInput").ap()
    out = nc.dram_tensor("out_0_dram", (B, T, C), F32, kind="ExternalOutput").ap()
    fusion_kernel(nc, aps, out)
    r = _run(nc, [arrays], core_ids=[0])
    return r.results[0]["out_0_dram"]
```

```python
from contextlib import ExitStack

import concourse.bass as bass
from concourse import mybir

ALU = mybir.AluOpType
ACT = mybir.ActivationFunctionType
F32 = mybir.dt.float32
BF16 = mybir.dt.bfloat16
AX_X = mybir.AxisListType.X

P = 128
B = 16
NPATCH = 36
NTXT = 32
T = NPATCH + NTXT
C = 192
C1 = C - P
HEADS = 12
HD = C // HEADS
SLOT = 32
NG = HEADS // 4
HALF = 6 * T
PF = 6
PAIR = 64 + NPATCH
E0, F0 = 16, 768
E1, R1 = 8, 64
FC = F0 // P
TOK = B * T
TOPK = 2
S = P
NBLK = (TOPK * TOK + E0 * (S - 1)) // S
NPICK = TOPK * B
MAXB = -(-TOK // S)
ROUND = 12582912.0
U32 = mybir.dt.uint32
I32 = mybir.dt.int32
RC = E1 * R1 // P
G4 = 4 * T
EPS = 1e-5
MASKED = -1.0e30


def fusion_kernel(nc, t, out):
    with ExitStack() as ctx:
        def sb(name, shape, dt=F32):
            return ctx.enter_context(nc.sbuf_tensor(name, shape, dt))

        def sem(name):
            return ctx.enter_context(nc.semaphore(name))

        bank = [ctx.enter_context(nc.psum_tensor(f"bank{i}", [P, 512], F32)) for i in range(4)]
        quad = ctx.enter_context(nc.psum_tensor("quad", [P, 4, 512], F32))
        bank += [quad[:, j, :] for j in range(4)]

        ident = sb("ident", [P, P])
        ident16 = sb("ident16", [T, T], BF16)
        mask16 = sb("mask16", [T, HALF], BF16)
        mask_in = sb("mask_in", [T, T])
        sel = sb("sel", [E1, RC * P])
        rope_in = sb("rope_in", [T, 2, HD])
        rope_c, rope_s = rope_in[:, 0, :], rope_in[:, 1, :]
        patches = sb("patches", [P, B // 2, PF, PAIR])
        w_tok = sb("w_tok", [P, PF, C])
        qkv_w0 = [sb(f"qkv_w0_{l}", [P, 3 * C]) for l in range(2)]
        qkv_w1 = [sb(f"qkv_w1_{l}", [C1 + 1, 3 * C]) for l in range(2)]
        proj_w = [sb(f"proj_w{l}", [P, 2, C]) for l in range(2)]
        proj_b = [sb(f"proj_b{l}", [T, C]) for l in range(2)]
        ln0, ln1 = sb("ln0", [P, 2]), sb("ln1", [C1, 2])
        sinks = sb("sinks", [T, HEADS])
        sinks4 = sb("sinks4", [T, HEADS])
        rezero = sb("rezero", [T, 1])
        router0, router1 = sb("router0", [P, E0]), sb("router1", [C1, E0])
        enc_w0, enc_w1 = sb("enc_w0", [P, R1]), sb("enc_w1", [C1 + 1, R1])
        sw_w = sb("sw_w", [R1 + 1, E1])
        f1_w0, f1_w1 = sb("f1_w0", [P, E1 * R1]), sb("f1_w1", [C1 + 1, E1 * R1])
        f1_w2 = sb("f1_w2", [P, RC, C])
        f1_b2 = sb("f1_b2", [E1, C])

        h = sb("h", [T, B, C])
        stats = sb("stats", [T, B, 6])
        lnv = sb("lnv", [T, 8, B])
        mean, rstd = sb("mean", [T, B]), sb("rstd", [T, B])

        xn = sb("xn", [T, C])
        xT0, xT1 = sb("xT0", [P, T]), sb("xT1", [C1 + 1, T])
        v_all = sb("v_all", [T, B, HEADS, HD])
        v_cur = sb("v_cur", [T, HEADS // 2, 4, HD])
        rope_a, rope_b = sb("rope_a", [T, 2 * HEADS, HD]), sb("rope_b", [T, 2 * HEADS, HD])
        qk = sb("qk", [T, 2 * HEADS, SLOT])
        qT = sb("qT", [P, NG, T])
        kT = sb("kT", [P, NG, 4, T])
        top = sb("top", [T, B, HEADS])
        sink_e = sb("sink_e", [T, B, HEADS])
        sc = sb("sc", [T, HEADS, T])
        pT = sb("pT", [T, HEADS, T])
        prob = sb("prob", [T, HEADS, T])
        den, rden = sb("den", [T, HEADS]), sb("rden", [T, HEADS])
        oT = sb("oT", [P, 2, T])

        XT0, XT1 = sb("XT0", [P, B * T]), sb("XT1", [C1 + 1, B * T])
        encT = sb("encT", [R1 + 1, B * T])
        r1, r2, r3 = (sb(f"route{i}", [T, B, E0]) for i in range(3))
        one_hot1 = sb("one_hot1", [T, B, E1])
        oneT, oneT16 = sb("oneT", [E1, B * T]), sb("oneT16", [E1, B * T], BF16)
        sel16 = sb("sel16", [E1, RC * P], BF16)
        yT0, yT1 = sb("yT0", [P, G4]), sb("yT1", [C1, G4])
        rs = [sb(f"rs{i}", [T, B]) for i in range(4)]
        iota = sb("iota", [P, P])
        tri_in = sb("tri_in", [T, T])
        tri16, ones16 = sb("tri16", [T, T], BF16), sb("ones16", [T, T], BF16)
        zeros = sb("zeros", [P, 512], BF16)
        tick, warm = sb("tick", [1, 1]), sb("warm", [1, 1])
        tok1, pad = sb("tok1", [T, 1]), sb("pad", [P, NBLK])
        pick = [sb(f"pick{k}", [T, B, E0]) for k in range(TOPK)]
        gates = sb("gates", [T, TOPK, B])
        picks16 = sb("picks16", [T, B, E0], BF16)
        picked = sb("picked", [T, E0])
        limits = sb("limits", [T, MAXB])
        over = sb("over", [T, E0, MAXB])
        nblk, blk_a, blk_b, first_slot = (sb(x, [T, E0]) for x in ("nblk", "blk_a", "blk_b", "first_slot"))
        place = sb("place", [T, B, E0])
        slot, blk_of, in_blk = (sb(x, [T, TOPK, B]) for x in ("slot", "blk_of", "in_blk"))
        in_hot = sb("in_hot", [T, NPICK, S], BF16)
        blk_hot = sb("blk_hot", [T, NPICK, NBLK], BF16)
        named = sb("named", [T, NPICK, 2, NBLK], BF16)
        passed = sb("passed", [1, NBLK, E0])
        expert_f = sb("expert_f", [1, NBLK])
        expert_i = sb("expert_i", [1, NBLK], I32)
        who = sb("who", [P, 2, NBLK])
        wt = [sb(f"wt{i}", [P, NBLK]) for i in range(4)]
        row_in, row_out = sb("row_in", [P, NBLK], U32), sb("row_out", [P, NBLK], U32)
        idx_in = [sb(f"idx_in{i}", [P, 1], U32) for i in range(2)]
        idx_out = [sb(f"idx_out{i}", [P, 1], U32) for i in range(2)]
        xg = [sb(f"xg{i}", [P, C]) for i in range(2)]
        xs0 = [sb(f"xs0_{i}", [P, S]) for i in range(2)]
        xs1 = [sb(f"xs1_{i}", [C1 + 1, S]) for i in range(2)]
        w1a = [sb(f"w1a{i}", [P, F0]) for i in range(2)]
        w1b = [sb(f"w1b{i}", [C1 + 1, F0]) for i in range(2)]
        w2a = [sb(f"w2a{i}", [P, FC, C]) for i in range(2)]
        b2a = [sb(f"b2a{i}", [P, C]) for i in range(2)]
        hb = [sb(f"hb{i}", [P, FC, S]) for i in range(2)]
        ys = [sb(f"ys{i}", [P, C]) for i in range(2)]
        xn_all = sb("xn_all", [T, B, C])
        yout = v_all[:, :, :, :].rearrange("t b h d -> t b (h d)")
        yk = [yout, xn_all]
        pixels = patches[:, :, :, :].rearrange("p i c n -> p (i c n)")
        hid, gm = (pixels[:, i * RC * G4:(i + 1) * RC * G4].rearrange("p (c n) -> p c n", c=RC) for i in range(2))
        marks = pixels[:, 2 * RC * G4:4 * RC * G4].bitcast(BF16).rearrange("p (c n) -> p c n", c=RC)

        patch_in = [sem(f"patch_in{i}") for i in range(B // 4)]
        tok_in, txt_in, attn_in, late_in = (sem(x) for x in ("tok_in", "txt_in", "attn_in", "late_in"))
        ln_stored, out_sent = (sem(x) for x in ("ln_stored", "out_sent"))
        picks_in = [sem(f"picks_in{i}") for i in range(B // 4)]
        w1_in = [sem(f"w1_in{i}") for i in range(2)]
        w2_in = [sem(f"w2_in{i}") for i in range(2)]
        x_in = [sem(f"x_in{i}") for i in range(2)]
        y_out = [sem(f"y_out{i}") for i in range(2)]
        (pick_done, count_ps, sort_step, who_ready, rb_set, who_ps, rows_ready, idx_set, xg_ps, xs_sb, hid_ps, hid_sb,
         blk_ps, ys_done, moe_done) = (sem(x) for x in (
             "pick_done", "count_ps", "sort_step", "who_ready", "rb_set", "who_ps", "rows_ready", "idx_set", "xg_ps",
             "xs_sb", "hid_ps", "hid_sb", "blk_ps", "ys_done", "moe_done"))
        (filled, patch_ps, patch_sb, stats_done, sqrt_done, ln_step, ln_done, xn_done, xT_ps, xT_sb, v_ps, qk_ps, v_sb,
         rope_mul, qk_done, qkT_ps, q_sb, k_sb, s_ps, top_raw, top_done, s_sub, e_done, sink_done, pT_ps, pT_sb, o_ps,
         den_done, rden_done, p_done, v_set, b_added, oT_sb, y_ps, h_done) = (sem(x) for x in (
             "filled", "patch_ps", "patch_sb", "stats_done", "sqrt_done", "ln_step", "ln_done", "xn_done", "xT_ps",
             "xT_sb", "v_ps", "qk_ps", "v_sb", "rope_mul", "qk_done", "qkT_ps", "q_sb", "k_sb", "s_ps", "top_raw",
             "top_done", "s_sub", "e_done", "sink_done", "pT_ps", "pT_sb", "o_ps", "den_done", "rden_done", "p_done",
             "v_set", "b_added", "oT_sb", "y_ps", "h_done"))
        (f_xT_ps, f_xT_sb, f_hadd, f_enc_ps, f_enc_sb, f_log_ps, f_route, f_exp, oneT_ps, oneT_sb, mark_ps,
         f_hid_ps, f_hid_sb, gm_done, yT_ps, yT_sb, f_y_ps, yout_done) = (sem(x) for x in (
             "f_xT_ps", "f_xT_sb", "f_hadd", "f_enc_ps", "f_enc_sb", "f_log_ps", "f_route", "f_exp", "oneT_ps",
             "oneT_sb", "mark_ps", "f_hid_ps", "f_hid_sb", "gm_done", "yT_ps", "yT_sb", "f_y_ps",
             "yout_done"))

        one16_done, sel_done = sem("one16_done"), sem("sel_done")
        named_done, slot_known = sem("named_done"), sem("slot_known")
        mark_sb = [sem(f"mark_sb{i}") for i in range(2)]

        ln_rows = nc.dram_tensor("ln_rows", (TOK, C), F32, kind="Internal").ap()
        y_rows = nc.dram_tensor("y_rows", (TOPK * TOK + NBLK * S, C), F32, kind="Internal").ap()

        attn_consts = [
            (ident[:, :], t["ident"]),
            (qkv_w0[0][:, :], t["qkv0"][0:P]), (qkv_w1[0][:, :], t["qkv0"][P:C + 1]),
            (ln0[:, :], t["ln0"][0:P]), (ln1[:, :], t["ln0"][P:C]),
            (rope_in[:, :, :], t["rope"]), (mask_in[:, :], t["mask"]), (tri_in[:, :], t["tri"]),
            (proj_w[0][:, 0, :], t["proj0"][0:P]), (proj_w[0][0:C1, 1, :], t["proj0"][P:C]),
            (proj_b[0][:, :], t["bproj0"].to_broadcast([T, C])),
            (sinks[:, :], t["sinks"].to_broadcast([T, HEADS])), (rezero[:, :], t["rezero"].to_broadcast([T, 1])),
        ]
        late_consts = [
            (router0[:, :], t["wrT"][0:P]), (router1[:, :], t["wrT"][P:C]),
            (iota[:, :], t["iota"].to_broadcast([P, P])),
            (tok1[:, :], t["tok1"]), (pad[:, :], t["pad"]),
            (qkv_w0[1][:, :], t["qkv1"][0:P]), (qkv_w1[1][:, :], t["qkv1"][P:C + 1]),
            (proj_w[1][:, 0, :], t["proj1"][0:P]), (proj_w[1][0:C1, 1, :], t["proj1"][P:C]),
            (proj_b[1][:, :], t["bproj1"].to_broadcast([T, C])),
            (enc_w0[:, :], t["encw"][0:P]), (enc_w1[:, :], t["encw"][P:C + 1]), (sw_w[:, :], t["sww"]),
            (f1_w0[:, :], t["f1w1"][0:P]), (f1_w1[:, :], t["f1w1"][P:C + 1]),
            (f1_w2[:, :, :], t["f1w2"].rearrange("(c p) n -> p c n", p=P)), (f1_b2[:, :], t["f1b2"]),
            (sel[:, :], t["sel"]),
        ]
        ATTN_IN, LATE_IN = 16 * len(attn_consts), 16 * len(late_consts)
        FILLS = 10

        def blk(m, k):
            return 2 * m + k, k % 2, m + k // 2 + 1

        def positive(x):
            return not isinstance(x, int) or x > 0

        HB, LB = B // 2, B - 4
        TURN_BANKS = [(1, 3), (4, 5)]

        def static_in(s, table):
            return isinstance(s, int) and s in table

        def keep_mark(engine, copy, i):
            engine.wait_ge(mark_ps, i + 1)
            g, c = i // RC, i % RC
            copy(marks[:, c, g * G4:(g + 1) * G4], bank[4 + i % 4][:, 0:G4]).then_inc(mark_sb[i % 2], 1)

        DEPTH = 5

        def in_flight(s, lag):
            return not isinstance(s, int) or lag <= s < B + lag

        block = ctx.enter_context(nc.Block())

        @block.sync
        def _(sp):
            sp.dma_start(w_tok[:, :, :], t["wtokT"]).then_inc(tok_in, 16)
            sp.dma_start(h[NPATCH:T, :, :], t["txt"].rearrange("b n c -> n b c")).then_inc(txt_in, 16)
            for i in range(B // 4):
                sp.dma_start(patches[:, 2 * i:2 * i + 2, :, :], t["patchT"][i]).then_inc(patch_in[i], 16)
            for dst, src in attn_consts:
                sp.dma_start(dst, src).then_inc(attn_in, 16)
            for dst, src in late_consts:
                sp.dma_start(dst, src).then_inc(late_in, 16)
            sp.wait_ge(xn_done, 2 * B)
            sp.dma_start(ln_rows.rearrange("(b t) c -> t b c", b=B), xn_all[:, :, :]).then_inc(ln_stored, 16)

            def expert_of(j):
                e = sp.value_load(expert_i[0:1, bass.ds(j, 1)], min_val=0, max_val=E0 - 1)
                return bass.ds(e, 1)

            def load_first(m, k):
                j, p, u = blk(m, k)
                e = expert_of(j)
                if positive(j - 1):
                    sp.wait_ge(hid_ps, 2 * (j - 1))
                w1 = t["w1"][e, :, :].rearrange("o k f -> (o k) f")
                sp.dma_start(w1a[p][:, :], w1[0:P]).then_inc(w1_in[p], 16)
                sp.dma_start(w1b[p][:, :], w1[P:C + 1]).then_inc(w1_in[p], 16)

            def load_second(m, k):
                j, p, u = blk(m, k)
                e = expert_of(j)
                if positive(j - 1):
                    sp.wait_ge(blk_ps, j - 1)
                    sp.wait_ge(ys_done, j - 1)
                w2 = t["w2"][e, :, :].rearrange("o p n -> (o p) n")
                sp.dma_start(w2a[p][:, :, :].rearrange("p c n -> p (c n)"), w2).then_inc(w2_in[p], 16)
                sp.dma_start(b2a[p][:, :], t["b2"][e, :].to_broadcast([P, C])).then_inc(w2_in[p], 16)
            sp.wait_ge(who_ready, 1)
            load_first(0, 0)
            load_second(0, 0)
            load_first(0, 1)
            load_second(0, 1)
            load_first(0, 2)
            load_first(0, 3)
            load_second(0, 2)
            with sp.Fori(1, NBLK // 2 - 1) as m:
                for k in range(2):
                    load_first(m, k + 2)
                    load_second(m, k + 1)
            load_second(NBLK // 2 - 1, 1)
            for p in range(2):
                sp.wait_ge(y_out[p], 16 * (NBLK // 2))
            sp.wait_ge(f_hadd, B)
            for g in range(B // 4):
                for k in range(TOPK):
                    rows = y_rows[k * TOK + g * G4:k * TOK + (g + 1) * G4].rearrange("(b t) c -> t b c", b=4)
                    sp.dma_start(yk[k][:, 4 * g:4 * g + 4, :], rows).then_inc(picks_in[g], 16)
            for g in range(B // 4):
                sp.wait_ge(yout_done, 4 * g + 4)
                sp.dma_start(out.rearrange("b n c -> n b c")[:, 4 * g:4 * g + 4, :],
                             yout[:, 4 * g:4 * g + 4, :]).then_inc(out_sent, 16)
            sp.wait_ge(out_sent, 16 * (B // 4))

        @block.gpsimd
        def _(pool):
            nc.gpsimd.memset(ones16[:, :], 1.0).then_inc(filled, 1)
            nc.gpsimd.memset(zeros[:, :], 0.0).then_inc(filled, 1)
            nc.gpsimd.memset(qk[:, :, :], 0.0).then_inc(filled, 1)
            nc.gpsimd.memset(kT[:, :, :, :], 0.0).then_inc(filled, 1)
            nc.gpsimd.memset(v_cur[:, :, :, :], 0.0).then_inc(filled, 1)
            nc.gpsimd.memset(xT1[:, :], 1.0).then_inc(filled, 1)
            nc.gpsimd.memset(XT1[:, :], 1.0).then_inc(filled, 1)
            nc.gpsimd.memset(encT[:, :], 1.0).then_inc(filled, 1)
            for p in range(2):
                nc.gpsimd.memset(xs1[p][:, :], 1.0).then_inc(filled, 1)
            pool.wait_ge(filled, FILLS)
            pool.wait_ge(attn_in, ATTN_IN)

            def attention(l):
                base = l * B

                def set_v(b):
                    pool.wait_ge(v_sb, base + b + 1)
                    if positive(base + b):
                        pool.wait_ge(o_ps, base + b)
                    nc.gpsimd.tensor_copy(v_cur[:, :, ::3, :],
                                          v_all[:, b, :, :].rearrange("p (a two) d -> p a two d", two=2)).then_inc(v_set, 1)

                def add_bias(b):
                    pool.wait_ge(xn_done, 2 * base + b + 1)
                    nc.gpsimd.tensor_tensor(h[:, b, :], h[:, b, :], proj_b[l][:, :], ALU.add).then_inc(b_added, 1)

                def rope_add(b):
                    pool.wait_ge(rope_mul, b + 1)
                    if positive(b):
                        pool.wait_ge(qkT_ps, b)
                    nc.gpsimd.tensor_tensor(qk[:, :, 0:HD], rope_a[:, :, :], rope_b[:, :, :],
                                            ALU.add).then_inc(qk_done, 1)

                def divide(b):
                    pool.wait_ge(rden_done, base + b + 1)
                    if positive(base + b):
                        pool.wait_ge(pT_ps, base + b)
                    nc.gpsimd.tensor_tensor(prob[:, :, :], sc[:, :, :],
                                            rden[:, :].unsqueeze(2).to_broadcast([T, HEADS, T]),
                                            ALU.mult).then_inc(p_done, 1)

                def step(s):
                    if in_flight(s, 3):
                        set_v(s - 3)
                    if in_flight(s, 0):
                        add_bias(s)
                    if l == 0 and in_flight(s, 0):
                        rope_add(s)
                    if in_flight(s, 2):
                        divide(s - 2)
                for s in range(DEPTH + 1):
                    step(s)
                with pool.Fori(DEPTH + 1, B - 1, 2) as s:
                    step(s)
                    step(s + 1)
                for s in range(B, B + DEPTH):
                    step(s)
            pool.wait_ge(rb_set, 1)
            attention(0)

            def add_ln(b):
                pool.wait_ge(xn_done, B + b + 1)
                nc.gpsimd.tensor_tensor(h[:, b, :], h[:, b, :], xn_all[:, b, :], ALU.add).then_inc(f_hadd, 1)
            with pool.Fori(0, B) as b:
                add_ln(b)
            pool.wait_ge(late_in, LATE_IN)
            nc.gpsimd.tensor_copy(sel16[:, :], sel[:, :]).then_inc(sel_done, 1)
            pool.wait_ge(slot_known, 2)
            nc.gpsimd.tensor_tensor(named[:, :, 0, :], blk_hot[:, :, :],
                                    tok1[:, 0:1].unsqueeze(2).to_broadcast([T, NPICK, NBLK]), ALU.mult).then_inc(named_done, 1)
            nc.gpsimd.tensor_tensor(named[:, :, 1, :], blk_hot[:, :, :],
                                    iota[0:T, 0:NPICK].unsqueeze(2).to_broadcast([T, NPICK, NBLK]),
                                    ALU.mult).then_inc(named_done, 1)

            def take_waits():
                nc.gpsimd.tensor_tensor(tick[:, :], tok1[0:1, 0:1], tok1[0:1, 0:1], ALU.add)

            def fetch(m, k, n):
                j, p, u = blk(m, k)
                if positive(u - 1):
                    pool.wait_ge(x_in[p], 16 * (u - 1))
                    pool.wait_ge(xg_ps, j - 1)
                pool.wait_ge(rows_ready, 1)
                nc.gpsimd.tensor_copy(idx_in[p][:, :], row_in[:, bass.ds(j, 1)]).then_inc(idx_set, 1)
                pool.wait_ge(idx_set, n)
                pool.wait_ge(ln_stored, 16)
                take_waits()
                nc.gpsimd.indirect_dma_start(xg[p][:, :], None, ln_rows,
                                             bass.IndirectOffsetOnAxis(idx_in[p][:, 0:1], 0)).then_inc(x_in[p], 16)

            def store(m, k, n):
                j, p, u = blk(m, k)
                if positive(u - 1):
                    pool.wait_ge(y_out[p], 16 * (u - 1))
                pool.wait_ge(rows_ready, 1)
                nc.gpsimd.tensor_copy(idx_out[p][:, :], row_out[:, bass.ds(j, 1)]).then_inc(idx_set, 1)
                pool.wait_ge(idx_set, n)
                pool.wait_ge(ys_done, j + 1)
                take_waits()
                nc.gpsimd.indirect_dma_start(y_rows, bass.IndirectOffsetOnAxis(idx_out[p][:, 0:1], 0), ys[p][:, :],
                                             None).then_inc(y_out[p], 16)
            for k in range(4):
                fetch(0, k, k + 1)
            for k in range(2):
                fetch(1, k + 2, 2 * k + 5)
                store(0, k, 2 * k + 6)
            with pool.Fori(1, NBLK // 2 - 2) as m:
                for k in range(2):
                    fetch(m, k + 4, 4 * m + 2 * k + 5)
                    store(m, k, 4 * m + 2 * k + 6)
            for k in range(4):
                store(NBLK // 2 - 2, k, 2 * NBLK - 3 + k)
            attention(1)

        @block.scalar
        def _(act):
            def sqrt_var(k, lo, hi):
                act.wait_ge(ln_step, 10 * k + 5)
                nc.scalar.activation(lnv[:, 5, lo:hi], lnv[:, 4, lo:hi], ACT.Sqrt).then_inc(sqrt_done, 1)

            def attention(l, before):
                base = l * B

                def evac_qk(b):
                    act.wait_ge(qkT_ps, base + b + 1)
                    act.wait_ge(s_ps, 2 * (base + b))
                    nc.scalar.copy(qT[:, :, :], bank[3][:, 0:NG * T]).then_inc(q_sb, 1)
                    for j in range(4):
                        nc.scalar.copy(kT[SLOT * j:SLOT * j + SLOT, :, j, :],
                                       bank[3][SLOT * j:SLOT * j + SLOT, NG * T:2 * NG * T]).then_inc(k_sb, 1)

                def evac_x(b):
                    act.wait_ge(xT_ps, base + b + 1)
                    act.wait_ge(v_ps, base + b)
                    if l == 0:
                        nc.scalar.activation(xT0[:, :], bank[0][:, 0:T], ACT.Identity, bias=ln0[:, 1:2],
                                             scale=ln0[:, 0:1]).then_inc(xT_sb, 1)
                        nc.scalar.activation(xT1[0:C1, :], bank[0][0:C1, T:2 * T], ACT.Identity, bias=ln1[:, 1:2],
                                             scale=ln1[:, 0:1]).then_inc(xT_sb, 1)
                    else:
                        nc.scalar.copy(xT0[:, :], bank[0][:, 0:T]).then_inc(xT_sb, 1)
                        nc.scalar.copy(xT1[0:C1, :], bank[0][0:C1, T:2 * T]).then_inc(xT_sb, 1)

                def evac_p(b):
                    act.wait_ge(pT_ps, base + b + 1)
                    if positive(base + b):
                        act.wait_ge(o_ps, base + b)
                    nc.scalar.copy(pT[:, :, :].rearrange("p (j h) q -> p j (h q)", j=2),
                                   quad[0:T, 2:4, 0:HALF]).then_inc(pT_sb, 1)

                def evac_o(b):
                    act.wait_ge(o_ps, base + b + 1)
                    if positive(base + b):
                        act.wait_ge(y_ps, base + b)
                    nc.scalar.copy(oT[:, 0, :], bank[2][:, C:C + T])
                    nc.scalar.copy(oT[0:C1, 1, :], bank[2][0:C1, C + T:C + 2 * T]).then_inc(oT_sb, 1)

                def exp(b):
                    act.wait_ge(s_sub, base + b + 1)
                    nc.scalar.activation(sc[:, :, :], sc[:, :, :], ACT.Exp, scale=0.25).then_inc(e_done, 1)
                    if l == 0:
                        nc.scalar.activation(sink_e[:, b, :], sink_e[:, b, :], ACT.Exp,
                                             scale=0.25).then_inc(sink_done, 1)

                def evac_v(b):
                    act.wait_ge(v_ps, base + b + 1)
                    nc.scalar.copy(v_all[:, b, :, 0:HD],
                                   bank[2][0:T, 0:C].rearrange("p (h d) -> p h d", d=HD)).then_inc(v_sb, 1)

                def step(s):
                    if static_in(s, before):
                        before[s]()
                    if in_flight(s, 4):
                        evac_p(s - 4)
                    if in_flight(s, 0):
                        evac_x(s)
                    if in_flight(s, 4):
                        evac_o(s - 4)
                    if in_flight(s, 1):
                        evac_qk(s - 1)
                    if in_flight(s, 2):
                        exp(s - 2)
                    if in_flight(s, 0):
                        evac_v(s)
                for s in range(DEPTH + 1):
                    step(s)
                with act.Fori(DEPTH + 1, B - 1, 2) as s:
                    step(s)
                    step(s + 1)
                for s in range(B, B + DEPTH):
                    step(s)

            def keep_rows(l, g):
                a, c = TURN_BANKS[g % 2]
                act.wait_ge(f_xT_ps, 4 * l + g + 1)
                nc.scalar.copy(XT0[:, g * G4:(g + 1) * G4], bank[a][:, 0:G4]).then_inc(f_xT_sb, 1)
                nc.scalar.copy(XT1[0:C1, g * G4:(g + 1) * G4], bank[c][0:C1, 0:G4]).then_inc(f_xT_sb, 1)

            act.wait_ge(filled, FILLS)
            nc.scalar.activation(warm[:, :], ones16[0:1, 0:1], ACT.Sqrt)
            sqrt_var(0, 0, HB)
            act.wait_ge(attn_in, ATTN_IN)
            attention(0, {2: lambda: sqrt_var(1, HB, B), B + 2: lambda: sqrt_var(2, 0, LB),
                          B + 4: lambda: (keep_rows(0, 0), keep_rows(0, 1))})
            sqrt_var(3, LB, B)
            keep_rows(0, 2)
            keep_rows(0, 3)
            act.wait_ge(f_route, 2)
            nc.scalar.activation(r1[:, :, :], r1[:, :, :], ACT.Exp).then_inc(f_exp, 1)
            def keep_block(m, k):
                j, p, u = blk(m, k)
                act.wait_ge(xg_ps, j + 1)
                if positive(j - 1):
                    act.wait_ge(hid_ps, 2 * (j - 1))
                nc.scalar.copy(xs0[p][:, :], bank[0][:, 0:S]).then_inc(xs_sb, 1)
                nc.scalar.copy(xs1[p][0:C1, :], bank[0][0:C1, S:2 * S]).then_inc(xs_sb, 1)

            def gelu_block(m, k):
                j, p, u = blk(m, k)
                if positive(j - 1):
                    act.wait_ge(blk_ps, j - 1)
                act.wait_ge(hid_ps, 2 * j + 1)
                nc.scalar.activation(hb[p][:, 0:4, :].rearrange("p c s -> p (c s)"), bank[1 + 2 * p][:, 0:4 * S],
                                     ACT.Gelu).then_inc(hid_sb, 1)
                act.wait_ge(hid_ps, 2 * j + 2)
                nc.scalar.activation(hb[p][:, 4:6, :].rearrange("p c s -> p (c s)"), bank[2 + 2 * p][:, 0:2 * S],
                                     ACT.Gelu).then_inc(hid_sb, 1)
            keep_block(0, 0)
            keep_block(0, 1)
            gelu_block(0, 0)
            for k in range(1, 3):
                keep_block(0, k + 1)
                gelu_block(0, k)
            with act.Fori(1, NBLK // 2 - 1) as m:
                for k in range(1, 3):
                    keep_block(m, k + 1)
                    gelu_block(m, k)
            gelu_block(NBLK // 2 - 1, 1)
            sqrt_var(4, 0, 4)
            attention(1, {2: lambda: sqrt_var(5, 4, HB), 5: lambda: sqrt_var(6, HB, B),
                          B + 2: lambda: sqrt_var(7, 0, LB), B + 4: lambda: (keep_rows(1, 0), keep_rows(1, 1))})
            sqrt_var(8, LB, B)
            def keep_code(g):
                act.wait_ge(f_enc_ps, g + 1)
                nc.scalar.copy(encT[0:R1, g * G4:(g + 1) * G4], bank[6 + g % 2][0:R1, 0:G4]).then_inc(f_enc_sb, 1)
            keep_code(0)
            keep_code(1)
            keep_rows(1, 2)
            keep_rows(1, 3)
            keep_code(2)
            keep_code(3)
            act.wait_ge(f_route, 9)
            nc.scalar.activation(r1[:, :, 0:E1], r1[:, :, 0:E1], ACT.Exp).then_inc(f_exp, 1)
            for g in range(B // 4):
                act.wait_ge(oneT_ps, g + 1)
                nc.scalar.copy(oneT[:, g * G4:(g + 1) * G4], bank[4 + g][0:E1, 0:G4]).then_inc(oneT_sb, 1)
            def gelus(g):
                if positive(g):
                    act.wait_ge(gm_done, RC * g)
                for c in range(RC):
                    act.wait_ge(f_hid_ps, g * RC + c + 1)
                    nc.scalar.activation(hid[:, c, :], bank[c][:, 0:G4], ACT.Gelu).then_inc(f_hid_sb, 1)

            def keep_yT(g):
                act.wait_ge(yT_ps, 2 * g + 1)
                if positive(g):
                    act.wait_ge(f_y_ps, 2 * g)
                nc.scalar.copy(yT0[:, :], bank[6][:, 0:G4]).then_inc(yT_sb, 1)
                act.wait_ge(yT_ps, 2 * g + 2)
                nc.scalar.copy(yT1[:, :], bank[7][0:C1, 0:G4]).then_inc(yT_sb, 1)
            for i in range(0, 8, 2):
                keep_mark(act, nc.scalar.copy, i)
            gelus(0)
            for i in range(8, 16, 2):
                keep_mark(act, nc.scalar.copy, i)
            for g in range(1, B // 4):
                gelus(g)
                keep_yT(g - 1)
            keep_yT(B // 4 - 1)

        @block.vector
        def _(dve):
            def row_stats(b):
                nc.vector.bn_stats(stats[:, b, :], h[:, b, :]).then_inc(stats_done, 1)

            def ln(k, phase, lo, hi):
                dve.wait_ge(stats_done, B * phase + hi)
                n = 10 * k
                add, sub, mul = ALU.add, ALU.subtract, ALU.mult
                nc.vector.tensor_tensor(lnv[:, 0, lo:hi], stats[:, lo:hi, 1], stats[:, lo:hi, 4], add).then_inc(ln_step, 1)
                nc.vector.tensor_tensor(lnv[:, 1, lo:hi], stats[:, lo:hi, 1], stats[:, lo:hi, 4], sub).then_inc(ln_step, 1)
                nc.vector.tensor_tensor(lnv[:, 3, lo:hi], stats[:, lo:hi, 2], stats[:, lo:hi, 5], add).then_inc(ln_step, 1)
                dve.wait_ge(ln_step, n + 3)
                nc.vector.scalar_tensor_tensor(lnv[:, 2, lo:hi], lnv[:, 1, lo:hi], 0.25, lnv[:, 1, lo:hi], mul, mul).then_inc(ln_step, 1)
                nc.vector.tensor_scalar(mean[:, lo:hi], lnv[:, 0, lo:hi], 0.5, None, mul).then_inc(ln_done, 1)
                nc.vector.tensor_scalar(lnv[:, 6, lo:hi], lnv[:, 3, lo:hi], 1.0 / C, EPS, mul, add).then_inc(ln_done, 1)
                dve.wait_ge(ln_done, 2 * k + 2)
                dve.wait_ge(ln_step, n + 4)
                nc.vector.tensor_tensor(lnv[:, 4, lo:hi], lnv[:, 6, lo:hi], lnv[:, 2, lo:hi], add).then_inc(ln_step, 1)
                dve.wait_ge(sqrt_done, k + 1)
                nc.vector.reciprocal(lnv[:, 0, lo:hi], lnv[:, 5, lo:hi]).then_inc(ln_step, 1)
                dve.wait_ge(ln_step, n + 6)
                nc.vector.tensor_tensor(lnv[:, 1, lo:hi], lnv[:, 4, lo:hi], lnv[:, 0, lo:hi], mul).then_inc(ln_step, 1)
                dve.wait_ge(ln_step, n + 7)
                nc.vector.tensor_tensor(lnv[:, 2, lo:hi], lnv[:, 1, lo:hi], lnv[:, 5, lo:hi], add).then_inc(ln_step, 1)
                dve.wait_ge(ln_step, n + 8)
                nc.vector.tensor_scalar(lnv[:, 3, lo:hi], lnv[:, 2, lo:hi], 0.5, None, mul).then_inc(ln_step, 1)
                dve.wait_ge(ln_step, n + 9)
                nc.vector.reciprocal(rstd[:, lo:hi], lnv[:, 3, lo:hi]).then_inc(ln_step, 1)
                dve.wait_ge(ln_step, n + 10)

            def normalise(b, n):
                dve.wait_ge(xT_ps, n)
                nc.vector.tensor_scalar(xn[:, :], h[:, b, :], mean[:, bass.ds(b, 1)], rstd[:, bass.ds(b, 1)],
                                        ALU.subtract, ALU.mult).then_inc(xn_done, 1)

            def normalise_all(phase, lo, hi):
                for b in range(lo, hi):
                    nc.vector.tensor_scalar(xn_all[:, b, :], h[:, b, :], mean[:, b:b + 1], rstd[:, b:b + 1],
                                            ALU.subtract, ALU.mult).then_inc(xn_done, 1)

            def attention(l, after):
                base = l * B

                def row_max(b):
                    raw = quad[0:T, 0:2, 0:HALF].rearrange("p j (h k) -> p j h k", k=T)
                    by_bank = lambda x: x.rearrange("p (j h) -> p j h", j=2)
                    dve.wait_ge(s_ps, 2 * (base + b + 1))
                    nc.vector.tensor_reduce(by_bank(top[:, b, :]), raw, AX_X, ALU.max).then_inc(top_raw, 1)
                    dve.wait_ge(top_raw, base + b + 1)
                    if l == 0:
                        nc.vector.tensor_tensor(top[:, b, :], top[:, b, :], sinks4[:, :], ALU.max).then_inc(top_done, 1)
                        dve.wait_ge(top_done, b + 1)
                        nc.vector.tensor_tensor(sink_e[:, b, :], sinks4[:, :], top[:, b, :], ALU.subtract)
                    if positive(base + b):
                        dve.wait_ge(p_done, base + b)
                    nc.vector.tensor_tensor(sc[:, :, :].rearrange("p (j h) k -> p j h k", j=2), raw,
                                            by_bank(top[:, b, :]).unsqueeze(3).to_broadcast([T, 2, HEADS // 2, T]),
                                            ALU.subtract).then_inc(s_sub, 1)

                def rope(b):
                    dve.wait_ge(qk_ps, base + b + 1)
                    x = bank[1][0:T, 0:2 * C].rearrange("p (h d) -> p h d", d=HD)
                    if l == 1:
                        dve.wait_ge(qkT_ps, base + b)
                        nc.vector.tensor_copy(qk[:, :, 0:HD], x).then_inc(rope_mul, 1)
                        return
                    if not isinstance(b, int) or b:
                        dve.wait_ge(qk_done, b)
                    nc.vector.tensor_tensor(rope_a[:, :, :], x, rope_c.unsqueeze(1).to_broadcast([T, 2 * HEADS, HD]),
                                            ALU.mult)
                    xs = bank[1][0:T, 0:2 * C].rearrange("p (h i two) -> p h i two", i=HD // 2, two=2)
                    nc.vector.tensor_tensor(
                        rope_b[:, :, :].rearrange("p h (i two) -> p h i two", two=2), xs[:, :, :, ::-1],
                        rope_s.rearrange("p (i two) -> p i two", two=2).unsqueeze(1)
                        .to_broadcast([T, 2 * HEADS, HD // 2, 2]), ALU.mult).then_inc(rope_mul, 1)

                def residual(b):
                    dve.wait_ge(y_ps, base + b + 1)
                    dve.wait_ge(b_added, base + b + 1)
                    y = bank[0][0:T, 2 * T:2 * T + C]
                    if l == 0:
                        nc.vector.scalar_tensor_tensor(h[:, b, :], y, rezero[:, 0:1], h[:, b, :], ALU.mult,
                                                       ALU.add).then_inc(h_done, 1)
                    else:
                        nc.vector.tensor_tensor(h[:, b, :], y, h[:, b, :], ALU.add).then_inc(h_done, 1)
                    dve.wait_ge(h_done, base + b + 1)
                    row_stats(b)

                def row_sum(b):
                    dve.wait_ge(e_done, base + b + 1)
                    nc.vector.tensor_reduce(den[:, :], sc[:, :, :], AX_X, ALU.add).then_inc(den_done, 1)
                    if l == 0:
                        dve.wait_ge(den_done, 2 * b + 1)
                        dve.wait_ge(sink_done, b + 1)
                        nc.vector.tensor_tensor(den[:, :], den[:, :], sink_e[:, b, :], ALU.add).then_inc(den_done, 1)
                        dve.wait_ge(den_done, 2 * b + 2)
                    else:
                        dve.wait_ge(den_done, 2 * B + b + 1)
                    nc.vector.reciprocal(rden[:, :], den[:, :]).then_inc(rden_done, 1)

                def step(s):
                    if in_flight(s, 2):
                        row_max(s - 2)
                    if in_flight(s, 0):
                        rope(s)
                    if in_flight(s + 1, 0):
                        normalise(s + 1, base + s + 1)
                    if in_flight(s, 2):
                        row_sum(s - 2)
                    if in_flight(s, 4):
                        residual(s - 4)
                    if static_in(s, after):
                        after[s]()

                if l:
                    normalise(0, base)
                for s in range(DEPTH):
                    step(s)
                with dve.Fori(DEPTH, B - 2, 2) as s:
                    step(s)
                    step(s + 1)
                for s in range(B - 1, B + DEPTH):
                    step(s)

            dve.wait_ge(txt_in, 16)
            for i in range(B // 2):
                dve.wait_ge(patch_ps, i + 1)
                nc.vector.tensor_copy(h[0:NPATCH, 2 * i, :], bank[i % 4][0:NPATCH, 0:C])
                nc.vector.tensor_copy(h[0:NPATCH, 2 * i + 1, :], bank[i % 4][64:64 + NPATCH, 0:C]).then_inc(patch_sb, 1)
                dve.wait_ge(patch_sb, i + 1)
                row_stats(2 * i)
                row_stats(2 * i + 1)
                if i == HB // 2:
                    ln(0, 0, 0, HB)
                    normalise(0, 0)

            dve.wait_ge(attn_in, ATTN_IN)
            dve.wait_ge(filled, FILLS)
            nc.vector.tensor_copy(ident16[:, :], ident[0:T, 0:T])
            nc.vector.tensor_copy(mask16[:, :].rearrange("p (h k) -> p h k", k=T),
                                  mask_in[:, :].unsqueeze(1).to_broadcast([T, 6, T]))
            nc.vector.tensor_copy(tri16[:, :], tri_in[:, :])
            nc.vector.tensor_scalar(proj_b[0][:, :], proj_b[0][:, :], rezero[:, 0:1], None, ALU.mult).then_inc(rb_set, 1)
            nc.vector.tensor_scalar(sinks4[:, :], sinks[:, :], 4.0, None, ALU.mult)
            def ln_early(k, phase):
                ln(k, phase, 0, LB)
                normalise_all(phase, 0, HB)

            def ln_late(k, phase):
                normalise_all(phase, HB, LB)
                ln(k, phase, LB, B)
                normalise_all(phase, LB, B)
            attention(0, {1: lambda: ln(1, 0, HB, B), B + 1: lambda: ln_early(2, 1)})
            ln_late(3, 1)

            dve.wait_ge(late_in, LATE_IN)
            dve.wait_ge(f_log_ps, B)
            bc = lambda x, n: x.unsqueeze(2).to_broadcast([T, B, n])
            logit0 = bank[2][0:T, 0:B * E0].rearrange("p (b e) -> p b e", e=E0)
            nexp = iota[0:T, 0:E0].unsqueeze(1).to_broadcast([T, B, E0])
            nc.vector.tensor_reduce(rs[0][:, :], logit0, AX_X, ALU.max).then_inc(f_route, 1)
            dve.wait_ge(f_route, 1)
            nc.vector.tensor_tensor(r1[:, :, :], logit0, bc(rs[0][:, :], E0), ALU.subtract).then_inc(f_route, 1)
            dve.wait_ge(f_exp, 1)
            nc.vector.tensor_reduce(rs[1][:, :], r1[:, :, :], AX_X, ALU.add).then_inc(f_route, 1)
            dve.wait_ge(f_route, 3)
            nc.vector.reciprocal(rs[2][:, :], rs[1][:, :]).then_inc(f_route, 1)
            dve.wait_ge(f_route, 4)
            nc.vector.tensor_tensor(r1[:, :, :], r1[:, :, :], bc(rs[2][:, :], E0), ALU.mult).then_inc(f_route, 1)
            cnt = 5
            for k in range(TOPK):
                best = gates[:, k, :]
                dve.wait_ge(f_route, cnt + k)
                nc.vector.tensor_reduce(best, r1[:, :, :], AX_X, ALU.max).then_inc(pick_done, 1)
                dve.wait_ge(pick_done, 5 * k + 1)
                nc.vector.tensor_tensor(r2[:, :, :], r1[:, :, :], bc(best, E0), ALU.is_lt).then_inc(pick_done, 1)
                dve.wait_ge(pick_done, 5 * k + 2)
                nc.vector.scalar_tensor_tensor(r3[:, :, :], r2[:, :, :], float(E0), nexp, ALU.mult, ALU.add).then_inc(pick_done, 1)
                dve.wait_ge(pick_done, 5 * k + 3)
                nc.vector.tensor_reduce(rs[1][:, :], r3[:, :, :], AX_X, ALU.min).then_inc(pick_done, 1)
                dve.wait_ge(pick_done, 5 * k + 4)
                nc.vector.tensor_tensor(pick[k][:, :, :], nexp, bc(rs[1][:, :], E0), ALU.is_equal).then_inc(pick_done, 1)
                dve.wait_ge(pick_done, 5 * k + 5)
                if k == 0:
                    nc.vector.scalar_tensor_tensor(r1[:, :, :], pick[0][:, :, :], -2.0, r1[:, :, :], ALU.mult, ALU.add) \
                        .then_inc(f_route, 1)
            steps = [0]

            def link(ins):
                steps[0] += 1
                ins.then_inc(sort_step, 1)
                dve.wait_ge(sort_step, steps[0])
            tt, ts, stt = nc.vector.tensor_tensor, nc.vector.tensor_scalar, nc.vector.scalar_tensor_tensor
            tt(picks16[:, :, :], pick[0][:, :, :], pick[1][:, :, :], ALU.add).then_inc(pick_done, 1)
            dve.wait_ge(count_ps, 1)
            link(nc.vector.tensor_reduce(picked[:, :], bank[1][0:T, 0:B * E0].rearrange("p (b e) -> p e b", e=E0),
                                         AX_X, ALU.add))
            link(ts(limits[:, :], iota[0:T, 0:MAXB], float(S), None, ALU.mult))
            link(tt(over[:, :, :], picked[:, :].unsqueeze(2).to_broadcast([T, E0, MAXB]),
                    limits[:, :].unsqueeze(1).to_broadcast([T, E0, MAXB]), ALU.is_gt))
            link(nc.vector.tensor_reduce(nblk[:, :], over[:, :, :], AX_X, ALU.add))
            src, dst = nblk, blk_a
            for d in (1, 2, 4, 8):
                nc.vector.tensor_copy(dst[:, 0:d], src[:, 0:d]).then_inc(sort_step, 1)
                steps[0] += 1
                link(tt(dst[:, d:E0], src[:, d:E0], src[:, 0:E0 - d], ALU.add))
                src, dst = dst, (blk_b if dst is blk_a else blk_a)
            blk_end = src
            link(tt(passed[:, :, :], blk_end[0:1, :].unsqueeze(1).to_broadcast([1, NBLK, E0]),
                    iota[0:1, 0:NBLK].unsqueeze(2).to_broadcast([1, NBLK, E0]), ALU.is_le))
            link(nc.vector.tensor_reduce(expert_f[:, :], passed[:, :, :], AX_X, ALU.add))
            ts(expert_i[:, :], expert_f[:, :], float(E0 - 1), None, ALU.min).then_inc(who_ready, 1)
            link(tt(first_slot[:, :], blk_end[:, :], nblk[:, :], ALU.subtract))
            link(ts(first_slot[:, :], first_slot[:, :], float(S), None, ALU.mult))
            dve.wait_ge(count_ps, 2)
            link(tt(place[:, :, :], bank[0][0:T, 0:B * E0].rearrange("p (b e) -> p b e", e=E0),
                    first_slot[:, :].unsqueeze(1).to_broadcast([T, B, E0]), ALU.add))
            for k in range(TOPK):
                link(tt(r2[:, :, :], pick[k][:, :, :], place[:, :, :], ALU.mult))
                link(nc.vector.tensor_reduce(slot[:, k, :], r2[:, :, :], AX_X, ALU.add))
            link(ts(blk_of[:, :, :], slot[:, :, :], 1.0 / S, -(S - 1) / (2.0 * S), ALU.mult, ALU.add))
            link(ts(blk_of[:, :, :], blk_of[:, :, :], ROUND, -ROUND, ALU.add, ALU.add))
            link(stt(in_blk[:, :, :], blk_of[:, :, :], -float(S), slot[:, :, :], ALU.mult, ALU.add))
            flat = lambda x, n: x[:, :, :].rearrange("p k b -> p (k b)").unsqueeze(2).to_broadcast([T, NPICK, n])
            tt(blk_hot[:, :, :], flat(blk_of, NBLK), iota[0:T, 0:NBLK].unsqueeze(1).to_broadcast([T, NPICK, NBLK]),
               ALU.is_equal).then_inc(slot_known, 2)
            tt(in_hot[:, :, :], flat(in_blk, S), iota[0:T, :].unsqueeze(1).to_broadcast([T, NPICK, S]),
               ALU.is_equal).then_inc(who_ready, 1)
            dve.wait_ge(who_ps, 1)
            link(nc.vector.tensor_copy(who[:, :, :], bank[2][:, 0:2 * NBLK].rearrange("p (x j) -> p x j", x=2)))
            link(stt(wt[0][:, :], who[:, 1, :], float(T), who[:, 0, :], ALU.mult, ALU.add))
            link(ts(wt[1][:, :], wt[0][:, :], float(TOK), -float(TOK), ALU.is_gt, ALU.mult))
            link(tt(wt[1][:, :], wt[1][:, :], wt[0][:, :], ALU.add))
            link(ts(wt[1][:, :], wt[1][:, :], -1.0, 0.0, ALU.add, ALU.max))
            link(nc.vector.tensor_copy(row_in[:, :], wt[1][:, :]))
            link(ts(wt[2][:, :], who[:, 0, :], 0.0, None, ALU.is_gt))
            link(stt(wt[3][:, :], wt[0][:, :], -1.0, pad[:, :], ALU.add, ALU.subtract))
            link(tt(wt[3][:, :], wt[3][:, :], wt[2][:, :], ALU.mult))
            link(tt(wt[3][:, :], wt[3][:, :], pad[:, :], ALU.add))
            nc.vector.tensor_copy(row_out[:, :], wt[3][:, :]).then_inc(rows_ready, 1)

            def finish_block(m, k):
                j, p, u = blk(m, k)
                if positive(u - 1):
                    dve.wait_ge(y_out[p], 16 * (u - 1))
                dve.wait_ge(w2_in[p], 32 * u)
                dve.wait_ge(blk_ps, j + 1)
                nc.vector.tensor_tensor(ys[p][:, :], bank[5 + p][:, 0:C], b2a[p][:, :], ALU.add).then_inc(ys_done, 1)
            finish_block(0, 0)
            finish_block(0, 1)
            with dve.Fori(1, NBLK // 2) as m:
                finish_block(m, 0)
                finish_block(m, 1)

            dve.wait_ge(f_hadd, B)

            def add_picks(g):
                dve.wait_ge(picks_in[g], 16 * TOPK)
                for k in range(TOPK):
                    for j in range(4):
                        b = 4 * g + j
                        if k:
                            dve.wait_ge(moe_done, 8 * g + j + 1)
                        nc.vector.scalar_tensor_tensor(h[:, b, :], yk[k][:, b, :], gates[:, k, b:b + 1], h[:, b, :],
                                                       ALU.mult, ALU.add).then_inc(moe_done, 1)
                for j in range(4):
                    dve.wait_ge(moe_done, 8 * g + 5 + j)
                    row_stats(4 * g + j)
            add_picks(0)
            ln(4, 2, 0, 4)
            attention(1, {0: lambda: add_picks(1), 1: lambda: ln(5, 2, 4, HB), 2: lambda: add_picks(2),
                          3: lambda: add_picks(3), 4: lambda: ln(6, 2, HB, B), B + 1: lambda: ln_early(7, 3)})
            ln_late(8, 3)

            dve.wait_ge(f_log_ps, 2 * B)
            logit1 = bank[2][0:T, 0:B * E1].rearrange("p (b e) -> p b e", e=E1)
            q1, q2, q3 = (x[:, :, 0:E1] for x in (r1, r2, r3))
            nexp1 = iota[0:T, 0:E1].unsqueeze(1).to_broadcast([T, B, E1])
            nc.vector.tensor_reduce(rs[0][:, :], logit1, AX_X, ALU.max).then_inc(f_route, 1)
            dve.wait_ge(f_route, 7)
            nc.vector.tensor_tensor(q2, logit1, bc(rs[0][:, :], E1), ALU.is_lt).then_inc(f_route, 1)
            nc.vector.tensor_tensor(q1, logit1, bc(rs[0][:, :], E1), ALU.subtract).then_inc(f_route, 1)
            dve.wait_ge(f_route, 9)
            nc.vector.scalar_tensor_tensor(q3, q2, float(E0), nexp1, ALU.mult, ALU.add).then_inc(f_route, 1)
            dve.wait_ge(f_route, 10)
            nc.vector.tensor_reduce(rs[1][:, :], q3, AX_X, ALU.min).then_inc(f_route, 1)
            dve.wait_ge(f_route, 11)
            nc.vector.tensor_tensor(one_hot1[:, :, :], nexp1, bc(rs[1][:, :], E1), ALU.is_equal).then_inc(f_route, 1)
            dve.wait_ge(f_exp, 2)
            nc.vector.tensor_reduce(rs[2][:, :], q1, AX_X, ALU.add).then_inc(f_route, 1)
            dve.wait_ge(f_route, 13)
            nc.vector.reciprocal(rs[3][:, :], rs[2][:, :]).then_inc(f_route, 1)
            dve.wait_ge(f_route, 14)

            for g in range(B // 4):
                dve.wait_ge(oneT_sb, g + 1)
                nc.vector.tensor_copy(oneT16[:, g * G4:(g + 1) * G4], oneT[:, g * G4:(g + 1) * G4]).then_inc(one16_done, 1)
            for i in range(1, 16, 2):
                keep_mark(dve, nc.vector.tensor_copy, i)
            dve.wait_ge(mark_sb[0], 8)

            def mask_hidden(g):
                if positive(g):
                    dve.wait_ge(yT_ps, 2 * g)
                for c in range(RC):
                    dve.wait_ge(f_hid_sb, g * RC + c + 1)
                    nc.vector.tensor_tensor(gm[:, c, :], hid[:, c, :], marks[:, c, bass.ds(g * G4, G4)],
                                            ALU.mult).then_inc(gm_done, 1)

            def finish(g):
                for j in range(4):
                    dve.wait_ge(f_y_ps, 2 * g + j // 2 + 1)
                    b = 4 * g + j
                    nc.vector.scalar_tensor_tensor(yout[:, b, :], bank[4 + j // 2][0:T, (j % 2) * C:(j % 2 + 1) * C],
                                                   rs[3][:, bass.ds(b, 1)], h[:, b, :], ALU.mult,
                                                   ALU.add).then_inc(yout_done, 1)
            mask_hidden(0)
            for g in range(1, B // 4):
                mask_hidden(g)
                finish(g - 1)
            finish(B // 4 - 1)

        @block.tensor
        def _(pe):
            mm = nc.tensor.matmul

            def product(dst, pairs, last):
                for i, (lhsT, rhs) in enumerate(pairs):
                    ins = mm(dst, lhsT, rhs, start=(i == 0), stop=(i == len(pairs) - 1))
                if last is not None:
                    ins.then_inc(last, 1)

            def keep_warm(n, spare):
                for _ in range(n):
                    mm(bank[spare][:, 0:512], zeros[:, 0:P], zeros[:, :],
                       start=True, stop=True)

            def turn_x(b, n, frees):
                pe.wait_ge(xn_done, n)
                for free, free_at in frees:
                    if not isinstance(free_at, int) or free_at > 0:
                        pe.wait_ge(free, free_at)
                nc.tensor.transpose(bank[0][:, 0:T], xn[:, 0:P], ident[0:T, 0:T])
                nc.tensor.transpose(bank[0][0:C1, T:2 * T], xn[:, P:C], ident[0:T, 0:T]).then_inc(xT_ps, 1)

            def turn_rows(l, g):
                a, c = TURN_BANKS[g % 2]
                pe.wait_ge(xn_done, (2 * l + 1) * B + 4 * g + 4)
                if g >= 2:
                    pe.wait_ge(f_xT_sb, 8 * l + 2 * (g - 1))
                for j in range(4):
                    b = 4 * g + j
                    nc.tensor.transpose(bank[a][:, j * T:(j + 1) * T], xn_all[:, b, 0:P], ident[0:T, 0:T])
                    ins = nc.tensor.transpose(bank[c][0:C1, j * T:(j + 1) * T], xn_all[:, b, P:C], ident[0:T, 0:T])
                ins.then_inc(f_xT_ps, 1)

            def attention(l, after):
                base = l * B

                def turn_qk(b):
                    if l == 0:
                        pe.wait_ge(qk_done, b + 1)
                    else:
                        pe.wait_ge(rope_mul, base + b + 1)
                    pe.wait_ge(q_sb, base + b)
                    pe.wait_ge(k_sb, 4 * (base + b))
                    for g in range(2 * NG):
                        ins = nc.tensor.transpose(bank[3][:, g * T:(g + 1) * T],
                                                  qk[:, 4 * g:4 * g + 4, :].rearrange("p h d -> p (h d)"),
                                                  ident[0:T, 0:T])
                    ins.then_inc(qkT_ps, 1)

                def turn_p(b):
                    pe.wait_ge(p_done, base + b + 1)
                    pe.wait_ge(pT_sb, base + b)
                    for i in range(HEADS):
                        ins = nc.tensor.transpose(bank[6 + i // 6][0:T, (i % 6) * T:(i % 6 + 1) * T], prob[:, i, :],
                                                  ident[0:T, 0:T])
                    ins.then_inc(pT_ps, 1)

                def scores(b):
                    pe.wait_ge(q_sb, base + b + 1)
                    pe.wait_ge(k_sb, 4 * (base + b + 1))
                    pe.wait_ge(s_sub, base + b)
                    parts = [(0, 0, 4, 0), (1, 0, 2, 0), (1, 2, 4, 1), (2, 0, 4, 1)]
                    for g, a, z, half in parts:
                        col = (4 * g + a) * T - half * HALF
                        first = (g, a) in ((0, 0), (1, 2))
                        ins = mm(bank[4 + half][0:T, col:col + (z - a) * T], qT[:, g, :],
                                 kT[:, g, a:z, :].rearrange("p h t -> p (h t)"), start=True, stop=(l == 1),
                                 skip_group_check=True)
                        if l == 0:
                            ins = mm(bank[4 + half][0:T, col:col + (z - a) * T], ident16[:, :],
                                     mask16[:, 0:(z - a) * T], start=False, stop=True, skip_group_check=True)
                        if z * T + 4 * g * T - half * HALF == HALF:
                            ins.then_inc(s_ps, 1)

                def qk_product(b):
                    pe.wait_ge(xT_sb, 2 * (base + b + 1))
                    pe.wait_ge(rope_mul, base + b)
                    product(bank[1][0:T, 0:2 * C], [(xT0[:, :], qkv_w0[l][:, 0:2 * C]), (xT1[:, :], qkv_w1[l][:, 0:2 * C])],
                            qk_ps)

                def v_product(b):
                    pe.wait_ge(v_sb, base + b)
                    if positive(base + b - 3):
                        pe.wait_ge(oT_sb, base + b - 3)
                    product(bank[2][0:T, 0:C], [(xT0[:, :], qkv_w0[l][:, 2 * C:]), (xT1[:, :], qkv_w1[l][:, 2 * C:])], v_ps)

                def project(b):
                    pe.wait_ge(oT_sb, base + b + 1)
                    pe.wait_ge(xT_sb, 2 * (base + (min(b + 5, B) if isinstance(b, int) else b + 5)))
                    if positive(base + b):
                        pe.wait_ge(h_done, base + b)
                    product(bank[0][0:T, 2 * T:2 * T + C],
                            [(oT[:, 0, :], proj_w[l][:, 0, :]), (oT[0:C1, 1, :], proj_w[l][0:C1, 1, :])], y_ps)

                def values(b):
                    pe.wait_ge(pT_sb, base + b + 1)
                    pe.wait_ge(v_set, base + b + 1)
                    pe.wait_ge(v_sb, base + (min(b + 4, B) if isinstance(b, int) else b + 4))
                    if positive(base + b):
                        pe.wait_ge(oT_sb, base + b)
                    for h0 in range(HEADS):
                        pair, half = h0 // 2, h0 % 2
                        at, col = SLOT * (pair % 4), C + (pair // 4) * T
                        ins = mm(bank[2][at:at + SLOT, col:col + T],
                                 v_cur[:, pair, 2 * half:2 * half + 2, :].rearrange("p a d -> p (a d)"),
                                 pT[:, h0, :], start=(half == 0), stop=(half == 1))
                    ins.then_inc(o_ps, 1)

                def step(s):
                    if in_flight(s, 2):
                        scores(s - 2)
                    if in_flight(s, 0):
                        turn_x(s, 2 * l * B + s + 1, [(xT_sb, 2 * (base + s)), (h_done, base + s - 4)])
                    if in_flight(s, 4):
                        values(s - 4)
                    if in_flight(s, 1):
                        turn_qk(s - 1)
                    if in_flight(s, 0):
                        qk_product(s)
                    if in_flight(s, 0):
                        v_product(s)
                    if in_flight(s, 4):
                        project(s - 4)
                    if in_flight(s, 3):
                        turn_p(s - 3)
                    if static_in(s, after):
                        after[s]()

                for s in range(DEPTH + 1):
                    step(s)
                with pe.Fori(DEPTH + 1, B - 1, 2) as s:
                    step(s)
                    step(s + 1)
                for s in range(B, B + DEPTH):
                    step(s)

            pe.wait_ge(filled, 2)
            keep_warm(10, 7)
            pe.wait_ge(tok_in, 16)
            for i in range(B // 2):
                if i >= 4:
                    pe.wait_ge(patch_sb, i - 3)
                pe.wait_ge(patch_in[i // 2], 16)
                product(bank[i % 4][0:PAIR, 0:C], [(patches[:, i, c, :], w_tok[:, c, :]) for c in range(PF)], patch_ps)
            pe.wait_ge(patch_sb, B // 2)
            pe.wait_ge(attn_in, ATTN_IN)
            pe.wait_ge(filled, FILLS)
            attention(0, {B + 2: lambda: (turn_rows(0, 0), turn_rows(0, 1)), B + 3: lambda: keep_warm(12, 7)})
            pe.wait_ge(late_in, LATE_IN)

            def route0(g):
                pe.wait_ge(f_xT_sb, 2 * (g + 1))
                for b in range(4 * g, 4 * g + 4):
                    cols = slice(b * T, (b + 1) * T)
                    product(bank[2][0:T, b * E0:(b + 1) * E0],
                            [(XT0[:, cols], router0[:, :]), (XT1[0:C1, cols], router1[:, :])], f_log_ps)
            route0(0)
            route0(1)
            turn_rows(0, 2)
            turn_rows(0, 3)
            route0(2)
            route0(3)
            pe.wait_ge(pick_done, 11)
            picks = picks16[:, :, :].rearrange("p b e -> p (b e)")
            product(bank[1][0:T, 0:B * E0], [(ones16[:, :], picks)], count_ps)
            mm(bank[0][0:T, 0:B * E0], tri16[:, :], picks, start=True, stop=False, skip_group_check=True)
            for b in range(B - 1):
                later = picks16[:, b:b + 1, :].to_broadcast([T, B - 1 - b, E0])
                ins = mm(bank[0][0:T, (b + 1) * E0:B * E0].rearrange("p (b e) -> p b e", e=E0), ones16[:, :], later,
                         start=False, stop=True, skip_group_check=True)
            ins.then_inc(count_ps, 1)
            pe.wait_ge(slot_known, 2)
            keep_warm(10, 7)
            pe.wait_ge(who_ready, 2)
            pe.wait_ge(named_done, 2)
            names3 = named[:, :, :, :].rearrange("p i x j -> p i (x j)")

            for i in range(NPICK):
                ins = mm(bank[2][:, 0:2 * NBLK], in_hot[:, i, :], names3[:, i, :], start=(i == 0), stop=(i == NPICK - 1))
            ins.then_inc(who_ps, 1)
            keep_warm(24, 7)

            def turn_block(m, k):
                j, p, u = blk(m, k)
                pe.wait_ge(x_in[p], 16 * u)
                if positive(j):
                    pe.wait_ge(xs_sb, 2 * j)
                nc.tensor.transpose(bank[0][:, 0:S], xg[p][:, 0:P], ident[:, :])
                nc.tensor.transpose(bank[0][0:C1, S:2 * S], xg[p][:, P:C], ident[:, :]).then_inc(xg_ps, 1)

            def hidden_block(m, k):
                j, p, u = blk(m, k)
                pe.wait_ge(w1_in[p], 32 * u)
                pe.wait_ge(xs_sb, 2 * j + 2)
                if positive(j - 1):
                    pe.wait_ge(hid_sb, 2 * (j - 1))
                for c in range(FC):
                    cols = slice(c * P, (c + 1) * P)
                    product(bank[1 + 2 * p + c // 4][:, (c % 4) * S:(c % 4 + 1) * S],
                            [(w1a[p][:, cols], xs0[p][:, :]), (w1b[p][:, cols], xs1[p][:, :])],
                            hid_ps if c in (3, FC - 1) else None)

            def down_block(m, k):
                j, p, u = blk(m, k)
                pe.wait_ge(w2_in[p], 32 * u)
                pe.wait_ge(hid_sb, 2 * j + 2)
                if positive(j - 1):
                    pe.wait_ge(ys_done, j - 1)
                product(bank[5 + p][:, 0:C], [(hb[p][:, c, :], w2a[p][:, c, :]) for c in range(FC)], blk_ps)
            turn_block(0, 0)
            turn_block(0, 1)
            hidden_block(0, 0)
            for k in range(1, 3):
                turn_block(0, k + 1)
                hidden_block(0, k)
                down_block(0, k - 1)
            with pe.Fori(1, NBLK // 2 - 1) as m:
                for k in range(1, 3):
                    turn_block(m, k + 1)
                    hidden_block(m, k)
                    down_block(m, k - 1)
            hidden_block(NBLK // 2 - 1, 1)
            down_block(NBLK // 2 - 1, 0)
            down_block(NBLK // 2 - 1, 1)
            keep_warm(56, 7)
            attention(1, {B + 2: lambda: (turn_rows(1, 0), turn_rows(1, 1)), B + 3: lambda: keep_warm(12, 7)})

            def encode(g):
                pe.wait_ge(f_xT_sb, 8 + 2 * (g + 1))
                if g >= 2:
                    pe.wait_ge(f_enc_sb, g - 1)
                cols = slice(g * G4, (g + 1) * G4)
                product(bank[6 + g % 2][0:R1, 0:G4], [(enc_w0[:, :], XT0[:, cols]), (enc_w1[:, :], XT1[:, cols])], f_enc_ps)

            def route1(g):
                pe.wait_ge(f_enc_sb, g + 1)
                for b in range(4 * g, 4 * g + 4):
                    product(bank[2][0:T, b * E1:(b + 1) * E1], [(encT[:, b * T:(b + 1) * T], sw_w[:, :])], f_log_ps)

            def hidden(g, own):
                cols = bass.ds(g * G4, G4)
                for c in range(RC):
                    if positive(g):
                        pe.wait_ge(f_hid_sb, (g - 1) * RC + c + 1)
                    if own is not None and c == 2:
                        pe.wait_ge(*own)
                    product(bank[c][:, 0:G4], [(f1_w0[:, c * P:(c + 1) * P], XT0[:, cols]),
                                               (f1_w1[:, c * P:(c + 1) * P], XT1[:, cols])], f_hid_ps)

            def down(g):
                pe.wait_ge(gm_done, (g + 1) * RC)
                cols = bass.ds(g * G4, G4)
                for k, (lo, hi) in enumerate([(0, P), (P, C)]):
                    if positive(g):
                        pe.wait_ge(yT_sb, 2 * (g - 1) + k + 1)
                    product(bank[6 + k][0:hi - lo, 0:G4], [(f1_w2[:, c, lo:hi], gm[:, c, :]) for c in range(RC)]
                            + [(f1_b2[:, lo:hi], oneT[:, cols])], yT_ps)

            def turn_back(g):
                pe.wait_ge(yT_sb, 2 * (g + 1))
                for j in range(4):
                    if positive(g):
                        pe.wait_ge(yout_done, 4 * (g - 1) + 2 * (j // 2) + 2)
                    tok = slice(j * T, (j + 1) * T)
                    dst = bank[4 + j // 2]
                    nc.tensor.transpose(dst[0:T, (j % 2) * C:(j % 2) * C + P], yT0[:, tok], ident[:, :])
                    ins = nc.tensor.transpose(dst[0:T, (j % 2) * C + P:(j % 2 + 1) * C], yT1[:, tok], ident[0:C1, 0:C1])
                    if j % 2:
                        ins.then_inc(f_y_ps, 1)
            encode(0)
            encode(1)
            turn_rows(1, 2)
            route1(0)
            turn_rows(1, 3)
            route1(1)
            encode(2)
            encode(3)
            route1(2)
            route1(3)
            hidden(0, (f_route, 9))
            pe.wait_ge(f_route, 12)
            for g in range(B // 4):
                for j in range(4):
                    ins = nc.tensor.transpose(bank[4 + g][0:E1, j * T:(j + 1) * T], one_hot1[:, 4 * g + j, :], ident[0:T, 0:T])
                ins.then_inc(oneT_ps, 1)
            pe.wait_ge(sel_done, 1)
            for i in range(16):
                g, c = i // RC, i % RC
                pe.wait_ge(one16_done, g + 1)
                pe.wait_ge(oneT_sb, 4)
                if i >= 4:
                    pe.wait_ge(mark_sb[i % 2], (i - 4) // 2 + 1)
                product(bank[4 + i % 4][:, 0:G4], [(sel16[:, c * P:(c + 1) * P], oneT16[:, g * G4:(g + 1) * G4])], mark_ps)
            for k in range(2):
                pe.wait_ge(mark_sb[k], 8)

            for g in range(1, B // 4):
                hidden(g, None)
                down(g - 1)
                turn_back(g - 1)
            down(B // 4 - 1)
            turn_back(B // 4 - 1)


def _layout(inputs):
    import numpy as np
    a = {k: np.asarray(v) for k, v in inputs.items()}
    f = np.ascontiguousarray
    hp = 6
    x = a["x"].reshape(B, 3, hp, 16, hp, 16).transpose(1, 3, 5, 0, 2, 4).reshape(PF, P, B // 2, 2, NPATCH)
    patch = np.zeros((PF, P, B // 2, PAIR), x.dtype)
    patch[..., :NPATCH] = x[..., 0, :]
    patch[..., PAIR - NPATCH:] = x[..., 1, :]
    patch = patch.transpose(1, 2, 0, 3).reshape(P, B // 4, 2, PF, PAIR).transpose(1, 0, 2, 3, 4)

    def with_bias(w, b):
        return f(np.concatenate([w, b.reshape(1, -1)]))
    d = {
        "patchT": f(patch),
        "wtokT": f(a["L0_tok_W"].T.reshape(PF, P, C).transpose(1, 0, 2)),
        "txt": f(a["txt"]),
        "qkv0": with_bias(a["L0_attn_W_attn"], a["L0_attn_b_attn"]),
        "proj0": f(a["L0_attn_W_proj"]), "bproj0": f(a["L0_attn_b_proj"].reshape(1, -1)),
        "ln0": f(np.stack([a["L0_attn_norm_scale"], a["L0_attn_norm_bias"]], axis=1)),
        "sinks": f(a["L0_attn_sinks"].reshape(1, -1)), "rezero": f(a["L0_attn_rezero"].reshape(1, 1)),
        "wrT": f(a["L0_ffn_Wr"].T), "w1": f(np.concatenate([a["L0_ffn_W1"], a["L0_ffn_b1"][:, None, :]], axis=1)),
        "w2": f(a["L0_ffn_W2"].reshape(E0, FC, P, C).transpose(0, 2, 1, 3).reshape(E0, P, FC * C)), "b2": f(a["L0_ffn_b2"]),
        "qkv1": with_bias(a["L1_attn_qkv_weight"].T, a["L1_attn_qkv_bias"]),
        "proj1": f(a["L1_attn_proj_weight"].T), "bproj1": f(a["L1_attn_proj_bias"].reshape(1, -1)),
        "encw": with_bias(a["L1_ffn_enc_w"], a["L1_ffn_enc_b"]),
        "sww": with_bias(a["L1_ffn_sw_w"], a["L1_ffn_sw_b"]),
        "f1w1": with_bias(a["L1_ffn_w1"].transpose(1, 0, 2).reshape(C, E1 * R1), a["L1_ffn_b1"]),
        "f1w2": f(a["L1_ffn_w2"].reshape(E1 * R1, C)), "f1b2": f(a["L1_ffn_b2"]),
    }
    ang = np.outer(np.arange(T, dtype=np.float32),
                   (1.0 / np.float32(10000.0) ** (np.arange(0, HD, 2, dtype=np.float32) / HD)).astype(np.float32))
    cos, sin = np.cos(ang).astype(np.float32), np.sin(ang).astype(np.float32)
    d["rope"] = f(np.stack([np.repeat(cos, 2, axis=1), np.stack([-sin, sin], axis=-1).reshape(T, HD)], axis=1))
    d["ident"] = np.eye(P, dtype=np.float32)
    d["mask"] = np.triu(np.full((T, T), MASKED, np.float32), 1)
    d["iota"] = np.arange(P, dtype=np.float32).reshape(1, -1)
    d["tri"] = np.triu(np.ones((T, T), np.float32), 1)
    d["tok1"] = np.arange(1, T + 1, dtype=np.float32).reshape(-1, 1)
    d["pad"] = f(TOPK * TOK + np.arange(NBLK * S, dtype=np.float32).reshape(NBLK, S).T)
    sel = np.zeros((E1, RC * P), np.float32)
    for e in range(E1):
        sel[e, e * R1:(e + 1) * R1] = 1.0
    d["sel"] = sel
    return d


def kernel(**inputs):
    import concourse.bacc as _bacc
    from concourse import mybir as _mybir
    from concourse.bass_utils import run_bass_kernel_spmd as _run

    nc = _bacc.Bacc("TRN2", target_bir_lowering=False, num_devices=1)
    data = _layout(inputs)
    arrays, aps = {}, {}
    for name, a in data.items():
        arrays[f"in_{name}_dram"] = a
        aps[name] = nc.dram_tensor(f"in_{name}_dram", a.shape, _mybir.dt.from_np(a.dtype), kind="ExternalInput").ap()
    out = nc.dram_tensor("out_0_dram", (B, T, C), F32, kind="ExternalOutput").ap()
    fusion_kernel(nc, aps, out)
    r = _run(nc, [arrays], core_ids=[0])
    return r.results[0]["out_0_dram"]
```
